# Optimizing a Trainium2 kernel written in Bass

```python
import numpy as np
import jax
import jax.numpy as jnp

def _softmax(x, axis=-1):
    return jax.nn.softmax(x, axis=axis)

def _gelu(x):
    return jax.nn.gelu(x, approximate=True)

def _silu(x):
    return jax.nn.silu(x)

def _sigmoid(x):
    return jax.nn.sigmoid(x)

def _layernorm(x, axis=-1, eps=1e-05):
    m = jnp.mean(x, axis=axis, keepdims=True)
    v = jnp.var(x, axis=axis, keepdims=True)
    return (x - m) / jnp.sqrt(v + eps)

def _scatter_add(tgt, idx, src, axis=0):
    return tgt.at[idx].add(src)

def _segment_sum(src, seg, n):
    return jax.ops.segment_sum(src, seg, n)
kernel_name = 'mk_early_fusion_d4_tok_img256_r4_13510b'

def setup_inputs(seed: int=0):
    np.random.seed(seed)
    _w = jnp.asarray

    def _rec_inputs():
        import jax
        import jax.numpy as jnp
        _rk = jax.random.key(seed)
        x = 7.22013e-05 + 1.00017 * jax.random.normal(jax.random.fold_in(_rk, 1), (2, 1, 1024, 64), jnp.float32)
        txt = 10 + 10 * jax.random.normal(jax.random.fold_in(_rk, 2), (2, 128, 64), jnp.float32)
        return (x, txt)
    x, txt = _rec_inputs()

    def _L0_tok_setup():
        import jax, jax.numpy as jnp
        import numpy as np
        T, D_IN, D_INT, D_OUT, B = (1024, 64, 64, 64, 8)
        key = jax.random.key(seed)
        ks = jax.random.split(key, 12)
        s_in = 1.0 / np.sqrt(D_IN)
        s_int = 1.0 / np.sqrt(D_INT)
        return {'x_batched': jax.random.normal(ks[0], (B, 1, T, D_IN), dtype=jnp.float32), 'd_gamma_batched': jax.random.uniform(ks[1], (T, T), dtype=jnp.float32), 'Wq': jax.random.uniform(ks[2], (D_IN, D_INT), jnp.float32, -s_in, s_in), 'bq': jax.random.uniform(ks[3], (D_INT,), jnp.float32, -s_in, s_in), 'Wk': jax.random.uniform(ks[4], (D_IN, D_INT), jnp.float32, -s_in, s_in), 'bk': jax.random.uniform(ks[5], (D_INT,), jnp.float32, -s_in, s_in), 'Wv': jax.random.uniform(ks[6], (D_IN, D_INT), jnp.float32, -s_in, s_in), 'bv': jax.random.uniform(ks[7], (D_INT,), jnp.float32, -s_in, s_in), 'Wo': jax.random.uniform(ks[8], (D_INT, D_OUT), jnp.float32, -s_int, s_int), 'bo': jax.random.uniform(ks[9], (D_OUT,), jnp.float32, -s_int, s_int), 'prelu_a': jnp.float32(0.25)}
    _L0_tok_all = _L0_tok_setup()
    _L0_tok_in = {k: v for k, v in _L0_tok_all.items() if k in ('d_gamma_batched', 'Wq', 'bq', 'Wk', 'bk', 'Wv', 'bv', 'Wo', 'bo', 'prelu_a')}
    del _L0_tok_all

    def _L0_attn_setup():
        import jax, jax.numpy as jnp
        import numpy as np
        B, N, C = (8, 2048, 64)
        HEADS, DH, KR = (8, 32, 4)
        INNER = HEADS * DH
        FF = 4 * C
        EPS = 1e-05

        def layernorm(x, g, b):
            mu = jnp.mean(x, axis=-1, keepdims=True)
            var = jnp.mean((x - mu) ** 2, axis=-1, keepdims=True)
            return (x - mu) * jax.lax.rsqrt(var + EPS) * g + b
        key = jax.random.key(seed)
        ks = jax.random.split(key, 16)
        s = 0.02
        return {'x': jax.random.normal(ks[0], (B, N, C), jnp.float32), 'ln1_g': jnp.ones((C,), jnp.float32), 'ln1_b': jnp.zeros((C,), jnp.float32), 'Wx': jax.random.normal(ks[1], (C, INNER), jnp.float32) * s, 'bx': jnp.zeros((INNER,), jnp.float32), 'Wq': jax.random.normal(ks[2], (DH, KR), jnp.float32) * s, 'Wk': jax.random.normal(ks[3], (DH, KR), jnp.float32) * s, 'Wv': jax.random.normal(ks[4], (DH, DH), jnp.float32) * s, 'Wo': jax.random.normal(ks[5], (INNER, C), jnp.float32) * s, 'bo': jnp.zeros((C,), jnp.float32), 'ln2_g': jnp.ones((C,), jnp.float32), 'ln2_b': jnp.zeros((C,), jnp.float32), 'W1': jax.random.normal(ks[6], (C, FF), jnp.float32) * s, 'b1': jnp.zeros((FF,), jnp.float32), 'W2': jax.random.normal(ks[7], (FF, C), jnp.float32) * s, 'b2': jnp.zeros((C,), jnp.float32)}
    _L0_attn_all = _L0_attn_setup()
    _L0_attn_in = {k: v for k, v in _L0_attn_all.items() if k in ('ln1_g', 'ln1_b', 'Wx', 'bx', 'Wq', 'Wk', 'Wv', 'Wo', 'bo', 'ln2_g', 'ln2_b', 'W1', 'b1', 'W2', 'b2')}
    del _L0_attn_all

    def _L0_ffn_setup():
        import jax, jax.numpy as jnp
        import numpy as np
        B, S, D = (8, 1024, 64)
        H = 4 * D
        CAPACITY = 0.5
        key = jax.random.key(seed)
        ks = jax.random.split(key, 6)
        x = jax.random.normal(ks[0], (B, S, D), dtype=jnp.float32)
        attention_mask = jnp.zeros((B, 1, 1, S), dtype=jnp.float32)
        wr = jax.random.normal(ks[1], (D, 1), dtype=jnp.float32) * 0.02
        br = jnp.zeros((1,), dtype=jnp.float32)
        w1 = jax.random.normal(ks[2], (D, H), dtype=jnp.float32) * 0.02
        b1 = jnp.zeros((H,), dtype=jnp.float32)
        w2 = jax.random.normal(ks[3], (H, D), dtype=jnp.float32) * 0.02
        b2 = jnp.zeros((D,), dtype=jnp.float32)
        return {'x': x, 'attention_mask': attention_mask, 'wr': wr, 'br': br, 'w1': w1, 'b1': b1, 'w2': w2, 'b2': b2}
    _L0_ffn_all = _L0_ffn_setup()
    _L0_ffn_in = {k: v for k, v in _L0_ffn_all.items() if k in ('attention_mask', 'wr', 'br', 'w1', 'b1', 'w2', 'b2')}
    del _L0_ffn_all

    def _L1_attn_setup():
        import jax, jax.numpy as jnp
        import numpy as np
        from jax import lax

        def _solve_im(u, a, W_B, b_B, dt):
            s = 1.0 / (1.0 + dt * dt * a)
            Bu = jnp.einsum('bnq,pq->bnp', u, W_B) + b_B
            f_x = dt * s * Bu
            f_z = dt * dt * s * Bu
            dsa = dt * s * a
            ds = dt * s

            def step(carry, f):
                x, z = carry
                fx, fz = f
                x_new = s * x - dsa * z + fx
                z_new = ds * x + s * z + fz
                return ((x_new, z_new), z_new)
            Bsz, _, q = u.shape
            init = (jnp.zeros((Bsz, q), u.dtype), jnp.zeros((Bsz, q), u.dtype))
            _, z_t = lax.scan(step, init, (jnp.moveaxis(f_x, 1, 0), jnp.moveaxis(f_z, 1, 0)))
            return jnp.moveaxis(z_t, 0, 1)

        def _reference_tuple_inner(u, a, W_B, b_B, W_C, b_C, W_D, b_D):
            N = u.shape[1]
            dt = 1.0 / N
            y = _solve_im(u, a, W_B, b_B, dt)
            x = jnp.einsum('bnq,pq->bnp', y, W_C) + b_C + (jnp.einsum('bnq,pq->bnp', u, W_D) + b_D)
            x = jax.nn.gelu(x, approximate=False)
            out = x * jax.nn.sigmoid(x) + u
            return (out, y)
        key = jax.random.key(seed)
        ks = jax.random.split(key, 8)
        B, N, q = (16, 1024, 64)
        sc = float(1.0 / np.sqrt(q))
        return {'u': jax.random.normal(ks[0], (B, N, q), jnp.float32), 'a': jax.random.normal(ks[1], (q,), jnp.float32), 'W_B': jax.random.normal(ks[2], (q, q), jnp.float32) * sc, 'b_B': jax.random.normal(ks[3], (q,), jnp.float32) * sc, 'W_C': jax.random.normal(ks[4], (q, q), jnp.float32) * sc, 'b_C': jax.random.normal(ks[5], (q,), jnp.float32) * sc, 'W_D': jax.random.normal(ks[6], (q, q), jnp.float32) * sc, 'b_D': jax.random.normal(ks[7], (q,), jnp.float32) * sc}
    _L1_attn_all = _L1_attn_setup()
    _L1_attn_in = {k: v for k, v in _L1_attn_all.items() if k in ('a', 'W_B', 'b_B', 'W_C', 'b_C', 'W_D', 'b_D')}
    del _L1_attn_all

    def _L1_ffn_setup():
        import jax, jax.numpy as jnp
        import numpy as np
        B, K, D = (128, 16, 64)
        E = 32
        H = int(D * 0.25)
        key = jax.random.key(seed)
        ks = jax.random.split(key, 7)
        d_rs = D ** (-0.5)
        h_rs = H ** (-0.5)
        x = jax.random.normal(ks[0], (B, K, D), dtype=jnp.float32)
        router_w = jax.random.uniform(ks[1], (E, D), jnp.float32, -d_rs, d_rs)
        router_b = jax.random.uniform(ks[2], (E,), jnp.float32, -d_rs, d_rs)
        W1 = jax.random.uniform(ks[3], (E, D, H), jnp.float32, -h_rs, h_rs)
        b1 = jax.random.uniform(ks[4], (E, H), jnp.float32, -h_rs, h_rs)
        W2 = jax.random.uniform(ks[5], (E, H, D), jnp.float32, -d_rs, d_rs)
        b2 = jax.random.uniform(ks[6], (E, D), jnp.float32, -d_rs, d_rs)
        return {'x': x, 'router_w': router_w, 'router_b': router_b, 'W1': W1, 'b1': b1, 'W2': W2, 'b2': b2}
    _L1_ffn_all = _L1_ffn_setup()
    _L1_ffn_in = {k: v for k, v in _L1_ffn_all.items() if k in ('router_w', 'router_b', 'W1', 'b1', 'W2', 'b2')}
    del _L1_ffn_all

    def _L2_attn_setup():
        import jax, jax.numpy as jnp
        import numpy as np
        B_SZ, L, N, H = (8, 1024, 64, 64)
        R_MIN, R_MAX, MAX_PHASE = (0.0, 1.0, 0.314)
        key = jax.random.key(seed)
        ks = jax.random.split(key, 8)
        x = jax.random.normal(ks[0], (B_SZ, L, H), jnp.float32)

        def glorot(k, shape):
            return jax.random.normal(k, shape, jnp.float32) * jnp.sqrt(2.0 / (shape[0] + shape[1])).astype(jnp.float32)
        B_re = glorot(ks[1], (N, H))
        B_im = glorot(ks[2], (N, H))
        C_re = glorot(ks[3], (H, N))
        C_im = glorot(ks[4], (H, N))
        u1 = jax.random.uniform(ks[5], (N,), jnp.float32, 1e-06, 1.0)
        u2 = jax.random.uniform(ks[6], (N,), jnp.float32, 1e-06, 1.0)
        nu_log = jnp.log(-0.5 * jnp.log(u1 * (R_MAX ** 2 - R_MIN ** 2) + R_MIN ** 2))
        theta_log = jnp.log(MAX_PHASE * u2)
        D = jax.random.normal(ks[7], (H,), jnp.float32) * 0.05
        return dict(x=x, B_re=B_re, B_im=B_im, C_re=C_re, C_im=C_im, nu_log=nu_log, theta_log=theta_log, D=D)
    _L2_attn_all = _L2_attn_setup()
    _L2_attn_in = {k: v for k, v in _L2_attn_all.items() if k in ('B_re', 'B_im', 'C_re', 'C_im', 'nu_log', 'theta_log', 'D')}
    del _L2_attn_all

    def _L2_ffn_setup():
        import jax, jax.numpy as jnp
        import numpy as np
        B, N, D = (16, 1024, 64)
        NUM_EXPERTS, TOP_K, HEADS = (4, 2, 4)
        N_EDGES = 262144
        LN_EPS = 1e-05

        def _layernorm(x, g, b):
            mu = x.mean(-1, keepdims=True)
            var = ((x - mu) ** 2).mean(-1, keepdims=True)
            return (x - mu) * jax.lax.rsqrt(var + LN_EPS) * g + b

        def _forward(x, edge_index, W_gat, att_src, att_dst, b_gat, ln_gamma, ln_beta, W1, b1, W2, b2):
            Bc, Nc, Dc = x.shape
            M = Bc * Nc
            x_flat = x.reshape(M, Dc)
            h = (x_flat @ W_gat).reshape(M, HEADS, NUM_EXPERTS)
            loops = jnp.arange(M, dtype=edge_index.dtype)
            src = jnp.concatenate([edge_index[0], loops])
            dst = jnp.concatenate([edge_index[1], loops])
            a_src = (h * att_src).sum(-1)
            a_dst = (h * att_dst).sum(-1)
            e = jax.nn.leaky_relu(a_src[src] + a_dst[dst], negative_slope=0.2)
            e_max = jax.ops.segment_max(e, dst, num_segments=M)
            ee = jnp.exp(e - e_max[dst])
            denom = jax.ops.segment_sum(ee, dst, num_segments=M)
            alpha = ee / (denom[dst] + 1e-16)
            msg = h[src] * alpha[:, :, None]
            agg = jax.ops.segment_sum(msg, dst, num_segments=M).reshape(M, HEADS * NUM_EXPERTS) + b_gat
            scores = _layernorm(agg, ln_gamma, ln_beta).reshape(M, HEADS, NUM_EXPERTS).mean(1)
            scores = scores.reshape(Bc, Nc, NUM_EXPERTS)
            topk_s, topk_i = jax.lax.top_k(scores, TOP_K)
            w = jax.nn.softmax(topk_s, axis=-1)
            out = jnp.zeros_like(x)
            for ei in range(NUM_EXPERTS):
                g = jnp.where(topk_i == ei, w, 0.0).sum(-1)
                hh = jax.nn.gelu(x @ W1[ei] + b1[ei], approximate=False)
                out = out + g[..., None] * (hh @ W2[ei] + b2[ei])
            return out
        key = jax.random.key(seed)
        ks = jax.random.split(key, 8)
        s = 0.05
        return {'x': jax.random.normal(ks[0], (B, N, D), jnp.float32), 'W_gat': jax.random.normal(ks[1], (D, HEADS * NUM_EXPERTS), jnp.float32) * s, 'att_src': jax.random.normal(ks[2], (HEADS, NUM_EXPERTS), jnp.float32) * s, 'att_dst': jax.random.normal(ks[3], (HEADS, NUM_EXPERTS), jnp.float32) * s, 'b_gat': jnp.zeros((HEADS * NUM_EXPERTS,), jnp.float32), 'ln_gamma': jnp.ones((HEADS * NUM_EXPERTS,), jnp.float32), 'ln_beta': jnp.zeros((HEADS * NUM_EXPERTS,), jnp.float32), 'W1': jax.random.normal(ks[4], (NUM_EXPERTS, D, 2 * D), jnp.float32) * s, 'b1': jnp.zeros((NUM_EXPERTS, 2 * D), jnp.float32), 'W2': jax.random.normal(ks[5], (NUM_EXPERTS, 2 * D, D), jnp.float32) * s, 'b2': jnp.zeros((NUM_EXPERTS, D), jnp.float32), 'edge_index': jax.random.randint(ks[6], (2, N_EDGES), 0, B * N, jnp.int32)}
    _L2_ffn_all = _L2_ffn_setup()
    _L2_ffn_in = {k: v for k, v in _L2_ffn_all.items() if k in ('W_gat', 'att_src', 'att_dst', 'b_gat', 'ln_gamma', 'ln_beta', 'W1', 'b1', 'W2', 'b2', 'edge_index')}
    del _L2_ffn_all

    def _L3_attn_setup():
        import jax, jax.numpy as jnp
        import numpy as np
        B, T, C = (4, 1024, 64)
        key = jax.random.key(seed)
        ks = jax.random.split(key, 7)
        s = 1.0 / np.sqrt(C)
        x = jax.random.normal(ks[0], (B, T, C), dtype=jnp.float32)
        Wq = jax.random.uniform(ks[1], (C, C), jnp.float32, -s, s)
        bq = jax.random.uniform(ks[2], (C,), jnp.float32, -s, s)
        Wk = jax.random.uniform(ks[3], (C, C), jnp.float32, -s, s)
        bk = jax.random.uniform(ks[4], (C,), jnp.float32, -s, s)
        Wv = jax.random.uniform(ks[5], (C, C), jnp.float32, -s, s)
        bv = jax.random.uniform(ks[6], (C,), jnp.float32, -s, s)
        return {'x': x, 'Wq': Wq, 'bq': bq, 'Wk': Wk, 'bk': bk, 'Wv': Wv, 'bv': bv}
    _L3_attn_all = _L3_attn_setup()
    _L3_attn_in = {k: v for k, v in _L3_attn_all.items() if k in ('Wq', 'bq', 'Wk', 'bk', 'Wv', 'bv')}
    del _L3_attn_all

    def _L3_ffn_setup():
        import jax, jax.numpy as jnp
        import numpy as np
        B, S, D, E, H, K = (4, 1024, 64, 8, 128, 2)
        key = jax.random.key(seed)
        ks = jax.random.split(key, 6)
        x = jax.random.normal(ks[0], (B, S, D), jnp.float32)
        Wg = jax.random.normal(ks[1], (D, E), jnp.float32) * 0.02
        bg = jnp.zeros((E,), jnp.float32)
        W1 = jax.random.normal(ks[2], (E, D, H), jnp.float32) * 0.02
        b1 = jnp.zeros((E, H), jnp.float32)
        W2 = jax.random.normal(ks[3], (E, H, D), jnp.float32) * 0.02
        b2 = jnp.zeros((E, D), jnp.float32)
        return {'x': x, 'Wg': Wg, 'bg': bg, 'W1': W1, 'b1': b1, 'W2': W2, 'b2': b2}
    _L3_ffn_all = _L3_ffn_setup()
    _L3_ffn_in = {k: v for k, v in _L3_ffn_all.items() if k in ('Wg', 'bg', 'W1', 'b1', 'W2', 'b2')}
    del _L3_ffn_all
    return {'x': x, 'txt': txt, 'L0_tok_d_gamma_batched': _L0_tok_in['d_gamma_batched'], 'L0_tok_Wq': _L0_tok_in['Wq'], 'L0_tok_bq': _L0_tok_in['bq'], 'L0_tok_Wk': _L0_tok_in['Wk'], 'L0_tok_bk': _L0_tok_in['bk'], 'L0_tok_Wv': _L0_tok_in['Wv'], 'L0_tok_bv': _L0_tok_in['bv'], 'L0_tok_Wo': _L0_tok_in['Wo'], 'L0_tok_bo': _L0_tok_in['bo'], 'L0_tok_prelu_a': _L0_tok_in['prelu_a'], 'L0_attn_ln1_g': _L0_attn_in['ln1_g'], 'L0_attn_ln1_b': _L0_attn_in['ln1_b'], 'L0_attn_Wx': _L0_attn_in['Wx'], 'L0_attn_bx': _L0_attn_in['bx'], 'L0_attn_Wq': _L0_attn_in['Wq'], 'L0_attn_Wk': _L0_attn_in['Wk'], 'L0_attn_Wv': _L0_attn_in['Wv'], 'L0_attn_Wo': _L0_attn_in['Wo'], 'L0_attn_bo': _L0_attn_in['bo'], 'L0_attn_ln2_g': _L0_attn_in['ln2_g'], 'L0_attn_ln2_b': _L0_attn_in['ln2_b'], 'L0_attn_W1': _L0_attn_in['W1'], 'L0_attn_b1': _L0_attn_in['b1'], 'L0_attn_W2': _L0_attn_in['W2'], 'L0_attn_b2': _L0_attn_in['b2'], 'L0_ffn_attention_mask': _L0_ffn_in['attention_mask'], 'L0_ffn_wr': _L0_ffn_in['wr'], 'L0_ffn_br': _L0_ffn_in['br'], 'L0_ffn_w1': _L0_ffn_in['w1'], 'L0_ffn_b1': _L0_ffn_in['b1'], 'L0_ffn_w2': _L0_ffn_in['w2'], 'L0_ffn_b2': _L0_ffn_in['b2'], 'L1_attn_a': _L1_attn_in['a'], 'L1_attn_W_B': _L1_attn_in['W_B'], 'L1_attn_b_B': _L1_attn_in['b_B'], 'L1_attn_W_C': _L1_attn_in['W_C'], 'L1_attn_b_C': _L1_attn_in['b_C'], 'L1_attn_W_D': _L1_attn_in['W_D'], 'L1_attn_b_D': _L1_attn_in['b_D'], 'L1_ffn_router_w': _L1_ffn_in['router_w'], 'L1_ffn_router_b': _L1_ffn_in['router_b'], 'L1_ffn_W1': _L1_ffn_in['W1'], 'L1_ffn_b1': _L1_ffn_in['b1'], 'L1_ffn_W2': _L1_ffn_in['W2'], 'L1_ffn_b2': _L1_ffn_in['b2'], 'L2_attn_B_re': _L2_attn_in['B_re'], 'L2_attn_B_im': _L2_attn_in['B_im'], 'L2_attn_C_re': _L2_attn_in['C_re'], 'L2_attn_C_im': _L2_attn_in['C_im'], 'L2_attn_nu_log': _L2_attn_in['nu_log'], 'L2_attn_theta_log': _L2_attn_in['theta_log'], 'L2_attn_D': _L2_attn_in['D'], 'L2_ffn_W_gat': _L2_ffn_in['W_gat'], 'L2_ffn_att_src': _L2_ffn_in['att_src'], 'L2_ffn_att_dst': _L2_ffn_in['att_dst'], 'L2_ffn_b_gat': _L2_ffn_in['b_gat'], 'L2_ffn_ln_gamma': _L2_ffn_in['ln_gamma'], 'L2_ffn_ln_beta': _L2_ffn_in['ln_beta'], 'L2_ffn_W1': _L2_ffn_in['W1'], 'L2_ffn_b1': _L2_ffn_in['b1'], 'L2_ffn_W2': _L2_ffn_in['W2'], 'L2_ffn_b2': _L2_ffn_in['b2'], 'L2_ffn_edge_index': _L2_ffn_in['edge_index'], 'L3_attn_Wq': _L3_attn_in['Wq'], 'L3_attn_bq': _L3_attn_in['bq'], 'L3_attn_Wk': _L3_attn_in['Wk'], 'L3_attn_bk': _L3_attn_in['bk'], 'L3_attn_Wv': _L3_attn_in['Wv'], 'L3_attn_bv': _L3_attn_in['bv'], 'L3_ffn_Wg': _L3_ffn_in['Wg'], 'L3_ffn_bg': _L3_ffn_in['bg'], 'L3_ffn_W1': _L3_ffn_in['W1'], 'L3_ffn_b1': _L3_ffn_in['b1'], 'L3_ffn_W2': _L3_ffn_in['W2'], 'L3_ffn_b2': _L3_ffn_in['b2']}

def reference(x, txt, L0_tok_d_gamma_batched, L0_tok_Wq, L0_tok_bq, L0_tok_Wk, L0_tok_bk, L0_tok_Wv, L0_tok_bv, L0_tok_Wo, L0_tok_bo, L0_tok_prelu_a, L0_attn_ln1_g, L0_attn_ln1_b, L0_attn_Wx, L0_attn_bx, L0_attn_Wq, L0_attn_Wk, L0_attn_Wv, L0_attn_Wo, L0_attn_bo, L0_attn_ln2_g, L0_attn_ln2_b, L0_attn_W1, L0_attn_b1, L0_attn_W2, L0_attn_b2, L0_ffn_attention_mask, L0_ffn_wr, L0_ffn_br, L0_ffn_w1, L0_ffn_b1, L0_ffn_w2, L0_ffn_b2, L1_attn_a, L1_attn_W_B, L1_attn_b_B, L1_attn_W_C, L1_attn_b_C, L1_attn_W_D, L1_attn_b_D, L1_ffn_router_w, L1_ffn_router_b, L1_ffn_W1, L1_ffn_b1, L1_ffn_W2, L1_ffn_b2, L2_attn_B_re, L2_attn_B_im, L2_attn_C_re, L2_attn_C_im, L2_attn_nu_log, L2_attn_theta_log, L2_attn_D, L2_ffn_W_gat, L2_ffn_att_src, L2_ffn_att_dst, L2_ffn_b_gat, L2_ffn_ln_gamma, L2_ffn_ln_beta, L2_ffn_W1, L2_ffn_b1, L2_ffn_W2, L2_ffn_b2, L2_ffn_edge_index, L3_attn_Wq, L3_attn_bq, L3_attn_Wk, L3_attn_bk, L3_attn_Wv, L3_attn_bv, L3_ffn_Wg, L3_ffn_bg, L3_ffn_W1, L3_ffn_b1, L3_ffn_W2, L3_ffn_b2):
    import jax
    import jax.numpy as jnp

    def _L0_tok_ref(x_batched, d_gamma_batched, Wq, bq, Wk, bk, Wv, bv, Wo, bo, prelu_a):
        import jax, jax.numpy as jnp
        import numpy as np
        T, D_IN, D_INT, D_OUT, B = (1024, 64, 64, 64, 8)
        x = x_batched.reshape(x_batched.shape[0], T, D_IN)
        q = x @ Wq + bq
        k = x @ Wk + bk
        v = x @ Wv + bv
        scores = jnp.einsum('btd,bsd->bts', q, k)
        retained = jnp.einsum('bts,bsd->btd', d_gamma_batched * scores, v)
        y = retained @ Wo + bo
        out = jnp.where(y >= 0, y, prelu_a * y)
        return out

    def _L0_attn_ref(x, ln1_g, ln1_b, Wx, bx, Wq, Wk, Wv, Wo, bo, ln2_g, ln2_b, W1, b1, W2, b2):
        import jax, jax.numpy as jnp
        import numpy as np
        B, N, C = (8, 2048, 64)
        HEADS, DH, KR = (8, 32, 4)
        INNER = HEADS * DH
        FF = 4 * C
        EPS = 1e-05

        def layernorm(x, g, b):
            mu = jnp.mean(x, axis=-1, keepdims=True)
            var = jnp.mean((x - mu) ** 2, axis=-1, keepdims=True)
            return (x - mu) * jax.lax.rsqrt(var + EPS) * g + b
        b, n, c = x.shape
        h = layernorm(x, ln1_g, ln1_b)
        xm = h @ Wx + bx
        xm = xm.reshape(b, n, HEADS, DH).transpose(0, 2, 1, 3)
        q = jax.nn.softmax(xm @ Wq, axis=-1)
        k = jax.nn.softmax(xm @ Wk, axis=-2)
        v = xm @ Wv
        kv = jnp.einsum('bhnr,bhnd->bhrd', k, v)
        qkv = jnp.einsum('bhnr,bhrd->bhnd', q, kv)
        attn = qkv.transpose(0, 2, 1, 3).reshape(b, n, INNER) @ Wo + bo
        fx = attn + x
        h2 = layernorm(fx, ln2_g, ln2_b)
        m = jax.nn.gelu(h2 @ W1 + b1, approximate=False) @ W2 + b2
        return m + fx

    def _L0_ffn_ref(x, attention_mask, wr, br, w1, b1, w2, b2):
        import jax, jax.numpy as jnp
        import numpy as np
        B, S, D = (8, 1024, 64)
        H = 4 * D
        CAPACITY = 0.5
        b, s, d = x.shape
        weights = (jnp.einsum('bsd,do->bso', x, wr) + br)[..., 0]
        k = max(1, int(CAPACITY * s))
        kk = k - 1 if k > 1 else 1
        _, idx = jax.lax.top_k(weights, k)
        sel_idx = idx[:, :kk]
        sel = jnp.take_along_axis(x, sel_idx[:, :, None], axis=1)
        h = jax.nn.gelu(jnp.einsum('bkd,dh->bkh', sel, w1) + b1)
        y = jnp.einsum('bkh,hd->bkd', h, w2) + b2
        w_sel = jnp.take_along_axis(weights, sel_idx, axis=1)
        y = y * w_sel[..., None]
        batch_idx = jnp.arange(b)[:, None]
        processed = jnp.zeros_like(x).at[batch_idx, sel_idx].set(y)
        return processed + x

    def _L1_attn_ref(u, a, W_B, b_B, W_C, b_C, W_D, b_D):
        import jax, jax.numpy as jnp
        import numpy as np
        from jax import lax

        def _solve_im(u, a, W_B, b_B, dt):
            s = 1.0 / (1.0 + dt * dt * a)
            Bu = jnp.einsum('bnq,pq->bnp', u, W_B) + b_B
            f_x = dt * s * Bu
            f_z = dt * dt * s * Bu
            dsa = dt * s * a
            ds = dt * s

            def step(carry, f):
                x, z = carry
                fx, fz = f
                x_new = s * x - dsa * z + fx
                z_new = ds * x + s * z + fz
                return ((x_new, z_new), z_new)
            Bsz, _, q = u.shape
            init = (jnp.zeros((Bsz, q), u.dtype), jnp.zeros((Bsz, q), u.dtype))
            _, z_t = lax.scan(step, init, (jnp.moveaxis(f_x, 1, 0), jnp.moveaxis(f_z, 1, 0)))
            return jnp.moveaxis(z_t, 0, 1)

        def _reference_tuple_inner(u, a, W_B, b_B, W_C, b_C, W_D, b_D):
            N = u.shape[1]
            dt = 1.0 / N
            y = _solve_im(u, a, W_B, b_B, dt)
            x = jnp.einsum('bnq,pq->bnp', y, W_C) + b_C + (jnp.einsum('bnq,pq->bnp', u, W_D) + b_D)
            x = jax.nn.gelu(x, approximate=False)
            out = x * jax.nn.sigmoid(x) + u
            return (out, y)
        return _reference_tuple_inner(u, a, W_B, b_B, W_C, b_C, W_D, b_D)[0]

    def _L1_ffn_ref(x, router_w, router_b, W1, b1, W2, b2):
        import jax, jax.numpy as jnp
        import numpy as np
        B, K, D = (128, 16, 64)
        E = 32
        H = int(D * 0.25)
        xf = x.reshape(-1, D)
        logits = xf @ router_w.T + router_b
        idx = jnp.argmax(logits, axis=-1)
        w1t = jnp.take(W1, idx, axis=0)
        h = jnp.einsum('nd,ndh->nh', xf, w1t) + jnp.take(b1, idx, axis=0)
        h = jax.nn.relu(h)
        w2t = jnp.take(W2, idx, axis=0)
        out = jnp.einsum('nh,nhd->nd', h, w2t) + jnp.take(b2, idx, axis=0)
        out = jax.nn.relu(out)
        return out.reshape(x.shape)

    def _L2_attn_ref(x, B_re, B_im, C_re, C_im, nu_log, theta_log, D):
        import jax, jax.numpy as jnp
        import numpy as np
        B_SZ, L, N, H = (8, 1024, 64, 64)
        R_MIN, R_MAX, MAX_PHASE = (0.0, 1.0, 0.314)
        Lambda = jnp.exp(jax.lax.complex(-jnp.exp(nu_log), jnp.exp(theta_log)))
        gamma = jnp.sqrt(1.0 - jnp.abs(Lambda) ** 2).astype(jnp.complex64)
        B_norm = (B_re + 1j * B_im).astype(jnp.complex64) * gamma[:, None]
        C = (C_re + 1j * C_im).astype(jnp.complex64)
        Bu = jnp.einsum('blh,nh->bln', x.astype(jnp.complex64), B_norm)
        Lambda_el = jnp.broadcast_to(Lambda, Bu.shape)

        def combine(a, b):
            la, ba = a
            lb, bb = b
            return (la * lb, lb * ba + bb)
        _, states = jax.lax.associative_scan(combine, (Lambda_el, Bu), axis=1)
        y = jnp.real(jnp.einsum('bln,hn->blh', states, C))
        y = y + x * D
        return y

    def _L2_ffn_ref(x, W_gat, att_src, att_dst, b_gat, ln_gamma, ln_beta, W1, b1, W2, b2, edge_index):
        import jax, jax.numpy as jnp
        import numpy as np
        B, N, D = (16, 1024, 64)
        NUM_EXPERTS, TOP_K, HEADS = (4, 2, 4)
        N_EDGES = 262144
        LN_EPS = 1e-05

        def _layernorm(x, g, b):
            mu = x.mean(-1, keepdims=True)
            var = ((x - mu) ** 2).mean(-1, keepdims=True)
            return (x - mu) * jax.lax.rsqrt(var + LN_EPS) * g + b

        def _forward(x, edge_index, W_gat, att_src, att_dst, b_gat, ln_gamma, ln_beta, W1, b1, W2, b2):
            Bc, Nc, Dc = x.shape
            M = Bc * Nc
            x_flat = x.reshape(M, Dc)
            h = (x_flat @ W_gat).reshape(M, HEADS, NUM_EXPERTS)
            loops = jnp.arange(M, dtype=edge_index.dtype)
            src = jnp.concatenate([edge_index[0], loops])
            dst = jnp.concatenate([edge_index[1], loops])
            a_src = (h * att_src).sum(-1)
            a_dst = (h * att_dst).sum(-1)
            e = jax.nn.leaky_relu(a_src[src] + a_dst[dst], negative_slope=0.2)
            e_max = jax.ops.segment_max(e, dst, num_segments=M)
            ee = jnp.exp(e - e_max[dst])
            denom = jax.ops.segment_sum(ee, dst, num_segments=M)
            alpha = ee / (denom[dst] + 1e-16)
            msg = h[src] * alpha[:, :, None]
            agg = jax.ops.segment_sum(msg, dst, num_segments=M).reshape(M, HEADS * NUM_EXPERTS) + b_gat
            scores = _layernorm(agg, ln_gamma, ln_beta).reshape(M, HEADS, NUM_EXPERTS).mean(1)
            scores = scores.reshape(Bc, Nc, NUM_EXPERTS)
            topk_s, topk_i = jax.lax.top_k(scores, TOP_K)
            w = jax.nn.softmax(topk_s, axis=-1)
            out = jnp.zeros_like(x)
            for ei in range(NUM_EXPERTS):
                g = jnp.where(topk_i == ei, w, 0.0).sum(-1)
                hh = jax.nn.gelu(x @ W1[ei] + b1[ei], approximate=False)
                out = out + g[..., None] * (hh @ W2[ei] + b2[ei])
            return out
        return _forward(x, edge_index, W_gat, att_src, att_dst, b_gat, ln_gamma, ln_beta, W1, b1, W2, b2)

    def _L3_attn_ref(x, Wq, bq, Wk, bk, Wv, bv):
        import jax, jax.numpy as jnp
        import numpy as np
        B, T, C = (4, 1024, 64)
        q = jnp.einsum('btc,dc->btd', x, Wq) + bq
        k = jnp.einsum('btc,dc->btd', x, Wk) + bk
        v = jnp.einsum('btc,dc->btd', x, Wv) + bv
        scale = x.shape[-1] ** (-0.5)
        scores = jnp.einsum('btd,bsd->bts', q, k) * scale
        Tn = x.shape[1]
        causal = jnp.tril(jnp.ones((Tn, Tn), dtype=bool))
        scores = jnp.where(causal, scores, -jnp.inf)
        attn = jax.nn.softmax(scores, axis=-1)
        return jnp.einsum('bts,bsd->btd', attn, v)

    def _L3_ffn_ref(x, Wg, bg, W1, b1, W2, b2):
        import jax, jax.numpy as jnp
        import numpy as np
        B, S, D, E, H, K = (4, 1024, 64, 8, 128, 2)
        Bv, Sv, Dv = x.shape
        gate_scores = x @ Wg + bg
        _, idx = jax.lax.top_k(gate_scores, K)
        mask = jax.nn.one_hot(idx, E, dtype=x.dtype).sum(axis=-2)
        xf = x.reshape(-1, Dv)
        mf = mask.reshape(-1, E)
        h = jax.nn.gelu(jnp.einsum('td,edh->teh', xf, W1) + b1[None], approximate=False)
        y = jnp.einsum('teh,ehd->ted', h, W2) + b2[None]
        out = jnp.einsum('ted,te->td', y, mf)
        return out.reshape(Bv, Sv, Dv)
    h = _L0_tok_ref(x, L0_tok_d_gamma_batched, L0_tok_Wq, L0_tok_bq, L0_tok_Wk, L0_tok_bk, L0_tok_Wv, L0_tok_bv, L0_tok_Wo, L0_tok_bo, L0_tok_prelu_a)
    h = jnp.concatenate([h, txt], axis=1)
    h = h + _L0_attn_ref(_layernorm(h, axis=-1), L0_attn_ln1_g, L0_attn_ln1_b, L0_attn_Wx, L0_attn_bx, L0_attn_Wq, L0_attn_Wk, L0_attn_Wv, L0_attn_Wo, L0_attn_bo, L0_attn_ln2_g, L0_attn_ln2_b, L0_attn_W1, L0_attn_b1, L0_attn_W2, L0_attn_b2)
    h = h + _L0_ffn_ref(_layernorm(h, axis=-1), L0_ffn_attention_mask, L0_ffn_wr, L0_ffn_br, L0_ffn_w1, L0_ffn_b1, L0_ffn_w2, L0_ffn_b2)
    h = h + _L1_attn_ref(_layernorm(h, axis=-1), L1_attn_a, L1_attn_W_B, L1_attn_b_B, L1_attn_W_C, L1_attn_b_C, L1_attn_W_D, L1_attn_b_D)
    h = h + _L1_ffn_ref(_layernorm(h, axis=-1), L1_ffn_router_w, L1_ffn_router_b, L1_ffn_W1, L1_ffn_b1, L1_ffn_W2, L1_ffn_b2)
    h = h + _L2_attn_ref(_layernorm(h, axis=-1), L2_attn_B_re, L2_attn_B_im, L2_attn_C_re, L2_attn_C_im, L2_attn_nu_log, L2_attn_theta_log, L2_attn_D)
    h = h + _L2_ffn_ref(_layernorm(h, axis=-1), L2_ffn_W_gat, L2_ffn_att_src, L2_ffn_att_dst, L2_ffn_b_gat, L2_ffn_ln_gamma, L2_ffn_ln_beta, L2_ffn_W1, L2_ffn_b1, L2_ffn_W2, L2_ffn_b2, L2_ffn_edge_index)
    h = h + _L3_attn_ref(_layernorm(h, axis=-1), L3_attn_Wq, L3_attn_bq, L3_attn_Wk, L3_attn_bk, L3_attn_Wv, L3_attn_bv)
    h = h + _L3_ffn_ref(_layernorm(h, axis=-1), L3_ffn_Wg, L3_ffn_bg, L3_ffn_W1, L3_ffn_b1, L3_ffn_W2, L3_ffn_b2)
    return h

_drawn_inputs = setup_inputs


def setup_inputs(seed=0):
    import zlib

    import numpy as np

    out = dict(_drawn_inputs(seed))
    spreads = {'L0_attn_ln1_g': (1.0, 0.6),
     'L0_attn_ln1_b': (0.0, 0.8),
     'L0_attn_bx': (0.0, 0.8),
     'L0_attn_bo': (0.0, 0.8),
     'L0_attn_ln2_g': (1.0, 0.6),
     'L0_attn_ln2_b': (0.0, 0.8),
     'L0_attn_b1': (0.0, 0.8),
     'L0_attn_b2': (0.0, 0.8),
     'L0_ffn_b1': (0.0, 0.8),
     'L0_ffn_b2': (0.0, 0.8),
     'L2_ffn_b_gat': (0.0, 0.8),
     'L2_ffn_ln_gamma': (1.0, 0.6),
     'L2_ffn_ln_beta': (0.0, 0.8),
     'L2_ffn_b1': (0.0, 0.8),
     'L2_ffn_b2': (0.0, 2.0),
     'L3_ffn_bg': (0.0, 0.8),
     'L3_ffn_b1': (0.0, 2.0),
     'L3_ffn_b2': (0.0, 2.0)}
    factors = {'L0_tok_bo': 8.0,
     'L0_attn_Wx': 8.0,
     'L0_attn_Wq': 8.0,
     'L0_attn_Wk': 8.0,
     'L0_attn_Wv': 8.0,
     'L0_attn_Wo': 8.0,
     'L0_attn_W1': 8.0,
     'L0_attn_W2': 8.0,
     'L0_ffn_wr': 8.0,
     'L0_ffn_w1': 8.0,
     'L0_ffn_w2': 8.0,
     'L1_attn_a': 8.0,
     'L1_attn_W_B': 8.0,
     'L1_attn_b_B': 8.0,
     'L1_attn_W_C': 8.0,
     'L1_attn_b_C': 8.0,
     'L1_attn_W_D': 4.977,
     'L1_attn_b_D': 8.0,
     'L1_ffn_router_w': 8.0,
     'L1_ffn_router_b': 8.0,
     'L1_ffn_W1': 8.0,
     'L1_ffn_b1': 8.0,
     'L1_ffn_W2': 8.0,
     'L1_ffn_b2': 29.825,
     'L2_attn_nu_log': 3.396,
     'L2_attn_theta_log': 3.478,
     'L2_attn_D': 31.334,
     'L2_ffn_W_gat': 8.0,
     'L2_ffn_att_src': 8.0,
     'L2_ffn_att_dst': 8.0,
     'L2_ffn_W1': 8.0,
     'L2_ffn_W2': 8.0,
     'L3_attn_Wq': 8.0,
     'L3_attn_bq': 8.0,
     'L3_attn_Wk': 8.0,
     'L3_attn_bk': 64.0,
     'L3_attn_Wv': 8.0,
     'L3_attn_bv': 31.632,
     'L3_ffn_Wg': 8.0,
     'L3_ffn_W1': 8.0,
     'L3_ffn_W2': 8.0}
    for name, (base, spread) in spreads.items():
        noise = np.random.default_rng([zlib.crc32(name.encode()), seed]).standard_normal(out[name].shape)
        drawn = base * np.exp(spread * noise) if base else spread * noise
        out[name] = jnp.asarray(drawn.astype(out[name].dtype))
    for name, factor in factors.items():
        out[name] = (out[name] * factor).astype(out[name].dtype)
    return out
```

```python
from contextlib import ExitStack

import numpy as np

import concourse.bass as bass
from concourse import mybir

P = 128
B, D = 2, 64
N_IMG, N_TXT = 1024, 128
N = N_IMG + N_TXT
KB = N // P
IB = N_IMG // P
Q = KB * B
CH = 384
NCH = N // CH
BC = CH // P
HEADS, DH, KR = 8, 32, 4
HR = HEADS * KR
EPS = 1e-5
TOPK = int(0.5 * N) - 1
DT = 1.0 / N
E1, H1 = 32, 16
E2 = 4
E3 = 8
NODES = B * N
NT = NODES // P
FEAT = 20
EDGES = 262144
EC = EDGES // P
SCALE = float(D) ** -0.5
TWO_PI = 2.0 * float(np.pi)
TWO_PI_HI = 6.28125
TWO_PI_LO = TWO_PI - TWO_PI_HI
BIG = 1e30
HG = 32
NHI, NLO = 36, 64
SLOTS = 64
PASSES = EC // SLOTS
PASS_STEPS = 15
GRP = 4

ALU = mybir.AluOpType
ACT = mybir.ActivationFunctionType
AX = mybir.AxisListType
F32 = mybir.dt.float32
BF16 = mybir.dt.bfloat16
I32 = mybir.dt.int32

GROUPS = [
    [("ident", P), ("tok_Wq", P), ("tok_Wk", P), ("tok_Wv", P), ("tok_Wo", P), ("tok_bq", 1), ("tok_bk", 1),
     ("tok_bv", D), ("tok_bo", D), ("prelu", 1)],
    [("WxT", 2 * P), ("WqBD", 2 * HR), ("WkBD", 4 * HR), ("bxrep", 2 * P), ("bxcol", 2), ("WxD", 2 * P),
     ("headmask", 2 * HR), ("WvT", P), ("Wo", 2 * D), ("a_bo", D), ("ln1_g", 1), ("ln1_b", 1), ("ln2_g", 1),
     ("ln2_b", 1), ("a_W1", 2 * P), ("a_b1", 2), ("a_W2", 2 * D), ("a_b2", D)],
    [("wr", P), ("br", 1), ("tri", P), ("f_w1", 2 * P), ("f_b1", 2), ("f_w2", 2 * D), ("f_b2", D)],
    [("WB", P), ("bB", 1), ("a", 1), ("WC", P), ("WD", P), ("bC", D), ("bD", D),
     ("rw", D), ("rb", E1), ("iota", E1), ("m_W1", 4 * P), ("m_b1", 4), ("m_W2", 4 * D), ("m_b2", P),
     ("sel1", 4 * P)],
    [("Bre", P), ("Bim", P), ("nu", 1), ("theta", 1), ("Cre", P), ("Cim", P), ("Dskip", D),
     ("Wgat", 32), ("att_src", 16), ("att_dst", 16), ("b_gat", 16), ("g_gamma", 16), ("g_beta", 16),
     ("g_W1", 4 * P), ("g_b1", 4), ("g_W2", 4 * D), ("g_b2", 4 * D), ("iota128", P), ("iota_p", 1)],
    [("Wq3", P), ("Wk3", P), ("Wv3", P), ("bq3", 1), ("bk3", 1), ("bv3", D), ("causal", P),
     ("Wg3", D), ("bg3", E3), ("e_W1", 8 * P), ("e_b1", 8), ("e_W2", 8 * D), ("e_b2", P), ("sel3", 8 * P)],
]
COLS, _at = {}, 0
GROUP_COLS = []
for _g in GROUPS:
    _from = _at
    for _name, _width in _g:
        COLS[_name] = (_at, _width)
        _at += _width
    GROUP_COLS.append((_from, _at))
WIDTH = _at


def build(nc, xT, txt, gammaT, edges, weights, out):
    ctx = ExitStack()
    with ctx:
        def sb(name, shape, dt=F32):
            return ctx.enter_context(nc.sbuf_tensor(name, shape, dt))

        def sem(name):
            return ctx.enter_context(nc.semaphore(name))

        ps = ctx.enter_context(nc.psum_tensor("ps", [P, 8, 512], F32))
        W_all = sb("weights_sb", [P, WIDTH])
        H = sb("H", [P, KB, B, D])
        X = sb("X", [P, KB, B, D])
        Z = sb("Z", [P, KB, B, D])
        XC = sb("XC", [P, KB, B, D])
        T1 = sb("T1", [P, KB, B, D])
        T2 = sb("T2", [P, KB, B, D])
        XF = sb("XF", [P, N])
        SA = sb("SA", [P, 2, N])
        VT = sb("VT", [P, KB, B, D])
        G = sb("G", [P, 2, E3, CH])
        gam = sb("gam", [P, IB, N_IMG])
        ring = sb("ring", [P, 4, 512])
        st = sb("st", [P, 16, Q])
        small = sb("small", [P, 64])
        KT = sb("KT", [P, KB, D])
        QS = sb("QS", [P, KB, D])
        LG = sb("LG", [P, KB, D])
        NF = sb("NF", [P, N])
        NB = sb("NB", [P, N], BF16)
        WQ = sb("WQ", [P, D])
        WK = sb("WK", [P, D])
        BQ = sb("BQ", [P, HR])
        BK = sb("BK", [D, 1])
        WVO = sb("WVO", [P, 2, D])
        UTs = sb("UTs", [P, HR])
        KX = sb("KX", [P, B, 2, HR])
        MB = sb("MB", [D, P])
        selb = sb("selb", [P, 12, P], BF16)
        powers = sb("powers", [P, 8, 4])
        coef = sb("coef", [P, 8])
        lam = sb("lam", [P, 12])
        lam_i = sb("lam_i", [P, 1], I32)
        bcd = sb("bcd", [P, D])
        iota64 = sb("iota64", [P, E1])
        PR = sb("PR", [P, 2, N])
        PT = sb("PT", [P, 2, KB, P])
        den3 = sb("den3", [P, 4, Q])
        held = sb("held", [1, 128])
        nhalf = sb("nhalf", [P, Q])

        def w(name, rows=slice(0, P)):
            at, width = COLS[name]
            return W_all[rows, at:at + width]

        T2_flat = T2[:, :, :, :].rearrange("p k b d -> p (k b d)")
        junk = ring[:, :, :].rearrange("p a b -> p (a b)")
        WROW = SA
        WBANK = ((3, 4, 5), (6, 7, 0))

        def flat(t):
            return t[:, :, :, :].rearrange("p k b d -> p (k b) d")

        def blk(t, k):
            return t[:, k, :, :].rearrange("p b d -> p (b d)")

        weights_in = [sem(f"weights_in_{i}") for i in range(len(GROUPS))]
        x_in, txt_in, out_stored = sem("x_in"), sem("txt_in"), sem("out_stored")
        gamma_in = [sem(f"gamma_in_{th}") for th in range(2)]
        dve_step, act_step, pool_step = sem("dve_step"), sem("act_step"), sem("pool_step")

        var_ready, rstd_ready, norm_ready = sem("var_ready"), sem("rstd_ready"), sem("norm_ready")
        turned, xf_ready = sem("turned"), sem("xf_ready")
        h_ready = sem("h_ready")

        def hold(engine, semaphore, value, alone=False):
            engine.wait_ge(semaphore, value)
            if alone:
                nc.vector.memset(held[:, sites[0]:sites[0] + 1], 0.0)
                sites[0] += 1

        sites = [0]

        class Chain:

            def __init__(self, engine, semaphore):
                self.engine, self.semaphore, self.count = engine, semaphore, 0

            def __call__(self, instruction):
                self.count += 1
                instruction.then_inc(self.semaphore, 1)
                self.engine.wait_ge(self.semaphore, self.count)

        t13 = T1[:, :, :, :].rearrange("p (c j) b d -> p c (j b) d", c=NCH)

        words = gam[:, :, :].rearrange("p j t -> p (j t)")
        e_src, e_dst = (words[:, i * EC:(i + 1) * EC].bitcast(I32) for i in range(2))
        e_key = words[:, 2 * EC:3 * EC]
        e_in = words[:, 3 * EC:4 * EC]
        e_in_i = e_in.bitcast(I32)
        digit_hi = words[:, 3 * EC:3 * EC + EC // 2].bitcast(BF16)
        digit_lo = words[:, 3 * EC + EC // 2:4 * EC].bitcast(BF16)
        half = HG * (NHI + NLO) // 2
        oh_hi = [words[:, s * half:s * half + HG * NHI // 2].bitcast(BF16).rearrange("p (v t) -> p v t", t=HG) for s in range(2)]
        oh_lo = [words[:, s * half + HG * NHI // 2:(s + 1) * half].bitcast(BF16).rearrange("p (v t) -> p v t", t=HG) for s in range(2)]
        digit_values = sb("digit_values", [P, NLO, HG], BF16)
        zeros = sb("zeros", [P, P])
        ident_b = sb("ident_b", [P, P], BF16)
        iota_p = sb("iota_p", [P, 1])
        key = sb("key", [P, SLOTS])
        key_i = sb("key_i", [P, SLOTS], I32)
        field = sb("field", [P, 4, SLOTS], I32)
        lo_b = sb("lo_b", [P, 2, SLOTS], BF16)
        rest8 = sb("rest8", [P, 8])
        flag = sb("flag", [1, PASSES], I32)
        table = sb("table", [P, FEAT, NT])
        dst_score = sb("dst_score", [P, E2, NT])
        local_max = sb("local_max", [P, E2])
        score_max = sb("score_max", [P, E2])
        last = sb("last", [P, FEAT])
        n_last = sb("n_last", [P, NT])
        gate4 = sb("gate4", [P, Q, E2])
        pick4 = sb("pick4", [P, 3, Q, E2])
        SAw = SA[:, :, :].rearrange("p a n -> p (a n)")
        e_val = SAw[:, 0:SLOTS * FEAT].rearrange("p (s f) -> p s f", f=FEAT)
        e_dsc = SAw[:, SLOTS * FEAT:SLOTS * (FEAT + E2)].rearrange("p (s f) -> p s f", f=E2)
        e_tmp = SAw[:, SLOTS * (FEAT + E2):SLOTS * (FEAT + 3 * E2)].rearrange("p (a s f) -> p a s f", a=2, f=E2)
        PRw = PR[:, :, :].rearrange("p a n -> p (a n)")
        e_w = PRw[:, 0:SLOTS * FEAT].rearrange("p (s f) -> p s f", f=FEAT)
        node_w = PRw[:, SLOTS * FEAT:SLOTS * FEAT + 6 * E2 * NT].rearrange("p (a b h t) -> p a b h t", a=3, b=2, t=NT)
        PTw = PT[:, :, :, :].rearrange("p a j n -> p (a j n)")
        src_hi_oh = PTw[:, 0:SLOTS * NT].rearrange("p (s t) -> p s t", t=NT)
        dst_hi_oh = PTw[:, SLOTS * NT:2 * SLOTS * NT].rearrange("p (s t) -> p s t", t=NT)
        Gw = G[:, :, :, :].rearrange("p a j n -> p (a j n)")
        GF = GRP * FEAT * NT
        product = Gw[:, 0:GF].rearrange("p (g f t) -> p g f t", g=GRP, t=NT)
        product_d = Gw[:, 0:GRP * E2 * NT].rearrange("p (g f t) -> p g f t", g=GRP, t=NT)
        outer = [Gw[:, (1 + s) * GF:(2 + s) * GF].rearrange("p (g f t) -> p g f t", g=GRP, t=NT) for s in range(2)]
        dst_lo_oh = [Gw[:, 3 * GF + s * GRP * P:3 * GF + (s + 1) * GRP * P].rearrange("p (g n) -> p g n", g=GRP) for s in range(2)]
        oht = [[ring[:, 2 * s + i, :] for i in range(2)] for s in range(2)]
        GN = SLOTS // GRP
        def turned_chunks(u):
            return sum((v // 2 + 4) // 4 for v in range(u))

        block = ctx.enter_context(nc.Block())

        (tok_proj, tok_proj_used, score_ready, decay_ready, kept_step, kept_copied, tok_y) = (
            sem("tok_proj"), sem("tok_proj_used"), sem("score_ready"), sem("decay_ready"), sem("kept_step"),
            sem("kept_copied"), sem("tok_y"))
        merged_ready, merged_used = sem("merged_ready"), sem("merged_used")
        (klog_ready, kshift_ready, kexp_ready, knorm_ready, kturned, kt_ready, ut_ready, uts_ready, kx_ready,
         kxs_ready, m_ready, mb_ready) = (sem(n) for n in (
            "klog_ready", "kshift_ready", "kexp_ready", "knorm_ready", "kturned", "kt_ready", "ut_ready", "uts_ready",
            "kx_ready", "kxs_ready", "m_ready", "mb_ready"))
        qlog_ready, qshift_ready, qexp_ready, qs_ready, qturned, qf_ready, attn_ready = (sem(n) for n in (
            "qlog_ready", "qshift_ready", "qexp_ready", "qs_ready", "qturned", "qf_ready", "attn_ready"))
        wrow_ready, wrow_copied, wcol_ready, wcol_used = (sem(n) for n in ("wrow_ready", "wrow_copied", "wcol_ready", "wcol_used"))
        hid_ready = [sem(f"hid_ready_{m}") for m in range(5)]
        g_ready = [sem(f"g_ready_{m}") for m in range(5)]
        mlp_out = [sem(f"mlp_out_{m}") for m in range(5)]

        bu_ready, force_ready, scan_ready, y_ready, cd_ready, silu_ready = (sem(n) for n in (
            "bu_ready", "force_ready", "scan_ready", "y_ready", "cd_ready", "silu_ready"))
        coef_ready, lambda_ready = sem("coef_ready"), sem("lambda_ready")
        router_ready, gates_ready, gates_turned, gates_copied, selb_ready = (sem(n) for n in (
            "router_ready", "gates_ready", "gates_turned", "gates_copied", "selb_ready"))
        qk3_ready, qk3_used, v3_ready, v3_used, s3_ready, shift3_ready, p3_ready, pt3_ready, pt3_copied, o3_ready, o3_used = (
            sem(n) for n in ("qk3_ready", "qk3_used", "v3_ready", "v3_used", "s3_ready", "shift3_ready", "p3_ready",
                             "pt3_ready", "pt3_copied", "o3_ready", "o3_used"))

        edges_in, onehots_ready, counted, counts_used = (sem(n) for n in (
            "edges_in", "onehots_ready", "counted", "counts_used"))
        gat_ready, table_ready, local_max_ready, score_max_ready, last_ready = (sem(n) for n in (
            "gat_ready", "table_ready", "local_max_ready", "score_max_ready", "last_ready"))
        (taken, fields_ready, rest_ready, rest_turned, flag_ready, spread_ready, oht_ready, gathered, product_step,
         selected, edge_shift_ready, edge_exp_ready, outer_ready, scattered, edge_step, sums_open) = (sem(n) for n in (
            "taken", "fields_ready", "rest_ready", "rest_turned", "flag_ready", "spread_ready", "oht_ready", "gathered",
            "product_step", "selected", "edge_shift_ready", "edge_exp_ready", "outer_ready", "scattered", "edge_step",
            "sums_open"))
        node_shift_ready, node_exp_ready, gate_shift_ready, gate_exp_ready, gated = (sem(n) for n in (
            "node_shift_ready", "node_exp_ready", "gate_shift_ready", "gate_exp_ready", "gated"))
        cd_step = sem("cd_step")
        @block.sync
        def _(sp):
            sp.dma_start(W_all[:, slice(*GROUP_COLS[0])], weights[:, slice(*GROUP_COLS[0])]).then_inc(weights_in[0], 16)
            sp.dma_start(XF[:, 0:N_IMG], xT).then_inc(x_in, 16)
            gview = gammaT.rearrange("(j p) t -> p j t", p=P)
            for th in range(2):
                sp.dma_start(gam[:, :, th * 512:(th + 1) * 512], gview[:, :, th * 512:(th + 1) * 512]).then_inc(gamma_in[th], 16)
            sp.dma_start(H[:, IB, :, :], txt.rearrange("b p d -> p b d")).then_inc(txt_in, 16)
            for i in range(1, len(GROUPS)):
                sp.dma_start(W_all[:, slice(*GROUP_COLS[i])], weights[:, slice(*GROUP_COLS[i])]).then_inc(weights_in[i], 16)
            sp.wait_ge(decay_ready, 32)
            for i, dst in enumerate((e_src, e_dst)):
                sp.dma_start(dst, edges[i]).then_inc(edges_in, 16)
            sp.wait_ge(h_ready, 1)
            for b in range(B):
                sp.dma_start(out[b].rearrange("(k p) d -> p k d", p=P), H[:, :, b, :]).then_inc(out_stored, 16)
            sp.wait_ge(out_stored, 16 * B)

        @block.gpsimd
        def _(pool):
            nc.gpsimd.memset(nhalf[:, :], -0.5).then_inc(pool_step, 1)
            pool.wait_ge(pool_step, 1)

            def rstd(n):
                pool.wait_ge(var_ready, n + 1)
                nc.gpsimd.tensor_tensor(st[:, 3, :], st[:, 2, :], nhalf[:, :], ALU.pow).then_inc(rstd_ready, 1)

            pool.wait_ge(weights_in[3], 16)
            nc.gpsimd.tensor_copy(selb[:, 0:4, :], w("sel1").rearrange("p (j n) -> p j n", j=4)).then_inc(selb_ready, 1)
            pool.wait_ge(weights_in[5], 16)
            nc.gpsimd.tensor_copy(selb[:, 4:12, :], w("sel3").rearrange("p (j n) -> p j n", j=8)).then_inc(selb_ready, 1)

            for n in range(8):
                rstd(n)
            pool.wait_ge(local_max_ready, 1)
            nc.gpsimd.partition_all_reduce(score_max[:, :], local_max[:, :], P, bass.bass_isa.ReduceOp.max).then_inc(score_max_ready, 1)
            for n in range(8, 11):
                rstd(n)

        @block.scalar
        def _(act):
            step = Chain(act, act_step)

            def input_to_channels(t, scale=None, bias=None):
                for c in range(NCH):
                    act.wait_ge(turned, NCH * t + c + 1)
                    dst, src = XF[:, c * CH:(c + 1) * CH], ps[:, c, 0:CH]
                    if scale is None:
                        nc.scalar.activation(dst, src, ACT.Copy).then_inc(xf_ready, 1)
                    else:
                        nc.scalar.activation(dst, src, ACT.Identity, bias=bias, scale=scale).then_inc(xf_ready, 1)

            def mlp(m, J, func, bias):
                for s in range(2 * NCH):
                    for j in range(J):
                        n = s * J + j
                        act.wait_ge(hid_ready[m], n + 1)
                        if s >= 2 and j == 0:
                            act.wait_ge(mlp_out[m], (s - 1) * (BC if m == 3 else 1))
                        nc.scalar.activation(G[:, s % 2, j, :], ps[:, 3 + n % 5, 0:CH], func,
                                             bias=bias[:, j:j + 1]).then_inc(g_ready[m], 1)

            act.wait_ge(weights_in[0], 16)
            act.wait_ge(tok_proj, 1)
            for i, (name, dst) in enumerate((("tok_bq", SA[:, 0, :]), ("tok_bk", SA[:, 1, :]))):
                for th in range(2):
                    nc.scalar.activation(dst[:, th * 512:(th + 1) * 512], ps[:, 2 * i + th, :], ACT.Identity,
                                         bias=w(name), scale=1.0).then_inc(tok_proj_used, 1)
            for th in range(2):
                act.wait_ge(kept_step, 16 * (th + 1))
                nc.scalar.activation(T2_flat[:, th * 512:(th + 1) * 512], ps[:, 6 + th, :], ACT.Copy).then_inc(kept_copied, 1)

            act.wait_ge(weights_in[1], 16)
            input_to_channels(0, w("ln1_g"), w("ln1_b"))
            act.wait_ge(kshift_ready, 1)
            nc.scalar.activation(NF[0:D, :].rearrange("p (c n) -> p c n", c=NCH), ps[0:D, 0:NCH, 0:CH], ACT.Exp,
                                 bias=small[0:D, 4:5], accum_out=small[0:D, 5:6]).then_inc(kexp_ready, 1)
            act.wait_ge(qshift_ready, 1)
            nc.scalar.activation(QS[:, :, :], LG[:, :, :], ACT.Exp).then_inc(qexp_ready, 1)
            for c in range(NCH):
                act.wait_ge(qturned, c + 1)
                nc.scalar.activation(NF[0:D, c * CH:(c + 1) * CH], ps[0:D, 3 + c, 0:CH], ACT.Copy).then_inc(qf_ready, 1)
            input_to_channels(1, w("ln2_g"), w("ln2_b"))
            mlp(0, 2, ACT.Gelu, w("a_b1"))

            act.wait_ge(weights_in[2], 16)
            input_to_channels(2)
            for b in range(B):
                act.wait_ge(wrow_ready, b + 1)
                for c in range(NCH):
                    nc.scalar.activation(WROW[:, b, c * CH:(c + 1) * CH], ps[:, WBANK[b][c], 0:CH], ACT.Identity,
                                         bias=w("br"), scale=1.0).then_inc(wrow_copied, 1)
            mlp(1, 2, ACT.Gelu_apprx_tanh, w("f_b1"))

            def gates_to_channels():
                for c in range(NCH):
                    act.wait_ge(gates_turned, gates[0] * NCH + c + 1)
                    nc.scalar.activation(NF[:, c * CH:(c + 1) * CH], ps[:, 3 + c, 0:CH], ACT.Copy).then_inc(gates_copied, 1)
                    nc.scalar.activation(NB[:, c * CH:(c + 1) * CH], ps[:, 3 + c, 0:CH], ACT.Copy, bias=-1.0).then_inc(gates_copied, 1)
                gates[0] += 1

            gates = [0]
            input_to_channels(3)
            act.wait_ge(coef_ready, 1)
            for c in range(NCH):
                act.wait_ge(bu_ready, c + 1)
                for s in range(2):
                    nc.scalar.activation(SA[:, s, c * CH:(c + 1) * CH], ps[:, 3 + c, 0:CH], ACT.Identity,
                                         bias=coef[:, 4 + s:5 + s], scale=coef[:, 2 + s:3 + s]).then_inc(force_ready, 1)
            act.wait_ge(cd_ready, 1)
            step(nc.scalar.activation(flat(Z), flat(T1), ACT.Gelu))
            nc.scalar.activation(flat(T2), flat(Z), ACT.Sigmoid).then_inc(silu_ready, 1)
            input_to_channels(4)
            gates_to_channels()
            mlp(2, 4, ACT.Relu, w("m_b1"))
            act.wait_ge(weights_in[4], 16)
            step(nc.scalar.activation(lam[:, 0:1], w("nu"), ACT.Exp))
            step(nc.scalar.activation(lam[:, 1:2], lam[:, 0:1], ACT.Exp, scale=-1.0))
            nc.scalar.activation(lam[:, 2:3], w("theta"), ACT.Exp).then_inc(lambda_ready, 1)
            act.wait_ge(coef_ready, 2)
            nc.scalar.activation(lam[:, 5:6], lam[:, 3:4], ACT.Sin).then_inc(lambda_ready, 1)
            nc.scalar.activation(lam[:, 6:7], lam[:, 4:5], ACT.Sin).then_inc(lambda_ready, 1)
            act.wait_ge(coef_ready, 3)
            step(nc.scalar.activation(lam[:, 8:9], lam[:, 7:8], ACT.Sqrt))
            input_to_channels(5)
            for s in range(2):
                for c in range(NCH):
                    act.wait_ge(bu_ready, NCH + s * NCH + c + 1)
                    nc.scalar.activation(SA[:, s, c * CH:(c + 1) * CH], ps[:, (3 + s * NCH + c) % 8, 0:CH], ACT.Copy,
                                         scale=lam[:, 8:9]).then_inc(force_ready, 1)

            input_to_channels(6)

            def edge_pass(it):
                act.wait_ge(edge_shift_ready, it + 1)
                nc.scalar.activation(e_w[:, :, 0:E2], e_tmp[:, 0, :, :], ACT.Exp).then_inc(edge_exp_ready, 1)

            edge_pass(0)
            act.wait_ge(flag_ready, 1)
            more = act.value_load(flag[0:1, 0:1], min_val=0, max_val=1)
            with act.If(more > 0):
                with act.Fori(1, PASSES) as it:
                    more = act.value_load(flag[0:1, bass.ds(it - 1, 1)], min_val=0, max_val=1)
                    with act.If(more > 0):
                        edge_pass(it)
            act.wait_ge(node_shift_ready, 1)
            nc.scalar.activation(node_w[:, 0, :, :, :], node_w[:, 1, :, :, :], ACT.Exp).then_inc(node_exp_ready, 1)
            act.wait_ge(gate_shift_ready, 1)
            nc.scalar.activation(st[:, 12, :], st[:, 13, :], ACT.Exp).then_inc(gate_exp_ready, 1)
            mlp(3, 4, ACT.Gelu, w("g_b1"))
            act.wait_ge(weights_in[5], 16)
            input_to_channels(7)
            for s, name in enumerate(("bq3", "bk3")):
                for c in range(NCH):
                    act.wait_ge(qk3_ready, s * NCH + c + 1)
                    nc.scalar.activation(SA[:, s, c * CH:(c + 1) * CH], ps[:, (3 + s * NCH + c) % 8, 0:CH], ACT.Identity,
                                         bias=w(name), scale=1.0).then_inc(qk3_used, 1)

            def expo(u):
                L = (u // 2 + 1) * P
                act.wait_ge(shift3_ready, u + 1)
                if u >= 2:
                    act.wait_ge(pt3_ready, turned_chunks(u - 1))
                nc.scalar.activation(PR[:, u % 2, 0:L], ps[:, 3 * (u % 2):3 * (u % 2) + 3, :].rearrange("p c n -> p (c n)")[:, 0:L],
                                     ACT.Exp, bias=den3[:, 1, u:u + 1], scale=SCALE, accum_out=den3[:, 2, u:u + 1]).then_inc(p3_ready, 1)

            def copies(u):
                if u >= 2:
                    act.wait_ge(o3_ready, u - 1)
                for cc in range(turned_chunks(u), turned_chunks(u + 1)):
                    act.wait_ge(pt3_ready, cc + 1)
                    c = cc - turned_chunks(u)
                    j, m = 4 * c, min(4, u // 2 + 1 - 4 * c)
                    nc.scalar.activation(PT[:, u % 2, j:j + m, :], ps[:, 3 * (u % 2) + c, 0:m * P].rearrange("p (j n) -> p j n", n=P),
                                         ACT.Copy).then_inc(pt3_copied, 1)

            expo(0)
            for u in range(Q):
                if u + 1 < Q:
                    expo(u + 1)
                copies(u)
            input_to_channels(8)
            gates_to_channels()
            mlp(4, 8, ACT.Gelu, w("e_b1"))

        @block.vector
        def _(dve):
            link = Chain(dve, dve_step)
            V = nc.vector

            def bc(ap, n):
                return ap.unsqueeze(ap.ndim).broadcast_to(list(ap.shape) + [n])

            def row(ap, n=Q):
                return ap.unsqueeze(1).broadcast_to([ap.shape[0], n, ap.shape[1]])

            def layernorm(src, dst, n, width=D, centred=None, squares=None):
                centred = flat(XC) if centred is None else centred
                squares = flat(T1) if squares is None else squares
                link(V.reduce_sum(st[:, 0, :], src, AX.X))
                link(V.tensor_scalar(st[:, 1, :], st[:, 0, :], 1.0 / width, None, ALU.mult))
                link(V.tensor_tensor(centred, src, bc(st[:, 1, :], width), ALU.subtract))
                link(V.tensor_tensor(squares, centred, centred, ALU.mult))
                link(V.reduce_sum(st[:, 4, :], squares, AX.X))
                V.tensor_scalar(st[:, 2, :], st[:, 4, :], 1.0 / width, EPS, ALU.mult, ALU.add).then_inc(var_ready, 1)
                dve.wait_ge(rstd_ready, n + 1)
                V.tensor_tensor(dst, centred, bc(st[:, 3, :], width), ALU.mult).then_inc(norm_ready, 1)
                dve.wait_ge(norm_ready, n + 1)

            def three(t):
                return t[:, :, :, :].rearrange("p (c j) b d -> p c (j b d)", c=NCH)

            def out_psum():
                return ps[:, 0:NCH, 0:CH]

            dve.wait_ge(weights_in[0], 16)
            dve.wait_ge(tok_proj, 2)
            for i in range(2):
                V.tensor_tensor(VT[:, 4 * i:4 * i + 4, :, :].rearrange("p k b d -> p (k b) d"),
                                ps[:, 4 + i, :].rearrange("p (q d) -> p q d", d=D), row(w("tok_bv"), 8),
                                ALU.add).then_inc(tok_proj_used, 1)
            for th in range(2):
                dve.wait_ge(gamma_in[th], 16)
                for u in range(16 * th, 16 * th + 16):
                    dve.wait_ge(score_ready, u + 1)
                    if u >= 4:
                        dve.wait_ge(kept_step, u - 3)
                    V.tensor_tensor(ring[:, u % 4, :], ps[:, u % 4, :],
                                    gam[:, u % IB, th * 512:(th + 1) * 512], ALU.mult).then_inc(decay_ready, 1)
            for i in range(2):
                dve.wait_ge(tok_y, i + 1)
                y = flat(T1)[:, 0:8, :]
                link(V.tensor_tensor(y, ps[:, i, :].rearrange("p (q d) -> p q d", d=D), row(w("tok_bo"), 8), ALU.add))
                neg = flat(XC)[:, 0:8, :]
                link(V.tensor_scalar(neg, y, 0.0, w("prelu"), ALU.min, ALU.mult))
                link(V.scalar_tensor_tensor(flat(H)[:, 8 * i:8 * i + 8, :], y, 0.0, neg, ALU.max, ALU.add))
            dve.wait_ge(txt_in, 16)

            dve.wait_ge(weights_in[1], 16)
            dve.wait_ge(merged_ready, 1)
            V.memset(WQ[:, :], 0.0).then_inc(dve_step, 1)
            V.memset(WK[:, :], 0.0).then_inc(dve_step, 1)
            link.count += 2
            link(V.memset(MB[:, :], 0.0))
            for b in range(B):
                rows = slice(b * D, (b + 1) * D)
                V.tensor_copy(WQ[rows, b * HR:(b + 1) * HR], ps[rows, 5, 0:HR]).then_inc(merged_used, 1)
                V.tensor_copy(WK[rows, b * HR:(b + 1) * HR], ps[rows, 5, HR:2 * HR]).then_inc(merged_used, 1)
            V.tensor_copy(BQ[:, :], ps[:, 5, 64:96]).then_inc(merged_used, 1)
            V.tensor_copy(BK[:, :], ps[0:D, 5, 96:97]).then_inc(merged_used, 1)
            V.tensor_copy(WVO[:, :, :], ps[:, 5, 128:256].rearrange("p (t d) -> p t d", t=2)).then_inc(merged_used, 1)
            layernorm(flat(H), flat(X), 0)
            layernorm(flat(X), flat(Z), 1)
            dve.wait_ge(klog_ready, 1)
            dve.wait_ge(merged_used, 7)
            link(V.tensor_reduce(small[0:D, 0:1], ps[0:D, 0:NCH, 0:CH], AX.XY, ALU.max))
            link(V.tensor_tensor(small[0:D, 1:2], small[0:D, 0:1], BK[:, :], ALU.add))
            V.tensor_tensor(small[0:D, 4:5], BK[:, :], small[0:D, 1:2], ALU.subtract).then_inc(kshift_ready, 1)
            dve.wait_ge(kexp_ready, 1)
            link(V.reciprocal(small[0:D, 6:7], small[0:D, 5:6]))
            V.tensor_scalar(NF[0:D, :], NF[0:D, :], small[0:D, 6:7], None, ALU.mult).then_inc(knorm_ready, 1)
            dve.wait_ge(kturned, 1)
            V.tensor_copy(KT[:, :, :].rearrange("p (c j) r -> p c (j r)", c=NCH), ps[:, 0:NCH, 0:BC * D]).then_inc(kt_ready, 1)
            dve.wait_ge(ut_ready, 1)
            for b in range(B):
                rows = slice(b * D, (b + 1) * D)
                V.tensor_scalar(UTs[rows, :], ps[rows, 6, b * HR:(b + 1) * HR], w("ln1_g", rows), w("ln1_b", rows),
                                ALU.mult, ALU.add).then_inc(uts_ready, 1)
            dve.wait_ge(kx_ready, 1)
            for b in range(B):
                for t in range(2):
                    V.scalar_tensor_tensor(KX[:, b, t, :], ps[:, 7 * b, t * HR:(t + 1) * HR],
                                           w("bxcol")[:, t:t + 1], w("headmask")[:, t * HR:(t + 1) * HR],
                                           ALU.add, ALU.mult).then_inc(kxs_ready, 1)
            dve.wait_ge(m_ready, 1)
            for b in range(B):
                V.tensor_copy(MB[b * HR:(b + 1) * HR, b * D:(b + 1) * D],
                              ps[b * HR:(b + 1) * HR, 6, 128:128 + D]).then_inc(mb_ready, 1)
            dve.wait_ge(qlog_ready, 1)
            lq = LG[:, :, :].rearrange("p (c j) (b r) -> p c (j b) r", c=NCH, b=B)
            bq = BQ[:, :].unsqueeze(1).broadcast_to([P, BC * B, HR])
            for c in range(NCH):
                V.tensor_tensor(lq[:, c], ps[:, 3 + c, 0:BC * D].rearrange("p (q r) -> p q r", r=HR), bq,
                                ALU.add).then_inc(dve_step, 1)
                link.count += 1
            dve.wait_ge(dve_step, link.count)
            l4 = LG[:, :, :].rearrange("p k (g r) -> p (k g) r", r=KR)
            q4 = QS[:, :, :].rearrange("p k (g r) -> p (k g) r", r=KR)
            gsum = T2_flat[:, 0:KB * 16]
            link(V.tensor_reduce(gsum, l4, AX.X, ALU.max))
            V.tensor_tensor(l4, l4, bc(gsum, KR), ALU.subtract).then_inc(qshift_ready, 1)
            dve.wait_ge(qexp_ready, 1)
            link(V.reduce_sum(gsum, q4, AX.X))
            grec = T2_flat[:, 256:256 + KB * 16]
            link(V.reciprocal(grec, gsum))
            V.tensor_tensor(q4, q4, bc(grec, KR), ALU.mult).then_inc(qs_ready, 1)
            link(V.tensor_tensor(flat(T1), flat(X), row(w("a_bo")), ALU.add))
            dve.wait_ge(attn_ready, 1)
            dve.wait_ge(qs_ready, 1)
            link(V.tensor_tensor(three(T2), out_psum(), three(T1), ALU.add))
            layernorm(flat(T2), flat(Z), 2)
            link(V.tensor_tensor(flat(T1), flat(T2), row(w("a_b2")), ALU.add))
            link(V.tensor_tensor(flat(H), flat(H), flat(T1), ALU.add))
            dve.wait_ge(mlp_out[0], 2 * NCH)
            link(V.tensor_tensor(three(H), out_psum(), three(H), ALU.add))

            dve.wait_ge(weights_in[2], 16)
            layernorm(flat(H), flat(X), 3)
            dve.wait_ge(wcol_ready, 1)
            WC = st[:, 5, :]
            V.tensor_copy(WC, ps[:, 1, 0:Q]).then_inc(wcol_used, 1)
            dve.wait_ge(wcol_used, 1)
            link(V.memset(st[:, 6, :], 0.0))
            for k in range(KB):
                for b in range(B):
                    q = 2 * k + b
                    wq = WC[:, q:q + 1]
                    if k:
                        V.tensor_scalar(junk[:, 0:k * P], WROW[:, b, 0:k * P], wq, None, ALU.is_ge, ALU.add,
                                        accum_out=st[:, 6, q:q + 1]).then_inc(dve_step, 1)
                        link.count += 1
                        dve.wait_ge(dve_step, link.count)
                    link(V.tensor_scalar(junk[:, 0:N - k * P], WROW[:, b, k * P:N], wq, None, ALU.is_gt, ALU.add,
                                         accum_out=st[:, 7, q:q + 1]))
                    link(V.scalar_tensor_tensor(junk[:, 0:P], WROW[:, b, k * P:(k + 1) * P], wq, w("tri"), ALU.is_equal,
                                                ALU.mult, accum_out=st[:, 8, q:q + 1]))
            link(V.tensor_tensor(st[:, 6, :], st[:, 6, :], st[:, 7, :], ALU.add))
            link(V.tensor_tensor(st[:, 6, :], st[:, 6, :], st[:, 8, :], ALU.add))
            link(V.scalar_tensor_tensor(st[:, 9, :], st[:, 6, :], float(TOPK), WC, ALU.is_lt, ALU.mult))
            link(V.tensor_tensor(flat(H), flat(H), flat(X), ALU.add))
            dve.wait_ge(mlp_out[1], 2 * NCH)
            out3 = out_psum().rearrange("p c (q d) -> p c q d", d=D)
            for c in range(NCH):
                V.tensor_tensor(t13[:, c], out3[:, c], row(w("f_b2"), BC * B), ALU.add).then_inc(dve_step, 1)
                link.count += 1
            dve.wait_ge(dve_step, link.count)
            link(V.tensor_tensor(flat(T1), flat(T1), bc(st[:, 9, :], D), ALU.mult))
            link(V.tensor_tensor(flat(H), flat(H), flat(T1), ALU.add))

            def powers_of(levels=7):
                for l in range(levels):
                    p0, q0, r0 = (powers[:, l, i:i + 1] for i in range(3))
                    link(V.tensor_tensor(powers[:, l, 3:4], q0, r0, ALU.mult))
                    link(V.scalar_tensor_tensor(powers[:, l + 1, 0:1], p0, p0, powers[:, l, 3:4], ALU.mult, ALU.add))
                    link(V.scalar_tensor_tensor(powers[:, l + 1, 1:2], q0, 2.0, p0, ALU.mult, ALU.mult))
                    link(V.scalar_tensor_tensor(powers[:, l + 1, 2:3], r0, 2.0, p0, ALU.mult, ALU.mult))

            def scan(n):
                def update(dst, src, l, done=None):
                    p0, q0, r0 = (powers[:, l, i:i + 1] for i in range(3))
                    link(V.scalar_tensor_tensor(SA[:, :, dst], SA[:, :, src], p0, SA[:, :, dst], ALU.mult, ALU.add))
                    a = V.scalar_tensor_tensor(SA[:, 0, dst], SA[:, 1, src], q0, SA[:, 0, dst], ALU.mult, ALU.add)
                    a.then_inc(done if done is not None else dve_step, 1)
                    b = V.scalar_tensor_tensor(SA[:, 1, dst], SA[:, 0, src], r0, SA[:, 1, dst], ALU.mult, ALU.add)
                    if done is not None:
                        b.then_inc(done, 1)
                    else:
                        link.count += 1
                        link(b)

                for l in range(7):
                    d = 1 << l
                    update(slice(2 * d - 1, N, 2 * d), slice(d - 1, N - d, 2 * d), l)
                for i in range(1, KB):
                    update(slice(P * (i + 1) - 1, P * (i + 1)), slice(P * i - 1, P * i), 7)
                for l in range(6, -1, -1):
                    d = 1 << l
                    update(slice(3 * d - 1, N, 2 * d), slice(2 * d - 1, N - d, 2 * d), l, scan_ready if l == 0 else None)

            def pick(logits, E, onehot, tmp):
                link(V.tensor_reduce(st[:, 10, :], logits, AX.X, ALU.max))
                link(V.tensor_tensor(tmp, logits, bc(st[:, 10, :], E), ALU.is_equal))
                link(V.scalar_tensor_tensor(tmp, tmp, -64.0, row(iota64[:, 0:E]), ALU.mult, ALU.add))
                link(V.tensor_reduce(st[:, 11, :], tmp, AX.X, ALU.min))
                link(V.tensor_tensor(onehot, row(w("iota")[:, 0:E]), bc(st[:, 11, :], E), ALU.is_equal))

            dve.wait_ge(weights_in[3], 16)
            layernorm(flat(H), flat(X), 4)
            link(V.tensor_scalar(coef[:, 0:1], w("a"), DT * DT, 1.0, ALU.mult, ALU.add))
            link(V.reciprocal(powers[:, 0, 0:1], coef[:, 0:1]))
            link(V.tensor_scalar(powers[:, 0, 2:3], powers[:, 0, 0:1], DT, None, ALU.mult))
            link(V.scalar_tensor_tensor(powers[:, 0, 1:2], powers[:, 0, 2:3], -1.0, w("a"), ALU.mult, ALU.mult))
            link(V.tensor_copy(coef[:, 2:3], powers[:, 0, 2:3]))
            link(V.tensor_scalar(coef[:, 3:4], coef[:, 2:3], DT, None, ALU.mult))
            link(V.tensor_tensor(coef[:, 4:5], coef[:, 2:3], w("bB"), ALU.mult))
            V.tensor_tensor(coef[:, 5:6], coef[:, 3:4], w("bB"), ALU.mult).then_inc(coef_ready, 1)
            powers_of()
            link(V.tensor_tensor(bcd[:, :], w("bC"), w("bD"), ALU.add))
            link(V.tensor_scalar(iota64[:, :], w("iota"), 64.0, None, ALU.add))
            link(V.tensor_tensor(flat(H), flat(H), flat(X), ALU.add))
            dve.wait_ge(force_ready, 2 * NCH)
            scan(0)
            dve.wait_ge(y_ready, 1)
            out3 = out_psum().rearrange("p c (q d) -> p c q d", d=D)
            for c in range(NCH):
                V.tensor_tensor(t13[:, c], out3[:, c], row(bcd[:, :], BC * B), ALU.add).then_inc(cd_step, 1)
            dve.wait_ge(cd_step, NCH)
            V.engine_nop().then_inc(cd_ready, 1)
            dve.wait_ge(silu_ready, 1)
            link(V.tensor_tensor(flat(T1), flat(Z), flat(T2), ALU.mult))
            link(V.tensor_tensor(flat(H), flat(H), flat(T1), ALU.add))

            layernorm(flat(H), flat(X), 5)
            link(V.memset(flat(Z), 0.0))
            dve.wait_ge(router_ready, 1)
            lv = LG[:, :, :].rearrange("p k (b e) -> p (k b) e", b=B)
            for c in range(NCH):
                V.tensor_tensor(lv[:, 6 * c:6 * c + 6, :], ps[:, 3 + c, 0:BC * D].rearrange("p (q e) -> p q e", e=E1),
                                row(w("rb"), 6), ALU.add).then_inc(dve_step, 1)
                link.count += 1
            dve.wait_ge(dve_step, link.count)
            pick(lv, E1, flat(Z)[:, :, 0:E1], QS[:, :, :].rearrange("p k (b e) -> p (k b) e", b=B))
            V.engine_nop().then_inc(gates_ready, 1)
            dve.wait_ge(mlp_out[2], 2 * NCH)
            link(V.scalar_tensor_tensor(three(H), out_psum(), 0.0, three(H), ALU.max, ALU.add))

            dve.wait_ge(weights_in[4], 16)
            layernorm(flat(H), flat(X), 6)
            dve.wait_ge(lambda_ready, 1)
            link(V.tensor_scalar(lam_i[:, :], lam[:, 2:3], 1.0 / TWO_PI, None, ALU.mult))
            link(V.tensor_copy(lam[:, 9:10], lam_i[:, :]))
            link(V.scalar_tensor_tensor(lam[:, 3:4], lam[:, 9:10], -TWO_PI_HI, lam[:, 2:3], ALU.mult, ALU.add))
            link(V.scalar_tensor_tensor(lam[:, 3:4], lam[:, 9:10], -TWO_PI_LO, lam[:, 3:4], ALU.mult, ALU.add))
            link(V.tensor_scalar(lam[:, 3:4], lam[:, 3:4], 3.1415925, -3.1415925, ALU.min, ALU.max))
            link(V.scalar_tensor_tensor(lam[:, 4:5], lam[:, 3:4], -1.0, lam[:, 3:4], ALU.mult, ALU.max))
            V.tensor_scalar(lam[:, 4:5], lam[:, 4:5], -1.0, TWO_PI / 4, ALU.mult, ALU.add).then_inc(coef_ready, 1)
            dve.wait_ge(lambda_ready, 3)
            link(V.tensor_tensor(powers[:, 0, 0:1], lam[:, 1:2], lam[:, 6:7], ALU.mult))
            link(V.tensor_tensor(powers[:, 0, 2:3], lam[:, 1:2], lam[:, 5:6], ALU.mult))
            link(V.tensor_scalar(powers[:, 0, 1:2], powers[:, 0, 2:3], -1.0, None, ALU.mult))
            link(V.tensor_tensor(lam[:, 10:11], powers[:, 0, 2:3], powers[:, 0, 2:3], ALU.mult))
            link(V.scalar_tensor_tensor(lam[:, 10:11], powers[:, 0, 0:1], powers[:, 0, 0:1], lam[:, 10:11], ALU.mult, ALU.add))
            link(V.tensor_scalar(lam[:, 10:11], lam[:, 10:11], -1.0, 1.0, ALU.mult, ALU.add))
            V.tensor_scalar(lam[:, 7:8], lam[:, 10:11], 0.0, None, ALU.max).then_inc(coef_ready, 1)
            powers_of()
            V.tensor_scalar(w("Cim"), w("Cim"), -1.0, None, ALU.mult).then_inc(coef_ready, 1)
            link(V.tensor_tensor(flat(T1), flat(X), row(w("Dskip")), ALU.mult))
            link(V.tensor_tensor(flat(H), flat(H), flat(T1), ALU.add))
            dve.wait_ge(force_ready, 4 * NCH)
            scan(1)
            dve.wait_ge(y_ready, 2)
            link(V.tensor_tensor(three(H), out_psum(), three(H), ALU.add))

            dve.wait_ge(edges_in, 32)
            last_node = float(NODES - 1)
            src_flag = e_in
            link(V.tensor_scalar(src_flag, e_src, last_node, None, ALU.is_lt))
            link(V.scalar_tensor_tensor(src_flag, e_dst, float(NODES), src_flag, ALU.is_lt, ALU.mult))
            link(V.scalar_tensor_tensor(e_key, e_dst, 4096.0, e_src, ALU.mult, ALU.add))
            link(V.scalar_tensor_tensor(e_key, e_key, 1.0, src_flag, ALU.add, ALU.mult))
            link(V.tensor_scalar(src_flag, e_src, last_node, None, ALU.is_ge))
            link(V.scalar_tensor_tensor(src_flag, e_dst, float(NODES), src_flag, ALU.is_lt, ALU.mult))
            link(V.scalar_tensor_tensor(src_flag, e_dst, -4095.0, src_flag, ALU.add, ALU.mult))
            link(V.tensor_scalar(e_in_i, src_flag, 4095.0, None, ALU.add))
            link(V.tensor_scalar(e_src, e_in_i, 6, None, ALU.logical_shift_right))
            link(V.tensor_scalar(e_dst, e_in_i, NLO - 1, None, ALU.bitwise_and))
            link(V.tensor_copy(digit_hi, e_src))
            link(V.tensor_copy(digit_lo, e_dst))
            link(V.tensor_copy(digit_values[:, :, :], bc(w("iota128")[:, 0:NLO], HG)))
            link(V.tensor_copy(ident_b[:, :], w("ident")))
            def onehots(i, s):
                at = bass.ts(i, HG)
                V.tensor_tensor(oh_hi[s], digit_hi[:, at].unsqueeze(1).broadcast_to([P, NHI, HG]),
                                digit_values[:, 0:NHI, :], ALU.is_equal).then_inc(onehots_ready, 1)
                V.tensor_tensor(oh_lo[s], digit_lo[:, at].unsqueeze(1).broadcast_to([P, NLO, HG]),
                                digit_values[:, :, :], ALU.is_equal).then_inc(onehots_ready, 1)

            for s in range(2):
                onehots(s, s)
            with dve.Fori(1, EC // HG // 2) as r:
                for s in range(2):
                    dve.wait_ge(counted, 2 * r + (s - 1))
                    onehots(2 * r + s, s)
            dve.wait_ge(counted, EC // HG)
            for o in range(2):
                V.tensor_copy(n_last[64 * o:64 * o + 64, :], ps[0:NLO, 7, 0:NHI].rearrange("p (t o) -> p t o", o=2)[:, :, o]).then_inc(counts_used, 1)

            layernorm(flat(H), flat(X), 7)
            dve.wait_ge(gat_ready, 1)
            hg = ps[:, 3, 0:Q * 16]
            link(V.tensor_copy(table[:, E2:FEAT, :].rearrange("p f (b k) -> p k b f", b=B), hg.rearrange("p (k b f) -> p k b f", b=B, f=16)))
            hq = hg.rearrange("p (q f) -> p q f", f=16)
            prod = flat(T1)[:, :, 0:16]
            for att, dst in (("att_src", table[:, 0:E2, :]), ("att_dst", dst_score[:, :, :])):
                link(V.tensor_tensor(prod, hq, row(w(att)), ALU.mult))
                link(V.reduce_sum(pick4[:, 0, :, :], prod.rearrange("p q (h e) -> p q h e", e=4), AX.X))
                link(V.tensor_copy(dst.rearrange("p h (b k) -> p k b h", b=B), pick4[:, 0, :, :].rearrange("p (k b) h -> p k b h", b=B)))
            V.tensor_reduce(local_max[:, :], table[:, 0:E2, :], AX.X, ALU.max).then_inc(local_max_ready, 1)
            V.tensor_copy(iota_p[:, :], w("iota_p")).then_inc(table_ready, 1)
            V.memset(zeros[:, :], 0.0).then_inc(sums_open, 1)
            dve.wait_ge(score_max_ready, 1)

            def edge_pass(it):
                for j in range(SLOTS // 8):
                    V.max(key[:, 8 * j:8 * j + 8], e_key).then_inc(taken, 1)
                    hold(dve, taken, it * (2 * (SLOTS // 8)) + (2 * j + 1), not isinstance(it, int))
                    V.match_replace(e_key, key[:, 8 * j:8 * j + 8], e_key, 0.0).then_inc(taken, 1)
                    hold(dve, taken, it * (2 * (SLOTS // 8)) + (2 * j + 2), not isinstance(it, int))
                n = [0]

                def linked(ins):
                    n[0] += 1
                    ins.then_inc(edge_step, 1)
                    hold(dve, edge_step, it * PASS_STEPS + n[0], not isinstance(it, int))

                linked(V.max(rest8[:, :], e_key))
                V.tensor_copy(rest8[:, 1:2], rest8[:, 0:1]).then_inc(rest_ready, 1)
                linked(V.tensor_scalar(key_i[:, :], key[:, :], -1.0, None, ALU.add))
                linked(V.tensor_scalar(field[:, 0, :], key_i[:, :], P - 1, None, ALU.bitwise_and))
                linked(V.tensor_scalar(field[:, 1, :], key_i[:, :], 7, 31, ALU.logical_shift_right, ALU.bitwise_and))
                linked(V.tensor_scalar(field[:, 2, :], key_i[:, :], 12, P - 1, ALU.logical_shift_right, ALU.bitwise_and))
                linked(V.tensor_scalar(field[:, 3, :], key_i[:, :], 19, None, ALU.arith_shift_right))
                for i in range(2):
                    V.tensor_copy(lo_b[:, i, :], field[:, 2 * i, :]).then_inc(fields_ready, 1)
                linked(V.tensor_tensor(src_hi_oh, bc(field[:, 1, :], NT), row(w("iota128")[:, 0:NT], SLOTS), ALU.is_equal))
                linked(V.tensor_tensor(dst_hi_oh, bc(field[:, 3, :], NT), row(w("iota128")[:, 0:NT], SLOTS), ALU.is_equal))
                hold(dve, rest_turned, it + 1, not isinstance(it, int))
                linked(V.tensor_reduce(small[0:1, 8:9], ps[0:1, 4, CH:CH + P], AX.X, ALU.max))
                V.tensor_scalar(flag[:, bass.ds(it, 1)], small[0:1, 8:9], 1.0, None, ALU.min).then_inc(flag_ready, 1)

                def select(g, s, first=False):
                    hold(dve, spread_ready, it * GN + g + 1, not isinstance(it, int))
                    if not first:
                        hold(dve, gathered, it * GN + g - 1, not isinstance(it, int))
                    for i in range(2):
                        V.tensor_scalar(oht[s][i], ps[:, 5 + i, :], iota_p[:, :], None, ALU.is_equal).then_inc(oht_ready, 1)
                    hold(dve, gathered, it * GN + g + 1, not isinstance(it, int))
                    at = bass.ts(g, GRP)
                    if not (first and s == 0):
                        hold(dve, selected, (it * GN + g) * 2, not isinstance(it, int))
                    V.tensor_tensor(product, ps[:, 0:GRP, 0:FEAT * NT].rearrange("p g (f t) -> p g f t", t=NT),
                                    src_hi_oh[:, at, :].unsqueeze(2).broadcast_to([P, GRP, FEAT, NT]), ALU.mult).then_inc(product_step, 1)
                    hold(dve, product_step, (it * GN + g) * 2 + 1, not isinstance(it, int))
                    V.reduce_sum(e_val[:, at, :], product, AX.X).then_inc(selected, 1)
                    hold(dve, selected, (it * GN + g) * 2 + 1, not isinstance(it, int))
                    V.tensor_tensor(product_d, ps[:, 4, 0:GRP * E2 * NT].rearrange("p (g f t) -> p g f t", f=E2, t=NT),
                                    dst_hi_oh[:, at, :].unsqueeze(2).broadcast_to([P, GRP, E2, NT]), ALU.mult).then_inc(product_step, 1)
                    hold(dve, product_step, (it * GN + g) * 2 + 2, not isinstance(it, int))
                    V.reduce_sum(e_dsc[:, at, :], product_d, AX.X).then_inc(selected, 1)

                for s in range(2):
                    select(s, s, first=isinstance(it, int))
                with dve.Fori(1, GN // 2) as r:
                    for s in range(2):
                        select(2 * r + s, s)
                hold(dve, selected, (it + 1) * GN * 2, not isinstance(it, int))
                t0, t1 = e_tmp[:, 0, :, :], e_tmp[:, 1, :, :]
                linked(V.tensor_tensor(t0, e_val[:, :, 0:E2], e_dsc[:, :, :], ALU.add))
                linked(V.tensor_tensor(t1, e_dsc[:, :, :], row(score_max[:, :], SLOTS), ALU.add))
                linked(V.scalar_tensor_tensor(t0, t0, 0.2, t0, ALU.mult, ALU.max))
                linked(V.scalar_tensor_tensor(t1, t1, 0.2, t1, ALU.mult, ALU.max))
                linked(V.tensor_tensor(t0, t0, t1, ALU.subtract))
                V.tensor_scalar(t0, t0, 0.0, None, ALU.min).then_inc(edge_shift_ready, 1)
                hold(dve, edge_exp_ready, it + 1, not isinstance(it, int))
                linked(V.tensor_tensor(e_w[:, :, E2:FEAT].rearrange("p s (h e) -> p s h e", e=4),
                                       e_val[:, :, E2:FEAT].rearrange("p s (h e) -> p s h e", e=4), bc(e_w[:, :, 0:E2], 4), ALU.mult))

                def spread_out(g, s, first=False):
                    if not first:
                        hold(dve, scattered, it * GN + g - 1, not isinstance(it, int))
                    at = bass.ts(g, GRP)
                    V.tensor_tensor(dst_lo_oh[s], row(w("iota128"), GRP), bc(field[:, 2, at], P), ALU.is_equal).then_inc(outer_ready, 1)
                    V.tensor_tensor(outer[s], bc(e_w[:, at, :], NT), dst_hi_oh[:, at, :].unsqueeze(2).broadcast_to([P, GRP, FEAT, NT]),
                                    ALU.mult).then_inc(outer_ready, 1)

                for s in range(2):
                    spread_out(s, s, first=isinstance(it, int))
                with dve.Fori(1, GN // 2) as r:
                    for s in range(2):
                        spread_out(2 * r + s, s)
                hold(dve, scattered, it * GN + GN, not isinstance(it, int))
                assert n[0] == PASS_STEPS

            edge_pass(0)
            more = dve.value_load(flag[0:1, 0:1], min_val=0, max_val=1)
            with dve.If(more > 0):
                with dve.Fori(1, PASSES) as it:
                    more = dve.value_load(flag[0:1, bass.ds(it - 1, 1)], min_val=0, max_val=1)
                    with dve.If(more > 0):
                        edge_pass(it)

            own, far, top = node_w[:, 1, 0, :, :], node_w[:, 1, 1, :, :], node_w[:, 2, 0, :, :]
            dve.wait_ge(last_ready, 1)
            link(V.tensor_copy(last[:, :], ps[:, 4, 0:FEAT]))
            link(V.tensor_tensor(own, table[:, 0:E2, :], dst_score[:, :, :], ALU.add))
            link(V.tensor_tensor(far, dst_score[:, :, :], bc(last[:, 0:E2], NT), ALU.add))
            link(V.tensor_tensor(top, dst_score[:, :, :], bc(score_max[:, :], NT), ALU.add))
            for x in (own, far, top):
                link(V.scalar_tensor_tensor(x, x, 0.2, x, ALU.mult, ALU.max))
            link(V.tensor_tensor(own, own, top, ALU.subtract))
            V.tensor_tensor(far, far, top, ALU.subtract).then_inc(node_shift_ready, 1)
            dve.wait_ge(node_exp_ready, 1)
            own, far = node_w[:, 0, 0, :, :], node_w[:, 0, 1, :, :]
            den, rden = node_w[:, 1, 0, :, :], node_w[:, 1, 1, :, :]
            dve.wait_ge(counts_used, 2)
            link(V.tensor_tensor(far, far, n_last[:, :].unsqueeze(1).broadcast_to([P, E2, NT]), ALU.mult))
            sums = ps[:, 7, 0:FEAT * NT].rearrange("p (f t) -> p f t", t=NT)
            link(V.tensor_tensor(den, own, far, ALU.add))
            link(V.tensor_tensor(den, den, sums[:, 0:E2, :], ALU.add))
            link(V.scalar_tensor_tensor(den, den, 1e-16, den, ALU.mult, ALU.add))
            link(V.reciprocal(rden, den))

            def four(x):
                return x.rearrange("p (h e) t -> p h e t", e=4)

            def per_head(x):
                return x.unsqueeze(2).broadcast_to([P, E2, 4, NT])

            a0 = T1[:, :, :, :].rearrange("p k b d -> p (k b d)")[:, 0:16 * NT].rearrange("p (f t) -> p f t", t=NT)
            a1 = T1[:, :, :, :].rearrange("p k b d -> p (k b d)")[:, 512:512 + 16 * NT].rearrange("p (f t) -> p f t", t=NT)
            link(V.tensor_tensor(four(a0), four(table[:, E2:FEAT, :]), per_head(own), ALU.mult))
            link(V.tensor_tensor(four(a1), four(bc(last[:, E2:FEAT], NT)), per_head(far), ALU.mult))
            link(V.tensor_tensor(a0, a0, a1, ALU.add))
            link(V.tensor_tensor(a0, a0, sums[:, E2:FEAT, :], ALU.add))
            link(V.tensor_tensor(four(a0), four(a0), per_head(rden), ALU.mult))
            agg = flat(T2)[:, :, 0:16]
            link(V.tensor_tensor(agg.rearrange("p (k b) f -> p k b f", b=B), a0.rearrange("p f (b k) -> p k b f", b=B),
                                 w("b_gat").unsqueeze(1).unsqueeze(1).broadcast_to([P, KB, B, 16]), ALU.add))
            layernorm(agg, agg, 8, 16, flat(XC)[:, :, 0:16], flat(T1)[:, :, 0:16])
            link(V.tensor_tensor(agg, agg, row(w("g_gamma")), ALU.mult))
            link(V.tensor_tensor(agg, agg, row(w("g_beta")), ALU.add))
            sc = pick4[:, 0, :, :]
            link(V.reduce_sum(sc, agg.rearrange("p q (h e) -> p q e h", e=4), AX.X))
            link(V.tensor_scalar(sc, sc, 0.25, None, ALU.mult))
            pick(sc, E2, pick4[:, 1, :, :], gate4[:, :, :])
            link(V.tensor_copy(st[:, 14, :], st[:, 10, :]))
            link(V.scalar_tensor_tensor(sc, pick4[:, 1, :, :], -BIG, sc, ALU.mult, ALU.add))
            pick(sc, E2, pick4[:, 2, :, :], gate4[:, :, :])
            V.tensor_tensor(st[:, 13, :], st[:, 10, :], st[:, 14, :], ALU.subtract).then_inc(gate_shift_ready, 1)
            dve.wait_ge(gate_exp_ready, 1)
            link(V.tensor_scalar(st[:, 14, :], st[:, 12, :], 1.0, None, ALU.add))
            link(V.reciprocal(st[:, 15, :], st[:, 14, :]))
            link(V.tensor_tensor(st[:, 12, :], st[:, 12, :], st[:, 15, :], ALU.mult))
            link(V.tensor_tensor(pick4[:, 1, :, :], pick4[:, 1, :, :], bc(st[:, 15, :], E2), ALU.mult))
            link(V.tensor_tensor(pick4[:, 2, :, :], pick4[:, 2, :, :], bc(st[:, 12, :], E2), ALU.mult))
            link(V.tensor_tensor(gate4[:, :, :], pick4[:, 1, :, :], pick4[:, 2, :, :], ALU.add))
            for v in range(Q):
                s, k = v // BC, v % BC
                kk, b = BC * (s // 2) + k, s % 2
                dve.wait_ge(mlp_out[3], v + 1)
                tmp = T2_flat[:, 0:256].rearrange("p (e d) -> p e d", e=E2)
                link(V.tensor_tensor(tmp, ps[:, v % 3, 0:256].rearrange("p (e d) -> p e d", e=E2), bc(gate4[:, 2 * kk + b, :], D), ALU.mult))
                V.reduce_sum(T1[:, kk, b, :], tmp.rearrange("p e d -> p d e"), AX.X).then_inc(gated, 1)
                dve.wait_ge(gated, v + 1)
            link(V.tensor_tensor(flat(H), flat(H), flat(T1), ALU.add))
            dve.wait_ge(weights_in[5], 16)
            layernorm(flat(H), flat(X), 9)
            dve.wait_ge(v3_ready, 1)
            for c in range(NCH):
                V.tensor_tensor(VT[:, BC * c:BC * c + BC, :, :].rearrange("p k b d -> p (k b) d"),
                                ps[:, 3 + c, 0:CH].rearrange("p (q d) -> p q d", d=D), row(w("bv3"), 6),
                                ALU.add).then_inc(v3_used, 1)

            def largest(u):
                i, base = u // 2, 3 * (u % 2)
                L = (i + 1) * P
                dve.wait_ge(s3_ready, u + 1)
                all3 = ps[:, base:base + 3, :].rearrange("p c n -> p (c n)")
                link(V.tensor_tensor(all3[:, L - P:L], all3[:, L - P:L], w("causal"), ALU.add))
                link(V.tensor_reduce(den3[:, 0, u:u + 1], all3[:, 0:L], AX.X, ALU.max))
                V.tensor_scalar(den3[:, 1, u:u + 1], den3[:, 0, u:u + 1], -SCALE, None, ALU.mult).then_inc(shift3_ready, 1)

            def attended(u):
                i, b = u // 2, u % 2
                dve.wait_ge(o3_ready, u + 1)
                link(V.reciprocal(den3[:, 3, u:u + 1], den3[:, 2, u:u + 1]))
                V.scalar_tensor_tensor(H[:, i, b, :], ps[:, 6 + u % 2, 0:D], den3[:, 3, u:u + 1], H[:, i, b, :],
                                       ALU.mult, ALU.add).then_inc(o3_used, 1)

            largest(0)
            for u in range(Q):
                if u + 1 < Q:
                    largest(u + 1)
                attended(u)
            dve.wait_ge(o3_used, Q)

            layernorm(flat(H), flat(X), 10)
            link(V.memset(flat(Z), 0.0))
            dve.wait_ge(router_ready, 2)
            lv = LG[:, :, :].rearrange("p k (b e) -> p (k b) e", b=B)[:, :, 0:E3]
            tmp = QS[:, :, :].rearrange("p k (b e) -> p (k b) e", b=B)
            for c in range(NCH):
                V.tensor_tensor(lv[:, 6 * c:6 * c + 6, :], ps[:, 3 + c, 0:BC * D].rearrange("p (q e) -> p q e", e=E1)[:, :, 0:E3],
                                row(w("bg3"), 6), ALU.add).then_inc(dve_step, 1)
                link.count += 1
            dve.wait_ge(dve_step, link.count)
            first, second = tmp[:, :, E3:2 * E3], tmp[:, :, 2 * E3:3 * E3]
            pick(lv, E3, first, tmp[:, :, 0:E3])
            link(V.scalar_tensor_tensor(lv, first, -BIG, lv, ALU.mult, ALU.add))
            pick(lv, E3, second, tmp[:, :, 0:E3])
            V.tensor_tensor(flat(Z)[:, :, 0:E3], first, second, ALU.add).then_inc(gates_ready, 1)
            dve.wait_ge(mlp_out[4], 2 * NCH)
            link(V.tensor_tensor(three(H), out_psum(), three(H), ALU.add))
            V.engine_nop().then_inc(h_ready, 1)

        @block.tensor
        def _(pe):
            MM = nc.tensor.matmul
            ident = w("ident")

            def turn(t, n, src):
                pe.wait_ge(norm_ready, n + 1)
                for c in range(NCH):
                    for j in range(BC):
                        last = nc.tensor.transpose(ps[:, c, j * P:(j + 1) * P], blk(src, BC * c + j), ident)
                    last.then_inc(turned, 1)

            def turn_narrow(src, done):
                for c in range(NCH):
                    for j in range(BC):
                        last = nc.tensor.transpose(ps[0:D, 3 + c, j * P:(j + 1) * P], src[:, BC * c + j, :], ident)
                    last.then_inc(done, 1)

            def mlp(m, t, J, w1, w2, gate=None, bias=None):
                def hidden(s):
                    c, b = s // 2, s % 2
                    rows = slice(b * D, (b + 1) * D)
                    if b == 0:
                        pe.wait_ge(xf_ready, NCH * t + c + 1)
                    for j in range(J):
                        n = s * J + j
                        if n >= 5:
                            pe.wait_ge(g_ready[m], n - 4)
                        o = ps[:, 3 + n % 5, 0:CH]
                        last = MM(o, w(w1, rows)[:, j * P:(j + 1) * P], XF[rows, c * CH:(c + 1) * CH], start=True, stop=gate is None)
                        if gate is not None:
                            last = MM(o, selb[rows, gate + j, :], NB[rows, c * CH:(c + 1) * CH],
                                      start=False, stop=True)
                        last.then_inc(hid_ready[m], 1)

                def output(s):
                    c, b = s // 2, s % 2
                    pe.wait_ge(g_ready[m], (s + 1) * J)
                    for k in range(BC):
                        o = ps[:, c, k * P + b * D:k * P + (b + 1) * D]
                        for j in range(J):
                            last = MM(o, G[:, s % 2, j, k * P:(k + 1) * P], w(w2)[:, j * D:(j + 1) * D],
                                      start=j == 0, stop=j == J - 1 and bias is None)
                        if bias is not None:
                            at = c * CH + k * P
                            last = MM(o, NF[:, at:at + P], w(bias)[:, b * D:(b + 1) * D],
                                      start=False, stop=True)
                    last.then_inc(mlp_out[m], 1)

                hidden(0)
                for s in range(2 * NCH):
                    if s + 1 < 2 * NCH:
                        hidden(s + 1)
                    output(s)

            pe.wait_ge(weights_in[0], 16)
            pe.wait_ge(x_in, 16)
            for i, name in enumerate(("tok_Wq", "tok_Wk")):
                for th in range(2):
                    last = MM(ps[:, 2 * i + th, :], w(name), XF[:, th * 512:(th + 1) * 512], start=True, stop=True)
            last.then_inc(tok_proj, 1)
            for k in range(IB):
                last = MM(ps[:, 4 + k // 4, (k % 4) * P:(k % 4 + 1) * P], XF[:, k * P:(k + 1) * P], w("tok_Wv"), start=True, stop=True)
            last.then_inc(tok_proj, 1)
            pe.wait_ge(tok_proj_used, 6)

            def scores(u):
                th, b, j = u // 16, u // IB % 2, u % IB
                rows = slice(b * D, (b + 1) * D)
                if u >= 4:
                    pe.wait_ge(decay_ready, u - 3)
                MM(ps[:, u % 4, :], SA[rows, 1, j * P:(j + 1) * P], SA[rows, 0, th * 512:(th + 1) * 512],
                   start=True, stop=True).then_inc(score_ready, 1)

            def kept(u):
                th, b, j = u // 16, u // IB % 2, u % IB
                pe.wait_ge(decay_ready, u + 1)
                MM(ps[b * D:(b + 1) * D, 6 + th, :], VT[:, j, b, :], ring[:, u % 4, :],
                   start=j == 0, stop=j == IB - 1).then_inc(kept_step, 1)

            for u in range(3):
                scores(u)
            for u in range(32):
                if u + 3 < 32:
                    scores(u + 3)
                kept(u)
            for i in range(2):
                pe.wait_ge(kept_copied, i + 1)
                for k in range(4 * i, 4 * i + 4):
                    last = MM(ps[:, i, (k % 4) * P:(k % 4 + 1) * P], T2_flat[:, k * P:(k + 1) * P], w("tok_Wo"), start=True, stop=True)
                last.then_inc(tok_y, 1)

            pe.wait_ge(weights_in[1], 16)
            bank = ps[:, 5, :]
            for o, lhs, rhs in (
                (bank[:, 0:32], lambda t: w("WxT")[:, t * P:(t + 1) * P], lambda t: w("WqBD")[:, t * HR:(t + 1) * HR]),
                (bank[:, 32:64], lambda t: w("WxT")[:, t * P:(t + 1) * P], lambda t: w("WkBD")[:, t * D:t * D + HR]),
                (bank[:, 64:96], lambda t: w("bxrep")[:, t * P:(t + 1) * P], lambda t: w("WqBD")[:, t * HR:(t + 1) * HR]),
                (bank[0:D, 96:97], lambda t: w("WkBD")[:, t * D:(t + 1) * D], lambda t: w("bxcol")[:, t:t + 1]),
            ):
                for t in range(2):
                    MM(o, lhs(t), rhs(t), start=t == 0, stop=t == 1)
            for t in range(2):
                last = MM(bank[:, 128 + t * D:128 + (t + 1) * D], w("WvT"), w("Wo")[:, t * D:(t + 1) * D], start=True, stop=True)
            last.then_inc(merged_ready, 1)
            turn(0, 1, Z)
            pe.wait_ge(merged_used, 7)
            pe.wait_ge(xf_ready, NCH)
            for c in range(NCH):
                last = MM(ps[0:D, c, 0:CH], WK[:, :], XF[:, c * CH:(c + 1) * CH], start=True, stop=True)
            last.then_inc(klog_ready, 1)
            for c in range(NCH):
                for j in range(BC):
                    last = MM(ps[:, 3 + c, j * D:(j + 1) * D], XF[:, (BC * c + j) * P:(BC * c + j + 1) * P], WQ[:, :],
                              start=True, stop=True)
            last.then_inc(qlog_ready, 1)
            pe.wait_ge(knorm_ready, 1)
            for c in range(NCH):
                for j in range(BC):
                    k = BC * c + j
                    last = nc.tensor.transpose(ps[:, c, j * D:(j + 1) * D], NF[0:D, k * P:(k + 1) * P], ident[0:D, 0:D])
            last.then_inc(kturned, 1)
            pe.wait_ge(kt_ready, 1)
            for k in range(KB):
                last = MM(ps[:, 6, 0:D], blk(Z, k), KT[:, k, :], start=k == 0, stop=k == KB - 1)
            last.then_inc(ut_ready, 1)
            pe.wait_ge(uts_ready, 2)
            for b in range(B):
                rows = slice(b * D, (b + 1) * D)
                for t in range(2):
                    last = MM(ps[:, 7 * b, t * HR:(t + 1) * HR], w("WxD", rows)[:, t * P:(t + 1) * P], UTs[rows, :],
                              start=True, stop=True)
            last.then_inc(kx_ready, 1)
            pe.wait_ge(kxs_ready, 4)
            for b in range(B):
                for t in range(2):
                    last = MM(ps[b * HR:(b + 1) * HR, 6, 128:128 + D], KX[:, b, t, :], WVO[:, t, :], start=t == 0, stop=t == 1)
            last.then_inc(m_ready, 1)
            pe.wait_ge(qs_ready, 1)
            turn_narrow(QS, qturned)
            pe.wait_ge(mb_ready, 2)
            for c in range(NCH):
                pe.wait_ge(qf_ready, c + 1)
                for j in range(BC):
                    k = BC * c + j
                    last = MM(ps[:, c, j * P:(j + 1) * P], NF[0:D, k * P:(k + 1) * P], MB[:, :], start=True, stop=True)
            last.then_inc(attn_ready, 1)
            turn(1, 2, Z)
            mlp(0, 1, 2, "a_W1", "a_W2")

            pe.wait_ge(weights_in[2], 16)
            turn(2, 3, X)
            pe.wait_ge(xf_ready, 3 * NCH)
            for b in range(B):
                rows = slice(b * D, (b + 1) * D)
                for c in range(NCH):
                    last = MM(ps[:, WBANK[b][c], 0:CH], w("wr", rows), XF[rows, c * CH:(c + 1) * CH], start=True, stop=True)
                last.then_inc(wrow_ready, 1)
            pe.wait_ge(wrow_copied, 2 * NCH)
            for k in range(KB):
                for b in range(B):
                    q = 2 * k + b
                    last = nc.tensor.transpose(ps[:, 1, q:q + 1], WROW[0:1, b, k * P:(k + 1) * P], ident[0:1, 0:1])
            last.then_inc(wcol_ready, 1)
            pe.wait_ge(wcol_used, 1)
            mlp(1, 2, 2, "f_w1", "f_w2")

            def gates_turn(n):
                pe.wait_ge(gates_ready, n + 1)
                for c in range(NCH):
                    for j in range(BC):
                        last = nc.tensor.transpose(ps[:, 3 + c, j * P:(j + 1) * P], blk(Z, BC * c + j), ident)
                    last.then_inc(gates_turned, 1)
                pe.wait_ge(gates_copied, 2 * NCH * (n + 1))

            def router(t, name):
                pe.wait_ge(xf_ready, NCH * (t + 1))
                for c in range(NCH):
                    for j in range(BC):
                        last = MM(ps[:, 3 + c, j * D:(j + 1) * D], XF[:, (BC * c + j) * P:(BC * c + j + 1) * P], w(name), start=True, stop=True)
                last.then_inc(router_ready, 1)

            def token_product(pairs, done):
                for c in range(NCH):
                    for j in range(BC):
                        at = (BC * c + j) * P
                        for i, (x, m) in enumerate(pairs):
                            last = MM(ps[:, c, j * P:(j + 1) * P], x[:, at:at + P], m, start=i == 0, stop=i == len(pairs) - 1)
                last.then_inc(done, 1)

            pe.wait_ge(weights_in[3], 16)
            turn(3, 4, X)
            for c in range(NCH):
                pe.wait_ge(xf_ready, 3 * NCH + c + 1)
                MM(ps[:, 3 + c, 0:CH], w("WB"), XF[:, c * CH:(c + 1) * CH], start=True, stop=True).then_inc(bu_ready, 1)
            pe.wait_ge(scan_ready, 2)
            token_product([(SA[:, 1, :], w("WC")), (XF[:, :], w("WD"))], y_ready)
            turn(4, 5, X)
            router(4, "rw")
            gates_turn(0)
            pe.wait_ge(selb_ready, 1)
            mlp(2, 4, 4, "m_W1", "m_W2", gate=0, bias="m_b2")
            pe.wait_ge(weights_in[4], 16)
            turn(5, 6, X)
            pe.wait_ge(xf_ready, 6 * NCH)
            for s, name in enumerate(("Bre", "Bim")):
                for c in range(NCH):
                    MM(ps[:, (3 + s * NCH + c) % 8, 0:CH], w(name), XF[:, c * CH:(c + 1) * CH], start=True, stop=True).then_inc(bu_ready, 1)
            pe.wait_ge(scan_ready, 4)
            pe.wait_ge(coef_ready, 4)
            token_product([(SA[:, 0, :], w("Cre")), (SA[:, 1, :], w("Cim"))], y_ready)

            def count(i, s, first=False, final=False):
                pe.wait_ge(onehots_ready, 2 * i + 2)
                for t in range(HG):
                    last_mm = MM(ps[0:NLO, 7, 0:NHI], oh_lo[s][:, :, t], oh_hi[s][:, :, t], start=first and t == 0,
                                 stop=final and t == HG - 1, skip_group_check=True)
                last_mm.then_inc(counted, 1)

            count(0, 0, first=True)
            count(1, 1)
            with pe.Fori(1, EC // HG // 2 - 1) as r:
                for s in range(2):
                    count(2 * r + s, s)
            count(EC // HG - 2, 0)
            count(EC // HG - 1, 1, final=True)
            turn(6, 7, X)
            pe.wait_ge(xf_ready, 7 * NCH)
            for k in range(KB):
                last_mm = MM(ps[:, 3, k * 32:(k + 1) * 32], XF[:, k * P:(k + 1) * P], w("Wgat"), start=True, stop=True)
            last_mm.then_inc(gat_ready, 1)
            pe.wait_ge(table_ready, 1)
            pe.wait_ge(counts_used, 2)
            pe.wait_ge(sums_open, 1)
            MM(ps[:, 7, 0:FEAT * NT], zeros[:, :], table[:, :, :].rearrange("p f t -> p (f t)"), start=True, stop=False, skip_group_check=True)

            def edge_pass(it):
                pe.wait_ge(rest_ready, it + 1)
                nc.tensor.transpose(ps[0:1, 4, CH:CH + P], rest8[:, 1:2], ident).then_inc(rest_turned, 1)
                pe.wait_ge(fields_ready, it * 2 + 2)

                def spread(g, first=False):
                    if not first:
                        pe.wait_ge(oht_ready, (it * GN + g) * 2)
                    for i in range(2):
                        for t in range(GRP):
                            last_mm = MM(ps[:, 5 + i, t * P:(t + 1) * P], lo_b[:, i, bass.ds(GRP * g + t, 1)].broadcast_to([P, P]),
                                         ident_b[:, :], start=True, stop=True)
                    last_mm.then_inc(spread_ready, 1)

                def gather(g, s, first=False):
                    pe.wait_ge(oht_ready, (it * GN + g) * 2 + 2)
                    if not first:
                        pe.wait_ge(selected, (it * GN + g) * 2)
                    for t in range(GRP):
                        MM(ps[:, t, 0:FEAT * NT], oht[s][0][:, t * P:(t + 1) * P], table[:, :, :].rearrange("p f t -> p (f t)"),
                           start=True, stop=True)
                        last_mm = MM(ps[:, 4, t * E2 * NT:(t + 1) * E2 * NT], oht[s][1][:, t * P:(t + 1) * P],
                                     dst_score[:, :, :].rearrange("p f t -> p (f t)"), start=True, stop=True)
                    last_mm.then_inc(gathered, 1)

                spread(0, first=isinstance(it, int))
                spread(1)
                gather(0, 0, first=isinstance(it, int))
                spread(2)
                gather(1, 1)
                with pe.Fori(1, GN // 2 - 1) as r:
                    spread(2 * r + 1)
                    gather(2 * r, 0)
                    spread(2 * r + 2)
                    gather(2 * r + 1, 1)
                spread(GN - 1)
                gather(GN - 2, 0)
                gather(GN - 1, 1)

                def scatter(g, s):
                    pe.wait_ge(outer_ready, (it * GN + g) * 2 + 2)
                    for t in range(GRP):
                        last_mm = MM(ps[:, 7, 0:FEAT * NT], dst_lo_oh[s][:, t, :], outer[s][:, t, :, :].rearrange("p f t -> p (f t)"),
                                     start=False, stop=False, skip_group_check=True)
                    last_mm.then_inc(scattered, 1)

                with pe.Fori(0, GN // 2) as r:
                    for s in range(2):
                        scatter(2 * r + s, s)

            edge_pass(0)
            pe.wait_ge(flag_ready, 1)
            more = pe.value_load(flag[0:1, 0:1], min_val=0, max_val=1)
            with pe.If(more > 0):
                with pe.Fori(1, PASSES) as it:
                    more = pe.value_load(flag[0:1, bass.ds(it - 1, 1)], min_val=0, max_val=1)
                    with pe.If(more > 0):
                        edge_pass(it)
            MM(ps[:, 4, 0:FEAT], ident[:, P - 1:P].broadcast_to([P, P]), table[:, :, NT - 1], start=True, stop=True).then_inc(last_ready, 1)

            def hidden(s):
                c, b = s // 2, s % 2
                rows = slice(b * D, (b + 1) * D)
                for j in range(E2):
                    n = s * E2 + j
                    if n >= 5:
                        pe.wait_ge(g_ready[3], n - 4)
                    MM(ps[:, 3 + n % 5, 0:CH], w("g_W1", rows)[:, j * P:(j + 1) * P], XF[rows, c * CH:(c + 1) * CH],
                       start=True, stop=True).then_inc(hid_ready[3], 1)

            def output(s):
                pe.wait_ge(g_ready[3], (s + 1) * E2)
                for k in range(BC):
                    v = BC * s + k
                    if v >= 3:
                        pe.wait_ge(gated, v - 2)
                    MM(ps[:, v % 3, 0:E2 * D], ident[:, 0:1].broadcast_to([P, P]), w("g_b2"), start=True, stop=False)
                    for j in range(E2):
                        last_mm = MM(ps[:, v % 3, j * D:(j + 1) * D], G[:, s % 2, j, k * P:(k + 1) * P], w("g_W2")[:, j * D:(j + 1) * D],
                                     start=False, stop=j == E2 - 1)
                    last_mm.then_inc(mlp_out[3], 1)

            pe.wait_ge(gate_shift_ready, 1)
            hidden(0)
            for s in range(2 * NCH):
                if s + 1 < 2 * NCH:
                    hidden(s + 1)
                output(s)
            pe.wait_ge(weights_in[5], 16)
            turn(7, 9, X)
            pe.wait_ge(xf_ready, 8 * NCH)
            for s, name in enumerate(("Wq3", "Wk3")):
                for c in range(NCH):
                    MM(ps[:, (3 + s * NCH + c) % 8, 0:CH], w(name), XF[:, c * CH:(c + 1) * CH], start=True, stop=True).then_inc(qk3_ready, 1)
            pe.wait_ge(qk3_used, NCH)
            for c in range(NCH):
                for j in range(BC):
                    at = (BC * c + j) * P
                    last = MM(ps[:, 3 + c, j * P:(j + 1) * P], XF[:, at:at + P], w("Wv3"), start=True, stop=True)
            last.then_inc(v3_ready, 1)
            pe.wait_ge(qk3_used, 2 * NCH)

            def scores3(u):
                i, b, base = u // 2, u % 2, 3 * (u % 2)
                rows = slice(b * D, (b + 1) * D)
                if u == 1:
                    pe.wait_ge(v3_used, NCH)
                if u >= 2:
                    pe.wait_ge(pt3_copied, turned_chunks(u - 1))
                L = (i + 1) * P
                for at in range(0, L, 512):
                    n = min(512, L - at)
                    last = MM(ps[:, base + at // 512, 0:n], SA[rows, 0, i * P:(i + 1) * P], SA[rows, 1, at:at + n], start=True, stop=True)
                last.then_inc(s3_ready, 1)

            def turn_probabilities(u):
                pe.wait_ge(p3_ready, u + 1)
                for cc in range(turned_chunks(u), turned_chunks(u + 1)):
                    c = cc - turned_chunks(u)
                    for j in range(4 * c, min(4 * c + 4, u // 2 + 1)):
                        last = nc.tensor.transpose(ps[:, 3 * (u % 2) + c, (j - 4 * c) * P:(j - 4 * c + 1) * P], PR[:, u % 2, j * P:(j + 1) * P], ident)
                    last.then_inc(pt3_ready, 1)

            def values3(u):
                i, b = u // 2, u % 2
                pe.wait_ge(pt3_copied, turned_chunks(u + 1))
                pe.wait_ge(v3_used, NCH)
                if u >= 2:
                    pe.wait_ge(o3_used, u - 1)
                for j in range(i + 1):
                    last = MM(ps[:, 6 + u % 2, 0:D], PT[:, u % 2, j, :], VT[:, j, b, :], start=j == 0, stop=j == i)
                last.then_inc(o3_ready, 1)

            scores3(0)
            for u in range(Q):
                if u + 1 < Q:
                    scores3(u + 1)
                turn_probabilities(u)
                values3(u)
            turn(8, 10, X)
            router(8, "Wg3")
            gates_turn(1)
            pe.wait_ge(selb_ready, 2)
            mlp(4, 8, 8, "e_W1", "e_W2", gate=4, bias="e_b2")


def host_layout(i):
    pack = np.zeros((P, WIDTH), np.float32)

    def put(name, value, rows=slice(0, P)):
        at, width = COLS[name]
        value = np.asarray(value)
        pack[rows, at:at + width] = value.reshape(value.shape[0], -1) if value.ndim > 1 else value

    def blocks(m):
        r, c = m.shape
        o = np.zeros((B, r, B, c), np.float32)
        for b in range(B):
            o[b, :, b, :] = m
        return o.reshape(B * r, B * c)

    def column(v):
        return np.concatenate([v] * B)[:, None]

    def twice(m):
        return np.concatenate([m] * B, axis=0)

    def tiles(m):
        return m.reshape(-1, P, m.shape[-1]).transpose(1, 0, 2).reshape(P, -1)

    put("ident", np.eye(P, dtype=np.float32))
    for n in "qkvo":
        put(f"tok_W{n}", blocks(i[f"L0_tok_W{n}"]))
    put("tok_bq", column(i["L0_tok_bq"])), put("tok_bk", column(i["L0_tok_bk"]))
    put("tok_bv", i["L0_tok_bv"]), put("tok_bo", i["L0_tok_bo"]), put("prelu", i["L0_tok_prelu_a"].reshape(1))

    Wx, bx = i["L0_attn_Wx"], i["L0_attn_bx"]
    WxT = Wx.T.reshape(2, P, D).transpose(1, 0, 2)
    put("WxT", np.concatenate([WxT, WxT], axis=2))
    heads = np.zeros((2, HEADS, DH, HEADS, KR), np.float32)
    mask = np.zeros((HEADS, DH, HEADS, KR), np.float32)
    for h in range(HEADS):
        heads[0, h, :, h, :] = i["L0_attn_Wq"]
        heads[1, h, :, h, :] = i["L0_attn_Wk"]
        mask[h, :, h, :] = 1.0
    put("WqBD", tiles(heads[0].reshape(256, HR)))
    k2 = heads[1].reshape(256, HR)
    put("WkBD", tiles(np.concatenate([k2, k2], axis=1)))
    put("headmask", tiles(mask.reshape(256, HR)))
    put("bxrep", np.broadcast_to(bx.reshape(2, P).T[:, :, None], (P, 2, P)))
    put("bxcol", bx.reshape(2, P).T)
    put("WxD", twice(Wx))
    wvt = np.zeros((4, DH, 4, DH), np.float32)
    for h in range(4):
        wvt[h, :, h, :] = i["L0_attn_Wv"].T
    put("WvT", wvt.reshape(P, P))
    put("Wo", tiles(i["L0_attn_Wo"]))
    put("a_bo", i["L0_attn_bo"])
    for n in ("ln1_g", "ln1_b", "ln2_g", "ln2_b"):
        put(n, column(i[f"L0_attn_{n}"]))

    def mlp(pre, w1, b1, w2, b2, upper):
        put(f"{pre}{upper[0]}1", twice(w1)), put(f"{pre}b1", b1.reshape(-1, P).T)
        put(f"{pre}{upper[0]}2", tiles(w2)), put(f"{pre}b2", b2)

    mlp("a_", i["L0_attn_W1"], i["L0_attn_b1"], i["L0_attn_W2"], i["L0_attn_b2"], "W")
    put("wr", np.broadcast_to(column(i["L0_ffn_wr"][:, 0]), (P, P)))
    put("br", i["L0_ffn_br"])
    put("tri", np.tril(np.ones((P, P), np.float32), -1))
    mlp("f_", i["L0_ffn_w1"], i["L0_ffn_b1"], i["L0_ffn_w2"], i["L0_ffn_b2"], "w")

    put("WB", blocks(i["L1_attn_W_B"].T)), put("bB", column(i["L1_attn_b_B"])), put("a", column(i["L1_attn_a"]))
    put("WC", blocks(i["L1_attn_W_C"].T)), put("WD", blocks(i["L1_attn_W_D"].T))
    put("bC", i["L1_attn_b_C"]), put("bD", i["L1_attn_b_D"])
    put("rw", blocks(i["L1_ffn_router_w"].T)), put("rb", i["L1_ffn_router_b"])
    put("iota", np.arange(E1, dtype=np.float32))
    put("m_W1", twice(i["L1_ffn_W1"].transpose(1, 0, 2).reshape(D, E1 * H1)))
    put("m_b1", i["L1_ffn_b1"].reshape(4, P).T)
    put("m_W2", tiles(i["L1_ffn_W2"].reshape(E1 * H1, D)))
    b2 = np.zeros((D, D), np.float32)
    b2[:E1] = i["L1_ffn_b2"]
    put("m_b2", blocks(b2))
    sel = np.zeros((D, E1, H1), np.float32)
    for e in range(E1):
        sel[e, e, :] = BIG
    put("sel1", twice(sel.reshape(D, -1)))

    put("Bre", blocks(i["L2_attn_B_re"].T)), put("Bim", blocks(i["L2_attn_B_im"].T))
    put("nu", column(i["L2_attn_nu_log"])), put("theta", column(i["L2_attn_theta_log"]))
    put("Cre", blocks(i["L2_attn_C_re"].T)), put("Cim", blocks(i["L2_attn_C_im"].T))
    put("Dskip", i["L2_attn_D"])
    put("Wgat", blocks(i["L2_ffn_W_gat"]))
    put("att_src", i["L2_ffn_att_src"].reshape(-1)), put("att_dst", i["L2_ffn_att_dst"].reshape(-1))
    put("b_gat", i["L2_ffn_b_gat"]), put("g_gamma", i["L2_ffn_ln_gamma"]), put("g_beta", i["L2_ffn_ln_beta"])
    put("g_W1", twice(i["L2_ffn_W1"].transpose(1, 0, 2).reshape(D, -1)))
    put("g_b1", i["L2_ffn_b1"].T), put("g_W2", i["L2_ffn_W2"].transpose(1, 0, 2))
    put("g_b2", i["L2_ffn_b2"].reshape(-1))
    put("iota128", np.arange(P, dtype=np.float32))

    put("iota_p", np.arange(P, dtype=np.float32)[:, None])

    for n in "qkv":
        put(f"W{n}3", blocks(i[f"L3_attn_W{n}"].T))
    put("bq3", column(i["L3_attn_bq"])), put("bk3", column(i["L3_attn_bk"])), put("bv3", i["L3_attn_bv"])
    put("causal", np.triu(np.full((P, P), -BIG, np.float32), 1))
    gate = np.zeros((D, E1), np.float32)
    gate[:, :E3] = i["L3_ffn_Wg"]
    put("Wg3", blocks(gate)), put("bg3", i["L3_ffn_bg"])
    put("e_W1", twice(i["L3_ffn_W1"].transpose(1, 0, 2).reshape(D, -1)))
    put("e_b1", i["L3_ffn_b1"].T), put("e_W2", i["L3_ffn_W2"].transpose(1, 0, 2))
    b2 = np.zeros((D, D), np.float32)
    b2[:E3] = i["L3_ffn_b2"]
    put("e_b2", blocks(b2))
    sel = np.zeros((D, E3, P), np.float32)
    for e in range(E3):
        sel[e, e, :] = BIG
    put("sel3", twice(sel.reshape(D, -1)))
    return pack


def kernel(**inputs):
    import concourse.bacc as bacc
    from concourse.bass_utils import run_bass_kernel_spmd

    i = {k: np.asarray(v) for k, v in inputs.items()}
    nc = bacc.Bacc("TRN2", target_bir_lowering=False, num_devices=1)
    arrays = {
        "xT": np.ascontiguousarray(i["x"].reshape(B, N_IMG, D).transpose(0, 2, 1).reshape(P, N_IMG)),
        "txt": np.ascontiguousarray(i["txt"]),
        "gammaT": np.ascontiguousarray(i["L0_tok_d_gamma_batched"].T),
        "edges": np.ascontiguousarray(i["L2_ffn_edge_index"].reshape(2, P, EC)),
        "weights": host_layout(i),
    }
    args = [nc.dram_tensor(n, a.shape, mybir.dt.from_np(a.dtype), kind="ExternalInput").ap() for n, a in arrays.items()]
    out = nc.dram_tensor("out", (B, N, D), F32, kind="ExternalOutput").ap()
    build(nc, *args, out)
    result = run_bass_kernel_spmd(nc, [arrays], core_ids=[0])
    return result.results[0]["out"]
```

```python
from contextlib import ExitStack

import numpy as np

import concourse.bass as bass
from concourse import mybir

P = 128
B, D = 2, 64
N_IMG, N_TXT = 1024, 128
N = N_IMG + N_TXT
KB = N // P
IB = N_IMG // P
Q = KB * B
CH = 384
NCH = N // CH
BC = CH // P
HEADS, DH, KR = 8, 32, 4
HR = HEADS * KR
EPS = 1e-5
ROOT_SEED = float(0x5F3759DF)
TOPK = int(0.5 * N) - 1
DT = 1.0 / N
E1, H1 = 32, 16
E2 = 4
E3 = 8
NODES = B * N
NT = NODES // P
FEAT = 20
EDGES = 262144
EC = EDGES // P
SCALE = float(D) ** -0.5
TWO_PI = 2.0 * float(np.pi)
TWO_PI_HI = 6.28125
TWO_PI_LO = TWO_PI - TWO_PI_HI
BIG = 1e30
HG = 24
NHI, NLO = 36, 64
SEG, SEG_TOP = 128, 24
CAND = EC // SEG * SEG_TOP
SLOTS = 64
PASSES = EC // SLOTS
PASS_STEPS = 17
GRP = 2

ALU = mybir.AluOpType
ACT = mybir.ActivationFunctionType
AX = mybir.AxisListType
F32 = mybir.dt.float32
BF16 = mybir.dt.bfloat16
I32 = mybir.dt.int32

GROUPS = [
    [("ident", P), ("tok_Wq", P), ("tok_Wk", P), ("tok_Wv", P), ("tok_Wo", P), ("tok_bq", 1), ("tok_bk", 1),
     ("tok_bv", D), ("tok_bo", D), ("prelu", 1)],
    [("WxT", 2 * P), ("WqBD", 2 * HR), ("WkBD", 4 * HR), ("bxrep", 2 * P), ("bxcol", 2), ("WxD", 2 * P),
     ("headmask", 2 * HR), ("WvT", P), ("Wo", 2 * D), ("a_bo", D), ("ln1_g", 1), ("ln1_b", 1), ("ln2_g", 1),
     ("ln2_b", 1), ("a_W1", 2 * P), ("a_b1", 2), ("a_W2", 2 * D), ("a_b2", D)],
    [("wr", P), ("br", 1), ("tri", P), ("f_w1", 2 * P), ("f_b1", 2), ("f_w2", 2 * D), ("f_b2", D)],
    [("WB", P), ("bB", 1), ("a", 1), ("WC", P), ("WD", P), ("bC", D), ("bD", D),
     ("rw", D), ("rb", E1), ("iota", E1), ("m_W1", B * 4 * P), ("m_b1", 4), ("m_W2", 4 * D), ("m_b2", P)],
    [("Bre", P), ("Bim", P), ("nu", 1), ("theta", 1), ("Cre", P), ("Cim", P), ("Dskip", D),
     ("Wgat", 32), ("att_src", 16), ("att_dst", 16), ("b_gat", 16), ("g_gamma", 16), ("g_beta", 16),
     ("g_W1", 4 * P), ("g_b1", 4), ("g_W2", 4 * D), ("g_b2", 4 * D), ("iota128", P), ("iota_p", 1)],
    [("Wq3", P), ("Wk3", P), ("Wv3", P), ("bq3", 1), ("bk3", 1), ("bv3", D), ("causal", P),
     ("Wg3", D), ("bg3", E3), ("e_W1", B * 8 * P), ("e_b1", 8), ("e_W2", 8 * D), ("e_b2", P)],
]
COLS, _at = {}, 0
GROUP_COLS = []
for _g in GROUPS:
    _from = _at
    for _name, _width in _g:
        COLS[_name] = (_at, _width)
        _at += _width
    GROUP_COLS.append((_from, _at))
WIDTH = _at


def build(nc, xT, txt, gammaT, edges, weights, out):
    ctx = ExitStack()
    with ctx:
        def sb(name, shape, dt=F32):
            return ctx.enter_context(nc.sbuf_tensor(name, shape, dt))

        def sem(name):
            return ctx.enter_context(nc.semaphore(name))

        ps = ctx.enter_context(nc.psum_tensor("ps", [P, 8, 512], F32))
        W_all = sb("weights_sb", [P, WIDTH])
        H = sb("H", [P, KB, B, D])
        X = sb("X", [P, KB, B, D])
        Z = sb("Z", [P, KB, B, D])
        XC = sb("XC", [P, KB, B, D])
        T1 = sb("T1", [P, KB, B, D])
        T2 = sb("T2", [P, KB, B, D])
        XF = sb("XF", [P, N])
        SA = sb("SA", [P, 2, N])
        VT = sb("VT", [P, KB, B, D])
        G = sb("G", [P, 2, E3, CH])
        gam = sb("gam", [P, IB, N_IMG])
        ring = sb("ring", [P, 4, 512])
        st = sb("st", [P, 16, Q])
        small = sb("small", [P, 64])
        KT = sb("KT", [P, KB, D])
        QS = sb("QS", [P, KB, D])
        LG = sb("LG", [P, KB, D])
        NF = sb("NF", [P, N])
        WQ = sb("WQ", [P, D])
        WK = sb("WK", [P, D])
        BQ = sb("BQ", [P, HR])
        BK = sb("BK", [D, 1])
        WVO = sb("WVO", [P, 2, D])
        UTs = sb("UTs", [P, HR])
        KX = sb("KX", [P, B, 2, HR])
        MB = sb("MB", [D, P])
        powers = sb("powers", [P, 8, 4])
        coef = sb("coef", [P, 8])
        lam = sb("lam", [P, 12])
        lam_i = sb("lam_i", [P, 1], I32)
        bcd = sb("bcd", [P, D])
        iota64 = sb("iota64", [P, E1])
        PR = sb("PR", [P, 2, N])
        PT = sb("PT", [P, 2, KB, P])
        den3 = sb("den3", [P, 4, Q])
        held = sb("held", [1, 128])
        root_i = sb("root_i", [P, Q], I32)

        def w(name, rows=slice(0, P)):
            at, width = COLS[name]
            return W_all[rows, at:at + width]

        T2_flat = T2[:, :, :, :].rearrange("p k b d -> p (k b d)")
        junk = ring[:, :, :].rearrange("p a b -> p (a b)")
        WROW = SA
        WBANK = ((3, 4, 5), (6, 7, 0))

        def flat(t):
            return t[:, :, :, :].rearrange("p k b d -> p (k b) d")

        def blk(t, k):
            return t[:, k, :, :].rearrange("p b d -> p (b d)")

        weights_in = [sem(f"weights_in_{i}") for i in range(len(GROUPS))]
        x_in, txt_in, out_stored = sem("x_in"), sem("txt_in"), sem("out_stored")
        gamma_in = [sem(f"gamma_in_{th}") for th in range(2)]
        dve_step, act_step = sem("dve_step"), sem("act_step")

        norm_ready = sem("norm_ready")
        turned, xf_ready = sem("turned"), sem("xf_ready")
        h_ready = sem("h_ready")

        def hold(engine, semaphore, value, alone=False):
            engine.wait_ge(semaphore, value)
            if alone:
                nc.vector.memset(held[:, sites[0]:sites[0] + 1], 0.0)
                sites[0] += 1

        sites = [0]

        class Chain:

            def __init__(self, engine, semaphore):
                self.engine, self.semaphore, self.count = engine, semaphore, 0

            def __call__(self, instruction):
                self.count += 1
                instruction.then_inc(self.semaphore, 1)
                self.engine.wait_ge(self.semaphore, self.count)

        t13 = T1[:, :, :, :].rearrange("p (c j) b d -> p c (j b) d", c=NCH)

        words = gam[:, :, :].rearrange("p j t -> p (j t)")
        SAw = SA[:, :, :].rearrange("p a n -> p (a n)")
        PRw = PR[:, :, :].rearrange("p a n -> p (a n)")
        PTw = PT[:, :, :, :].rearrange("p a j n -> p (a j n)")
        Gw = G[:, :, :, :].rearrange("p a j n -> p (a j n)")
        e_src, e_dst = (words[:, i * EC:(i + 1) * EC].bitcast(I32) for i in range(2))
        e_key = words[:, 2 * EC:3 * EC]
        e_last = words[:, 3 * EC:4 * EC]
        e_flag = PRw[:, 0:EC]
        cand = PTw[:, 0:CAND]
        picked = words[:, 3 * EC:4 * EC]
        cand_i, cand_j = picked[:, 0:CAND].bitcast(I32), picked[:, CAND:2 * CAND].bitcast(I32)
        digit_hi = picked[:, 2 * CAND:2 * CAND + CAND // 2].bitcast(BF16)
        digit_lo = picked[:, 2 * CAND + CAND // 2:3 * CAND].bitcast(BF16)
        half = HG * (NHI + NLO) // 2
        homes = [words[:, 0:half], words[:, half:2 * half]]
        oh_hi = [h[:, 0:HG * NHI // 2].bitcast(BF16).rearrange("p (v t) -> p v t", t=HG) for h in homes]
        oh_lo = [h[:, HG * NHI // 2:half].bitcast(BF16).rearrange("p (v t) -> p v t", t=HG) for h in homes]
        digit_values = sb("digit_values", [P, NLO, HG], BF16)
        zeros = sb("zeros", [P, P])
        ident_b = sb("ident_b", [P, P], BF16)
        key = sb("key", [P, SLOTS])
        key_i = sb("key_i", [P, SLOTS], I32)
        field = sb("field", [P, 4, SLOTS], I32)
        lo_b = sb("lo_b", [P, 2, SLOTS], BF16)
        rest8 = sb("rest8", [P, 8])
        flag = sb("flag", [1, PASSES], I32)
        table = sb("table", [P, FEAT + E2, NT])
        parts = sb("parts", [P, 3, FEAT, NT], BF16)
        dst_score = table[:, FEAT:FEAT + E2, :]
        local_max = sb("local_max", [P, E2])
        score_max = sb("score_max", [P, E2])
        last_node = sb("last_node", [P, FEAT])
        n_last = sb("n_last", [P, NT])
        gate4 = sb("gate4", [P, Q, E2])
        pick4 = sb("pick4", [P, 3, Q, E2])
        e_val = SAw[:, 0:SLOTS * FEAT].rearrange("p (s f) -> p s f", f=FEAT)
        e_tmp = SAw[:, SLOTS * FEAT:SLOTS * (FEAT + 2 * E2)].rearrange("p (a s f) -> p a s f", a=2, f=E2)
        e_w = PRw[:, 0:SLOTS * FEAT].rearrange("p (s f) -> p s f", f=FEAT)
        node_w = PRw[:, SLOTS * FEAT:SLOTS * FEAT + 6 * E2 * NT].rearrange("p (a b h t) -> p a b h t", a=3, b=2, t=NT)
        src_hi_oh = PTw[:, 0:SLOTS * NT].rearrange("p (s t) -> p s t", t=NT)
        dst_hi_oh = PTw[:, SLOTS * NT:2 * SLOTS * NT].rearrange("p (s t) -> p s t", t=NT)
        GF = GRP * FEAT * NT
        product = [Gw[:, s * GF:(s + 1) * GF].rearrange("p (g f t) -> p g f t", g=GRP, t=NT) for s in range(2)]
        outer = [Gw[:, (2 + s) * GF:(3 + s) * GF].rearrange("p (g f t) -> p g f t", g=GRP, t=NT) for s in range(2)]
        dst_lo_oh = [Gw[:, 4 * GF + s * GRP * P:4 * GF + (s + 1) * GRP * P].rearrange("p (g n) -> p g n", g=GRP) for s in range(2)]
        distance = [ring[:, s, GRP * P:2 * GRP * P].bitcast(BF16) for s in range(2)]
        turned_oh = [ring[:, s, 0:GRP * P].bitcast(BF16) for s in range(2)]
        GN = SLOTS // GRP

        def turned_chunks(u):
            return sum((v // 2 + 4) // 4 for v in range(u))

        block = ctx.enter_context(nc.Block())

        (tok_proj, tok_proj_used, score_ready, decay_ready, kept_step, kept_copied, tok_y) = (
            sem("tok_proj"), sem("tok_proj_used"), sem("score_ready"), sem("decay_ready"), sem("kept_step"),
            sem("kept_copied"), sem("tok_y"))
        merged_ready, merged_used = sem("merged_ready"), sem("merged_used")
        (klog_ready, kshift_ready, kexp_ready, knorm_ready, kturned, kt_ready, ut_ready, uts_ready, kx_ready,
         kxs_ready, m_ready, mb_ready) = (sem(n) for n in (
            "klog_ready", "kshift_ready", "kexp_ready", "knorm_ready", "kturned", "kt_ready", "ut_ready", "uts_ready",
            "kx_ready", "kxs_ready", "m_ready", "mb_ready"))
        qlog_ready, qshift_ready, qexp_ready, qs_ready, qturned, qf_ready, attn_ready = (sem(n) for n in (
            "qlog_ready", "qshift_ready", "qexp_ready", "qs_ready", "qturned", "qf_ready", "attn_ready"))
        wrow_ready, wrow_copied, wcol_ready, wcol_used = (sem(n) for n in ("wrow_ready", "wrow_copied", "wcol_ready", "wcol_used"))
        hid_ready = [sem(f"hid_ready_{m}") for m in range(5)]
        g_ready = [sem(f"g_ready_{m}") for m in range(5)]
        mlp_out = [sem(f"mlp_out_{m}") for m in range(5)]

        bu_ready, force_ready, scan_ready, y_ready, cd_ready, silu_ready = (sem(n) for n in (
            "bu_ready", "force_ready", "scan_ready", "y_ready", "cd_ready", "silu_ready"))
        coef_ready, lambda_ready = sem("coef_ready"), sem("lambda_ready")
        router_ready, gates_ready, gates_turned, gates_copied = (sem(n) for n in (
            "router_ready", "gates_ready", "gates_turned", "gates_copied"))
        qk3_ready, qk3_used, v3_ready, v3_used, s3_ready, shift3_ready, p3_ready, pt3_ready, pt3_copied, o3_ready, o3_used = (
            sem(n) for n in ("qk3_ready", "qk3_used", "v3_ready", "v3_used", "s3_ready", "shift3_ready", "p3_ready",
                             "pt3_ready", "pt3_copied", "o3_ready", "o3_used"))

        edges_in, digits_ready, onehots_ready, counted, counts_used = (sem(n) for n in (
            "edges_in", "digits_ready", "onehots_ready", "counted", "counts_used"))
        gat_ready, table_ready, local_max_ready, score_max_ready, last_ready = (sem(n) for n in (
            "gat_ready", "table_ready", "local_max_ready", "score_max_ready", "last_ready"))
        (taken, fields_ready, rest_ready, rest_turned, flag_ready, spread_ready, low_read, oht_ready, gathered, product_step,
         selected, edge_shift_ready, edge_exp_ready, zeros_ready, parts_ready, outer_ready, terms_ready, pool_outer, scattered, edge_step) = (sem(n) for n in (
            "taken", "fields_ready", "rest_ready", "rest_turned", "flag_ready", "spread_ready", "low_read", "oht_ready", "gathered",
            "product_step", "selected", "edge_shift_ready", "edge_exp_ready", "zeros_ready", "parts_ready", "outer_ready", "terms_ready", "pool_outer", "scattered", "edge_step"))
        node_shift_ready, node_exp_ready, gate_shift_ready, gate_exp_ready, gated = (sem(n) for n in (
            "node_shift_ready", "node_exp_ready", "gate_shift_ready", "gate_exp_ready", "gated"))
        cd_step = sem("cd_step")
        @block.sync
        def _(sp):
            sp.dma_start(W_all[:, slice(*GROUP_COLS[0])], weights[:, slice(*GROUP_COLS[0])]).then_inc(weights_in[0], 16)
            sp.dma_start(XF[:, 0:N_IMG], xT).then_inc(x_in, 16)
            gview = gammaT.rearrange("(j p) t -> p j t", p=P)
            for th in range(2):
                sp.dma_start(gam[:, :, th * 512:(th + 1) * 512], gview[:, :, th * 512:(th + 1) * 512]).then_inc(gamma_in[th], 16)
            sp.dma_start(H[:, IB, :, :], txt.rearrange("b p d -> p b d")).then_inc(txt_in, 16)
            for i in range(1, len(GROUPS)):
                sp.dma_start(W_all[:, slice(*GROUP_COLS[i])], weights[:, slice(*GROUP_COLS[i])]).then_inc(weights_in[i], 16)
            sp.wait_ge(decay_ready, 32)
            for i, dst in enumerate((e_src, e_dst)):
                sp.dma_start(dst, edges[i]).then_inc(edges_in, 16)
            sp.wait_ge(h_ready, 1)
            for b in range(B):
                sp.dma_start(out[b].rearrange("(k p) d -> p k d", p=P), H[:, :, b, :]).then_inc(out_stored, 16)
            sp.wait_ge(out_stored, 16 * B)

        @block.gpsimd
        def _(pool):
            nc.gpsimd.memset(zeros[:, :], 0.0).then_inc(zeros_ready, 1)
            pool.wait_ge(local_max_ready, 1)
            nc.gpsimd.partition_all_reduce(score_max[:, :], local_max[:, :], P, bass.bass_isa.ReduceOp.max).then_inc(score_max_ready, 1)
            pool.wait_ge(terms_ready, 1)

            def spread_out(g, first=False):
                if not first:
                    pool.wait_ge(scattered, g + (-1))
                at = bass.ts(g, GRP)
                nc.gpsimd.tensor_tensor(outer[0], e_w[:, at, :].unsqueeze(3).broadcast_to([P, GRP, FEAT, NT]),
                                        dst_hi_oh[:, at, :].unsqueeze(2).broadcast_to([P, GRP, FEAT, NT]), ALU.mult).then_inc(pool_outer, 1)

            spread_out(0, first=True)
            with pool.Fori(1, GN // 2) as r:
                spread_out(2 * r)

        @block.scalar
        def _(act):
            step = Chain(act, act_step)

            def input_to_channels(t, scale=None, bias=None):
                for c in range(NCH):
                    act.wait_ge(turned, NCH * t + c + 1)
                    dst, src = XF[:, c * CH:(c + 1) * CH], ps[:, c, 0:CH]
                    if scale is None:
                        nc.scalar.activation(dst, src, ACT.Copy).then_inc(xf_ready, 1)
                    else:
                        nc.scalar.activation(dst, src, ACT.Identity, bias=bias, scale=scale).then_inc(xf_ready, 1)

            def mlp(m, J, func, bias):
                for s in range(2 * NCH):
                    for j in range(J):
                        n = s * J + j
                        act.wait_ge(hid_ready[m], n + 1)
                        if s >= 2 and j == 0:
                            act.wait_ge(mlp_out[m], (s - 1) * (BC if m == 3 else 1))
                        nc.scalar.activation(G[:, s % 2, j, :], ps[:, 3 + n % 5, 0:CH], func,
                                             bias=bias[:, j:j + 1]).then_inc(g_ready[m], 1)

            act.wait_ge(weights_in[0], 16)
            act.wait_ge(tok_proj, 1)
            for i, (name, dst) in enumerate((("tok_bq", SA[:, 0, :]), ("tok_bk", SA[:, 1, :]))):
                for th in range(2):
                    nc.scalar.activation(dst[:, th * 512:(th + 1) * 512], ps[:, 2 * i + th, :], ACT.Identity,
                                         bias=w(name), scale=1.0).then_inc(tok_proj_used, 1)
            for th in range(2):
                act.wait_ge(kept_step, 16 * (th + 1))
                nc.scalar.activation(T2_flat[:, th * 512:(th + 1) * 512], ps[:, 6 + th, :], ACT.Copy).then_inc(kept_copied, 1)

            act.wait_ge(weights_in[1], 16)
            input_to_channels(0, w("ln1_g"), w("ln1_b"))
            act.wait_ge(kshift_ready, 1)
            nc.scalar.activation(NF[0:D, :].rearrange("p (c n) -> p c n", c=NCH), ps[0:D, 0:NCH, 0:CH], ACT.Exp,
                                 bias=small[0:D, 4:5], accum_out=small[0:D, 5:6]).then_inc(kexp_ready, 1)
            act.wait_ge(qshift_ready, 1)
            nc.scalar.activation(QS[:, :, :], LG[:, :, :], ACT.Exp).then_inc(qexp_ready, 1)
            for c in range(NCH):
                act.wait_ge(qturned, c + 1)
                nc.scalar.activation(NF[0:D, c * CH:(c + 1) * CH], ps[0:D, 3 + c, 0:CH], ACT.Copy).then_inc(qf_ready, 1)
            input_to_channels(1, w("ln2_g"), w("ln2_b"))
            mlp(0, 2, ACT.Gelu, w("a_b1"))

            act.wait_ge(weights_in[2], 16)
            input_to_channels(2)
            for b in range(B):
                act.wait_ge(wrow_ready, b + 1)
                for c in range(NCH):
                    nc.scalar.activation(WROW[:, b, c * CH:(c + 1) * CH], ps[:, WBANK[b][c], 0:CH], ACT.Identity,
                                         bias=w("br"), scale=1.0).then_inc(wrow_copied, 1)
            mlp(1, 2, ACT.Gelu_apprx_tanh, w("f_b1"))

            def input_beside_gates():
                for c in range(NCH):
                    nc.scalar.activation(NF[D:P, c * CH:(c + 1) * CH], ps[D:P, c, 0:CH], ACT.Copy).then_inc(gates_copied, 1)

            def gates_to_channels():
                for c in range(NCH):
                    act.wait_ge(gates_turned, gates[0] * NCH + c + 1)
                    for x, rows in ((XF, slice(D, P)), (NF, slice(0, D))):
                        nc.scalar.activation(x[rows, c * CH:(c + 1) * CH], ps[rows, 3 + c, 0:CH], ACT.Copy).then_inc(gates_copied, 1)
                gates[0] += 1

            gates = [0]
            input_to_channels(3)
            act.wait_ge(coef_ready, 1)
            for c in range(NCH):
                act.wait_ge(bu_ready, c + 1)
                for s in range(2):
                    nc.scalar.activation(SA[:, s, c * CH:(c + 1) * CH], ps[:, 3 + c, 0:CH], ACT.Identity,
                                         bias=coef[:, 4 + s:5 + s], scale=coef[:, 2 + s:3 + s]).then_inc(force_ready, 1)
            act.wait_ge(cd_ready, 1)
            step(nc.scalar.activation(flat(Z), flat(T1), ACT.Gelu))
            nc.scalar.activation(flat(T2), flat(Z), ACT.Sigmoid).then_inc(silu_ready, 1)
            input_to_channels(4)
            input_beside_gates()
            gates_to_channels()
            mlp(2, 4, ACT.Relu, w("m_b1"))
            act.wait_ge(weights_in[4], 16)
            step(nc.scalar.activation(lam[:, 0:1], w("nu"), ACT.Exp))
            step(nc.scalar.activation(lam[:, 1:2], lam[:, 0:1], ACT.Exp, scale=-1.0))
            nc.scalar.activation(lam[:, 2:3], w("theta"), ACT.Exp).then_inc(lambda_ready, 1)
            act.wait_ge(coef_ready, 2)
            nc.scalar.activation(lam[:, 5:6], lam[:, 3:4], ACT.Sin).then_inc(lambda_ready, 1)
            nc.scalar.activation(lam[:, 6:7], lam[:, 4:5], ACT.Sin).then_inc(lambda_ready, 1)
            act.wait_ge(coef_ready, 3)
            step(nc.scalar.activation(lam[:, 8:9], lam[:, 7:8], ACT.Sqrt))
            input_to_channels(5)
            for s in range(2):
                for c in range(NCH):
                    act.wait_ge(bu_ready, NCH + s * NCH + c + 1)
                    nc.scalar.activation(SA[:, s, c * CH:(c + 1) * CH], ps[:, (3 + s * NCH + c) % 8, 0:CH], ACT.Copy,
                                         scale=lam[:, 8:9]).then_inc(force_ready, 1)

            input_to_channels(6)

            def edge_pass(it):
                def turned_onehots(g, s, first=False):
                    act.wait_ge(spread_ready, it * GN + g + 1)
                    nc.scalar.activation(distance[s], ps[:, 5 + s, :], ACT.Abs, bias=w("iota_p"), scale=-1.0).then_inc(low_read, 1)
                    act.wait_ge(low_read, it * GN + g + 1)
                    if not first:
                        act.wait_ge(gathered, it * GN + g - 1)
                    nc.scalar.activation(turned_oh[s], distance[s], ACT.Relu, bias=1.0, scale=-1.0).then_inc(oht_ready, 1)

                for s in range(2):
                    turned_onehots(s, s, first=isinstance(it, int))
                with act.Fori(1, GN // 2) as r:
                    for s in range(2):
                        turned_onehots(2 * r + s, s)
                act.wait_ge(edge_shift_ready, it + 1)
                nc.scalar.activation(e_w[:, :, 0:E2], e_tmp[:, 0, :, :], ACT.Exp).then_inc(edge_exp_ready, 1)

            edge_pass(0)
            act.wait_ge(flag_ready, 1)
            more = act.value_load(flag[0:1, 0:1], min_val=0, max_val=1)
            with act.If(more > 0):
                with act.Fori(1, PASSES) as it:
                    more = act.value_load(flag[0:1, bass.ds(it - 1, 1)], min_val=0, max_val=1)
                    with act.If(more > 0):
                        edge_pass(it)
            act.wait_ge(node_shift_ready, 1)
            nc.scalar.activation(node_w[:, 0, :, :, :], node_w[:, 1, :, :, :], ACT.Exp).then_inc(node_exp_ready, 1)
            act.wait_ge(gate_shift_ready, 1)
            nc.scalar.activation(st[:, 12, :], st[:, 13, :], ACT.Exp).then_inc(gate_exp_ready, 1)
            mlp(3, 4, ACT.Gelu, w("g_b1"))
            act.wait_ge(weights_in[5], 16)
            input_to_channels(7)
            for s, name in enumerate(("bq3", "bk3")):
                for c in range(NCH):
                    act.wait_ge(qk3_ready, s * NCH + c + 1)
                    nc.scalar.activation(SA[:, s, c * CH:(c + 1) * CH], ps[:, (3 + s * NCH + c) % 8, 0:CH], ACT.Identity,
                                         bias=w(name), scale=1.0).then_inc(qk3_used, 1)

            def expo(u):
                L = (u // 2 + 1) * P
                act.wait_ge(shift3_ready, u + 1)
                if u >= 2:
                    act.wait_ge(pt3_ready, turned_chunks(u - 1))
                nc.scalar.activation(PR[:, u % 2, 0:L], ps[:, 3 * (u % 2):3 * (u % 2) + 3, :].rearrange("p c n -> p (c n)")[:, 0:L],
                                     ACT.Exp, bias=den3[:, 1, u:u + 1], scale=SCALE, accum_out=den3[:, 2, u:u + 1]).then_inc(p3_ready, 1)

            def copies(u):
                if u >= 2:
                    act.wait_ge(o3_ready, u - 1)
                for cc in range(turned_chunks(u), turned_chunks(u + 1)):
                    act.wait_ge(pt3_ready, cc + 1)
                    c = cc - turned_chunks(u)
                    j, m = 4 * c, min(4, u // 2 + 1 - 4 * c)
                    nc.scalar.activation(PT[:, u % 2, j:j + m, :], ps[:, 3 * (u % 2) + c, 0:m * P].rearrange("p (j n) -> p j n", n=P),
                                         ACT.Copy).then_inc(pt3_copied, 1)

            expo(0)
            for u in range(Q):
                copies(u)
                if u + 1 < Q:
                    expo(u + 1)
            input_to_channels(8)
            input_beside_gates()
            gates_to_channels()
            mlp(4, 8, ACT.Gelu, w("e_b1"))

        @block.vector
        def _(dve):
            link = Chain(dve, dve_step)
            V = nc.vector

            def bc(ap, n):
                return ap.unsqueeze(ap.ndim).broadcast_to(list(ap.shape) + [n])

            def row(ap, n=Q):
                return ap.unsqueeze(1).broadcast_to([ap.shape[0], n, ap.shape[1]])

            def layernorm(src, dst, n, width=D, centred=None, squares=None):
                centred = flat(XC) if centred is None else centred
                squares = flat(T1) if squares is None else squares
                link(V.reduce_sum(st[:, 0, :], src, AX.X))
                link(V.tensor_scalar(st[:, 1, :], st[:, 0, :], 1.0 / width, None, ALU.mult))
                link(V.tensor_tensor(centred, src, bc(st[:, 1, :], width), ALU.subtract))
                link(V.tensor_tensor(squares, centred, centred, ALU.mult))
                link(V.reduce_sum(st[:, 4, :], squares, AX.X))
                link(V.tensor_scalar(st[:, 2, :], st[:, 4, :], 1.0 / width, EPS, ALU.mult, ALU.add))
                link(V.tensor_scalar(st[:, 1, :], st[:, 2, :], -0.5, None, ALU.mult))
                link(V.tensor_scalar(root_i[:, :], st[:, 2, :].bitcast(I32), 1, None, ALU.logical_shift_right))
                link(V.tensor_scalar(st[:, 3, :].bitcast(I32), root_i[:, :], -1.0, ROOT_SEED, ALU.mult, ALU.add))
                for _ in range(3):
                    link(V.tensor_tensor(st[:, 0, :], st[:, 3, :], st[:, 3, :], ALU.mult))
                    link(V.tensor_tensor(st[:, 0, :], st[:, 0, :], st[:, 1, :], ALU.mult))
                    link(V.scalar_tensor_tensor(st[:, 3, :], st[:, 0, :], 1.5, st[:, 3, :], ALU.add, ALU.mult))
                V.tensor_tensor(dst, centred, bc(st[:, 3, :], width), ALU.mult).then_inc(norm_ready, 1)
                dve.wait_ge(norm_ready, n + 1)

            def three(t):
                return t[:, :, :, :].rearrange("p (c j) b d -> p c (j b d)", c=NCH)

            def out_psum():
                return ps[:, 0:NCH, 0:CH]

            def edge_keys():
                dve.wait_ge(edges_in, 32)
                final = float(NODES - 1)
                link(V.tensor_scalar(e_flag, e_src, final, None, ALU.is_ge))
                link(V.scalar_tensor_tensor(e_flag, e_dst, float(NODES), e_flag, ALU.is_lt, ALU.mult))
                link(V.tensor_scalar(e_last, e_dst, 4096.0, final + 1.0, ALU.mult, ALU.add))
                link(V.tensor_tensor(e_last, e_last, e_flag, ALU.mult))
                for j in range(SEG_TOP // 8):
                    for k in range(EC // SEG):
                        V.max(cand[:, k * SEG_TOP + 8 * j:k * SEG_TOP + 8 * j + 8], e_last[:, k * SEG:(k + 1) * SEG]).then_inc(dve_step, 1)
                    link.count += EC // SEG
                    for k in range(EC // SEG):
                        dve.wait_ge(dve_step, link.count - EC // SEG + k + 1)
                        V.match_replace(e_last[:, k * SEG:(k + 1) * SEG], cand[:, k * SEG_TOP + 8 * j:k * SEG_TOP + 8 * j + 8],
                                        e_last[:, k * SEG:(k + 1) * SEG], 0.0).then_inc(dve_step, 1)
                    link.count += EC // SEG
                    dve.wait_ge(dve_step, link.count)

            def edge_digits():
                final = float(NODES - 1)
                link(V.tensor_scalar(e_flag, e_src, final, None, ALU.is_lt))
                link(V.scalar_tensor_tensor(e_flag, e_dst, float(NODES), e_flag, ALU.is_lt, ALU.mult))
                link(V.scalar_tensor_tensor(e_key, e_dst, 4096.0, e_src, ALU.mult, ALU.add))
                link(V.scalar_tensor_tensor(e_key, e_key, 1.0, e_flag, ALU.add, ALU.mult))
                link(V.tensor_tensor(e_key, e_key, e_last, ALU.add))
                link(V.tensor_scalar(cand_i, cand, -1.0, None, ALU.add))
                link(V.tensor_scalar(cand_j, cand_i, 12, NLO - 1, ALU.logical_shift_right, ALU.bitwise_and))
                link(V.tensor_scalar(cand_i, cand_i, 18, None, ALU.arith_shift_right))
                link(V.tensor_copy(digit_hi, cand_i))
                link(V.tensor_copy(digit_lo, cand_j))
                dve.wait_ge(weights_in[4], 16)
                link(V.tensor_copy(ident_b[:, :], w("ident")))
                link(V.tensor_copy(digit_values[:, :, :], bc(w("iota128")[:, 0:NLO], HG)))

            steps = [0]

            def linked(it, instruction):
                steps[0] += 1
                instruction.then_inc(edge_step, 1)
                hold(dve, edge_step, it * PASS_STEPS + steps[0], not isinstance(it, int))

            def take_edges(it):
                reg = not isinstance(it, int)
                for j in range(SLOTS // 8):
                    V.max(key[:, 8 * j:8 * j + 8], e_key).then_inc(taken, 1)
                    hold(dve, taken, it * (2 * (SLOTS // 8)) + (2 * j + 1), reg)
                    V.match_replace(e_key, key[:, 8 * j:8 * j + 8], e_key, 0.0).then_inc(taken, 1)
                    hold(dve, taken, it * (2 * (SLOTS // 8)) + (2 * j + 2), reg)
                steps[0] = 0
                linked(it, V.max(rest8[:, :], e_key))
                V.tensor_copy(rest8[:, 1:2], rest8[:, 0:1]).then_inc(rest_ready, 1)
                linked(it, V.tensor_scalar(key_i[:, :], key[:, :], -1.0, None, ALU.add))
                linked(it, V.tensor_scalar(field[:, 0, :], key_i[:, :], P - 1, None, ALU.bitwise_and))
                linked(it, V.tensor_scalar(field[:, 1, :], key_i[:, :], 7, 31, ALU.logical_shift_right, ALU.bitwise_and))
                linked(it, V.tensor_scalar(field[:, 2, :], key_i[:, :], 12, P - 1, ALU.logical_shift_right, ALU.bitwise_and))
                linked(it, V.tensor_scalar(field[:, 3, :], key_i[:, :], 19, None, ALU.arith_shift_right))
                for i in range(2):
                    V.tensor_copy(lo_b[:, i, :], field[:, 2 * i, :]).then_inc(fields_ready, 1)
                linked(it, V.tensor_tensor(src_hi_oh, bc(field[:, 1, :], NT), row(w("iota128")[:, 0:NT], SLOTS), ALU.is_equal))
                linked(it, V.tensor_tensor(dst_hi_oh, bc(field[:, 3, :], NT), row(w("iota128")[:, 0:NT], SLOTS), ALU.is_equal))

            dve.wait_ge(weights_in[0], 16)
            dve.wait_ge(tok_proj, 2)
            for i in range(2):
                V.tensor_tensor(VT[:, 4 * i:4 * i + 4, :, :].rearrange("p k b d -> p (k b) d"),
                                ps[:, 4 + i, :].rearrange("p (q d) -> p q d", d=D), row(w("tok_bv"), 8),
                                ALU.add).then_inc(tok_proj_used, 1)
            for th in range(2):
                dve.wait_ge(gamma_in[th], 16)
                for u in range(16 * th, 16 * th + 16):
                    dve.wait_ge(score_ready, u + 1)
                    if u >= 4:
                        dve.wait_ge(kept_step, u - 3)
                    V.tensor_tensor(ring[:, u % 4, :], ps[:, u % 4, :],
                                    gam[:, u % IB, th * 512:(th + 1) * 512], ALU.mult).then_inc(decay_ready, 1)
            for i in range(2):
                dve.wait_ge(tok_y, i + 1)
                y = flat(T1)[:, 0:8, :]
                link(V.tensor_tensor(y, ps[:, i, :].rearrange("p (q d) -> p q d", d=D), row(w("tok_bo"), 8), ALU.add))
                neg = flat(XC)[:, 0:8, :]
                link(V.tensor_scalar(neg, y, 0.0, w("prelu"), ALU.min, ALU.mult))
                link(V.scalar_tensor_tensor(flat(H)[:, 8 * i:8 * i + 8, :], y, 0.0, neg, ALU.max, ALU.add))
            dve.wait_ge(txt_in, 16)

            dve.wait_ge(weights_in[1], 16)
            dve.wait_ge(merged_ready, 1)
            V.memset(WQ[:, :], 0.0).then_inc(dve_step, 1)
            V.memset(WK[:, :], 0.0).then_inc(dve_step, 1)
            link.count += 2
            link(V.memset(MB[:, :], 0.0))
            for b in range(B):
                rows = slice(b * D, (b + 1) * D)
                V.tensor_copy(WQ[rows, b * HR:(b + 1) * HR], ps[rows, 5, 0:HR]).then_inc(merged_used, 1)
                V.tensor_copy(WK[rows, b * HR:(b + 1) * HR], ps[rows, 5, HR:2 * HR]).then_inc(merged_used, 1)
            V.tensor_copy(BQ[:, :], ps[:, 5, 64:96]).then_inc(merged_used, 1)
            V.tensor_copy(BK[:, :], ps[0:D, 5, 96:97]).then_inc(merged_used, 1)
            V.tensor_copy(WVO[:, :, :], ps[:, 5, 128:256].rearrange("p (t d) -> p t d", t=2)).then_inc(merged_used, 1)
            layernorm(flat(H), flat(X), 0)
            layernorm(flat(X), flat(Z), 1)
            dve.wait_ge(klog_ready, 1)
            dve.wait_ge(merged_used, 7)
            link(V.tensor_reduce(small[0:D, 0:1], ps[0:D, 0:NCH, 0:CH], AX.XY, ALU.max))
            link(V.tensor_tensor(small[0:D, 1:2], small[0:D, 0:1], BK[:, :], ALU.add))
            V.tensor_tensor(small[0:D, 4:5], BK[:, :], small[0:D, 1:2], ALU.subtract).then_inc(kshift_ready, 1)
            dve.wait_ge(kexp_ready, 1)
            link(V.reciprocal(small[0:D, 6:7], small[0:D, 5:6]))
            V.tensor_scalar(NF[0:D, :], NF[0:D, :], small[0:D, 6:7], None, ALU.mult).then_inc(knorm_ready, 1)
            dve.wait_ge(kturned, 1)
            V.tensor_copy(KT[:, :, :].rearrange("p (c j) r -> p c (j r)", c=NCH), ps[:, 0:NCH, 0:BC * D]).then_inc(kt_ready, 1)
            dve.wait_ge(ut_ready, 1)
            for b in range(B):
                rows = slice(b * D, (b + 1) * D)
                V.tensor_scalar(UTs[rows, :], ps[rows, 6, b * HR:(b + 1) * HR], w("ln1_g", rows), w("ln1_b", rows),
                                ALU.mult, ALU.add).then_inc(uts_ready, 1)
            dve.wait_ge(kx_ready, 1)
            for b in range(B):
                for t in range(2):
                    V.scalar_tensor_tensor(KX[:, b, t, :], ps[:, 7 * b, t * HR:(t + 1) * HR],
                                           w("bxcol")[:, t:t + 1], w("headmask")[:, t * HR:(t + 1) * HR],
                                           ALU.add, ALU.mult).then_inc(kxs_ready, 1)
            dve.wait_ge(m_ready, 1)
            for b in range(B):
                V.tensor_copy(MB[b * HR:(b + 1) * HR, b * D:(b + 1) * D],
                              ps[b * HR:(b + 1) * HR, 6, 128:128 + D]).then_inc(mb_ready, 1)
            dve.wait_ge(qlog_ready, 1)
            lq = LG[:, :, :].rearrange("p (c j) (b r) -> p c (j b) r", c=NCH, b=B)
            bq = BQ[:, :].unsqueeze(1).broadcast_to([P, BC * B, HR])
            for c in range(NCH):
                V.tensor_tensor(lq[:, c], ps[:, 3 + c, 0:BC * D].rearrange("p (q r) -> p q r", r=HR), bq,
                                ALU.add).then_inc(dve_step, 1)
                link.count += 1
            dve.wait_ge(dve_step, link.count)
            l4 = LG[:, :, :].rearrange("p k (g r) -> p (k g) r", r=KR)
            q4 = QS[:, :, :].rearrange("p k (g r) -> p (k g) r", r=KR)
            gsum = T2_flat[:, 0:KB * 16]
            link(V.tensor_reduce(gsum, l4, AX.X, ALU.max))
            V.tensor_tensor(l4, l4, bc(gsum, KR), ALU.subtract).then_inc(qshift_ready, 1)
            dve.wait_ge(qexp_ready, 1)
            link(V.reduce_sum(gsum, q4, AX.X))
            grec = T2_flat[:, 256:256 + KB * 16]
            link(V.reciprocal(grec, gsum))
            V.tensor_tensor(q4, q4, bc(grec, KR), ALU.mult).then_inc(qs_ready, 1)
            link(V.tensor_tensor(flat(T1), flat(X), row(w("a_bo")), ALU.add))
            dve.wait_ge(attn_ready, 1)
            dve.wait_ge(qs_ready, 1)
            link(V.tensor_tensor(three(T2), out_psum(), three(T1), ALU.add))
            layernorm(flat(T2), flat(Z), 2)
            link(V.tensor_tensor(flat(T1), flat(T2), row(w("a_b2")), ALU.add))
            link(V.tensor_tensor(flat(H), flat(H), flat(T1), ALU.add))
            edge_keys()
            dve.wait_ge(mlp_out[0], 2 * NCH)
            link(V.tensor_tensor(three(H), out_psum(), three(H), ALU.add))

            dve.wait_ge(weights_in[2], 16)
            layernorm(flat(H), flat(X), 3)
            dve.wait_ge(wcol_ready, 1)
            WC = st[:, 5, :]
            V.tensor_copy(WC, ps[:, 1, 0:Q]).then_inc(wcol_used, 1)
            dve.wait_ge(wcol_used, 1)
            link(V.memset(st[:, 6, :], 0.0))
            for k in range(KB):
                for b in range(B):
                    q = 2 * k + b
                    wq = WC[:, q:q + 1]
                    if k:
                        V.tensor_scalar(junk[:, 0:k * P], WROW[:, b, 0:k * P], wq, None, ALU.is_ge, ALU.add,
                                        accum_out=st[:, 6, q:q + 1]).then_inc(dve_step, 1)
                        link.count += 1
                        dve.wait_ge(dve_step, link.count)
                    link(V.tensor_scalar(junk[:, 0:N - k * P], WROW[:, b, k * P:N], wq, None, ALU.is_gt, ALU.add,
                                         accum_out=st[:, 7, q:q + 1]))
                    link(V.scalar_tensor_tensor(junk[:, 0:P], WROW[:, b, k * P:(k + 1) * P], wq, w("tri"), ALU.is_equal,
                                                ALU.mult, accum_out=st[:, 8, q:q + 1]))
            link(V.tensor_tensor(st[:, 6, :], st[:, 6, :], st[:, 7, :], ALU.add))
            link(V.tensor_tensor(st[:, 6, :], st[:, 6, :], st[:, 8, :], ALU.add))
            link(V.scalar_tensor_tensor(st[:, 9, :], st[:, 6, :], float(TOPK), WC, ALU.is_lt, ALU.mult))
            link(V.tensor_tensor(flat(H), flat(H), flat(X), ALU.add))
            dve.wait_ge(mlp_out[1], 2 * NCH)
            out3 = out_psum().rearrange("p c (q d) -> p c q d", d=D)
            for c in range(NCH):
                V.tensor_tensor(t13[:, c], out3[:, c], row(w("f_b2"), BC * B), ALU.add).then_inc(dve_step, 1)
                link.count += 1
            dve.wait_ge(dve_step, link.count)
            link(V.tensor_tensor(flat(T1), flat(T1), bc(st[:, 9, :], D), ALU.mult))
            link(V.tensor_tensor(flat(H), flat(H), flat(T1), ALU.add))

            def powers_of(levels=7):
                for l in range(levels):
                    p0, q0, r0 = (powers[:, l, i:i + 1] for i in range(3))
                    link(V.tensor_tensor(powers[:, l, 3:4], q0, r0, ALU.mult))
                    link(V.scalar_tensor_tensor(powers[:, l + 1, 0:1], p0, p0, powers[:, l, 3:4], ALU.mult, ALU.add))
                    link(V.scalar_tensor_tensor(powers[:, l + 1, 1:2], q0, 2.0, p0, ALU.mult, ALU.mult))
                    link(V.scalar_tensor_tensor(powers[:, l + 1, 2:3], r0, 2.0, p0, ALU.mult, ALU.mult))

            def scan(n):
                def update(dst, src, l, done=None):
                    p0, q0, r0 = (powers[:, l, i:i + 1] for i in range(3))
                    link(V.scalar_tensor_tensor(SA[:, :, dst], SA[:, :, src], p0, SA[:, :, dst], ALU.mult, ALU.add))
                    a = V.scalar_tensor_tensor(SA[:, 0, dst], SA[:, 1, src], q0, SA[:, 0, dst], ALU.mult, ALU.add)
                    a.then_inc(done if done is not None else dve_step, 1)
                    b = V.scalar_tensor_tensor(SA[:, 1, dst], SA[:, 0, src], r0, SA[:, 1, dst], ALU.mult, ALU.add)
                    if done is not None:
                        b.then_inc(done, 1)
                    else:
                        link.count += 1
                        link(b)

                for l in range(7):
                    d = 1 << l
                    update(slice(2 * d - 1, N, 2 * d), slice(d - 1, N - d, 2 * d), l)
                for i in range(1, KB):
                    update(slice(P * (i + 1) - 1, P * (i + 1)), slice(P * i - 1, P * i), 7)
                for l in range(6, -1, -1):
                    d = 1 << l
                    update(slice(3 * d - 1, N, 2 * d), slice(2 * d - 1, N - d, 2 * d), l, scan_ready if l == 0 else None)

            def pick(logits, E, onehot, tmp):
                link(V.tensor_reduce(st[:, 10, :], logits, AX.X, ALU.max))
                link(V.tensor_tensor(tmp, logits, bc(st[:, 10, :], E), ALU.is_equal))
                link(V.scalar_tensor_tensor(tmp, tmp, -64.0, row(iota64[:, 0:E]), ALU.mult, ALU.add))
                link(V.tensor_reduce(st[:, 11, :], tmp, AX.X, ALU.min))
                link(V.tensor_tensor(onehot, row(w("iota")[:, 0:E]), bc(st[:, 11, :], E), ALU.is_equal))

            dve.wait_ge(weights_in[3], 16)
            layernorm(flat(H), flat(X), 4)
            link(V.tensor_scalar(coef[:, 0:1], w("a"), DT * DT, 1.0, ALU.mult, ALU.add))
            link(V.reciprocal(powers[:, 0, 0:1], coef[:, 0:1]))
            link(V.tensor_scalar(powers[:, 0, 2:3], powers[:, 0, 0:1], DT, None, ALU.mult))
            link(V.scalar_tensor_tensor(powers[:, 0, 1:2], powers[:, 0, 2:3], -1.0, w("a"), ALU.mult, ALU.mult))
            link(V.tensor_copy(coef[:, 2:3], powers[:, 0, 2:3]))
            link(V.tensor_scalar(coef[:, 3:4], coef[:, 2:3], DT, None, ALU.mult))
            link(V.tensor_tensor(coef[:, 4:5], coef[:, 2:3], w("bB"), ALU.mult))
            V.tensor_tensor(coef[:, 5:6], coef[:, 3:4], w("bB"), ALU.mult).then_inc(coef_ready, 1)
            powers_of()
            link(V.tensor_tensor(bcd[:, :], w("bC"), w("bD"), ALU.add))
            link(V.tensor_scalar(iota64[:, :], w("iota"), 64.0, None, ALU.add))
            link(V.tensor_tensor(flat(H), flat(H), flat(X), ALU.add))
            dve.wait_ge(force_ready, 2 * NCH)
            scan(0)
            dve.wait_ge(y_ready, 1)
            out3 = out_psum().rearrange("p c (q d) -> p c q d", d=D)
            for c in range(NCH):
                V.tensor_tensor(t13[:, c], out3[:, c], row(bcd[:, :], BC * B), ALU.add).then_inc(cd_step, 1)
            dve.wait_ge(cd_step, NCH)
            V.engine_nop().then_inc(cd_ready, 1)
            dve.wait_ge(silu_ready, 1)
            link(V.tensor_tensor(flat(T1), flat(Z), flat(T2), ALU.mult))
            link(V.tensor_tensor(flat(H), flat(H), flat(T1), ALU.add))

            layernorm(flat(H), flat(X), 5)
            dve.wait_ge(router_ready, 1)
            lv = LG[:, :, :].rearrange("p k (b e) -> p (k b) e", b=B)
            for c in range(NCH):
                V.tensor_tensor(lv[:, 6 * c:6 * c + 6, :], ps[:, 3 + c, 0:BC * D].rearrange("p (q e) -> p q e", e=E1),
                                row(w("rb"), 6), ALU.add).then_inc(dve_step, 1)
                link.count += 1
            dve.wait_ge(dve_step, link.count)
            pick(lv, E1, flat(Z)[:, :, E1:2 * E1], QS[:, :, :].rearrange("p k (b e) -> p (k b) e", b=B))
            V.tensor_scalar(flat(Z)[:, :, 0:E1], flat(Z)[:, :, E1:2 * E1], -1.0, None, ALU.add).then_inc(gates_ready, 1)
            edge_digits()
            take_edges(0)
            dve.wait_ge(mlp_out[2], 2 * NCH)
            link(V.scalar_tensor_tensor(three(H), out_psum(), 0.0, three(H), ALU.max, ALU.add))

            dve.wait_ge(weights_in[4], 16)
            layernorm(flat(H), flat(X), 6)
            dve.wait_ge(lambda_ready, 1)
            link(V.tensor_scalar(lam_i[:, :], lam[:, 2:3], 1.0 / TWO_PI, None, ALU.mult))
            link(V.tensor_copy(lam[:, 9:10], lam_i[:, :]))
            link(V.scalar_tensor_tensor(lam[:, 3:4], lam[:, 9:10], -TWO_PI_HI, lam[:, 2:3], ALU.mult, ALU.add))
            link(V.scalar_tensor_tensor(lam[:, 3:4], lam[:, 9:10], -TWO_PI_LO, lam[:, 3:4], ALU.mult, ALU.add))
            link(V.tensor_scalar(lam[:, 3:4], lam[:, 3:4], 3.1415925, -3.1415925, ALU.min, ALU.max))
            link(V.scalar_tensor_tensor(lam[:, 4:5], lam[:, 3:4], -1.0, lam[:, 3:4], ALU.mult, ALU.max))
            V.tensor_scalar(lam[:, 4:5], lam[:, 4:5], -1.0, TWO_PI / 4, ALU.mult, ALU.add).then_inc(coef_ready, 1)
            dve.wait_ge(lambda_ready, 3)
            link(V.tensor_tensor(powers[:, 0, 0:1], lam[:, 1:2], lam[:, 6:7], ALU.mult))
            link(V.tensor_tensor(powers[:, 0, 2:3], lam[:, 1:2], lam[:, 5:6], ALU.mult))
            link(V.tensor_scalar(powers[:, 0, 1:2], powers[:, 0, 2:3], -1.0, None, ALU.mult))
            link(V.tensor_tensor(lam[:, 10:11], powers[:, 0, 2:3], powers[:, 0, 2:3], ALU.mult))
            link(V.scalar_tensor_tensor(lam[:, 10:11], powers[:, 0, 0:1], powers[:, 0, 0:1], lam[:, 10:11], ALU.mult, ALU.add))
            link(V.tensor_scalar(lam[:, 10:11], lam[:, 10:11], -1.0, 1.0, ALU.mult, ALU.add))
            V.tensor_scalar(lam[:, 7:8], lam[:, 10:11], 0.0, None, ALU.max).then_inc(coef_ready, 1)
            powers_of()
            V.tensor_scalar(w("Cim"), w("Cim"), -1.0, None, ALU.mult).then_inc(coef_ready, 1)
            link(V.tensor_tensor(flat(T1), flat(X), row(w("Dskip")), ALU.mult))
            link(V.tensor_tensor(flat(H), flat(H), flat(T1), ALU.add))
            dve.wait_ge(force_ready, 4 * NCH)
            scan(1)
            dve.wait_ge(y_ready, 2)
            link(V.tensor_tensor(three(H), out_psum(), three(H), ALU.add))

            layernorm(flat(H), flat(X), 7)
            dve.wait_ge(gat_ready, 1)
            hg = ps[:, 3, 0:Q * 16]
            link(V.tensor_copy(table[:, E2:FEAT, :].rearrange("p f (b k) -> p k b f", b=B), hg.rearrange("p (k b f) -> p k b f", b=B, f=16)))
            hq = hg.rearrange("p (q f) -> p q f", f=16)
            prod = flat(T1)[:, :, 0:16]
            for att, dst in (("att_src", table[:, 0:E2, :]), ("att_dst", dst_score)):
                link(V.tensor_tensor(prod, hq, row(w(att)), ALU.mult))
                link(V.reduce_sum(pick4[:, 0, :, :], prod.rearrange("p q (h e) -> p q h e", e=4), AX.X))
                link(V.tensor_copy(dst.rearrange("p h (b k) -> p k b h", b=B), pick4[:, 0, :, :].rearrange("p (k b) h -> p k b h", b=B)))
            V.tensor_reduce(local_max[:, :], table[:, 0:E2, :], AX.X, ALU.max).then_inc(local_max_ready, 1)
            left = T2_flat[:, 0:FEAT * NT].rearrange("p (f t) -> p f t", t=NT)
            link(V.tensor_copy(parts[:, 0, :, :], table[:, E2:, :]))
            link(V.tensor_tensor(left, table[:, E2:, :], parts[:, 0, :, :], ALU.subtract))
            link(V.tensor_copy(parts[:, 1, :, :], left))
            link(V.tensor_tensor(left, left, parts[:, 1, :, :], ALU.subtract))
            V.tensor_copy(parts[:, 2, :, :], left).then_inc(parts_ready, 1)
            dve.wait_ge(score_max_ready, 1)

            def edge_pass(it):
                reg = not isinstance(it, int)
                hold(dve, rest_turned, it + 1, reg)
                linked(it, V.tensor_reduce(small[0:1, 8:9], ps[0:1, 4, CH:CH + P], AX.X, ALU.max))
                V.tensor_scalar(flag[:, bass.ds(it, 1)], small[0:1, 8:9], 1.0, None, ALU.min).then_inc(flag_ready, 1)

                def mask(g, s, first=False):
                    hold(dve, gathered, it * GN + g + 1, reg)
                    if not first:
                        hold(dve, selected, it * GN + g - 1, reg)
                    at = bass.ts(g, GRP)
                    rows_of = ps[:, 2 * s:2 * s + GRP, 0:FEAT * NT].rearrange("p g (f t) -> p g f t", t=NT)
                    V.tensor_tensor(product[s][:, :, 0:16, :], rows_of[:, :, 0:16, :],
                                    src_hi_oh[:, at, :].unsqueeze(2).broadcast_to([P, GRP, 16, NT]), ALU.mult).then_inc(product_step, 1)
                    V.tensor_tensor(product[s][:, :, 16:FEAT, :], rows_of[:, :, 16:FEAT, :],
                                    dst_hi_oh[:, at, :].unsqueeze(2).broadcast_to([P, GRP, E2, NT]), ALU.mult).then_inc(product_step, 1)

                def select(g, s):
                    hold(dve, product_step, (it * GN + g) * 2 + 2, reg)
                    V.reduce_sum(e_val[:, bass.ts(g, GRP), :], product[s], AX.X).then_inc(selected, 1)

                for s in range(2):
                    mask(s, s, first=not reg)
                select(0, 0)
                with dve.Fori(1, GN // 2) as r:
                    mask(2 * r, 0)
                    select(2 * r + (-1), 1)
                    mask(2 * r + 1, 1)
                    select(2 * r, 0)
                select(GN - 1, 1)
                hold(dve, selected, (it + 1) * GN, reg)
                t0, t1, dsc = e_tmp[:, 0, :, :], e_tmp[:, 1, :, :], e_val[:, :, 16:FEAT]
                linked(it, V.tensor_tensor(e_w[:, :, 0:16], e_val[:, :, 0:16], row(w("att_src"), SLOTS), ALU.mult))
                linked(it, V.reduce_sum(t0, e_w[:, :, 0:16].rearrange("p s (h e) -> p s h e", e=4), AX.X))
                linked(it, V.tensor_tensor(t0, t0, dsc, ALU.add))
                linked(it, V.tensor_tensor(t1, dsc, row(score_max[:, :], SLOTS), ALU.add))
                linked(it, V.scalar_tensor_tensor(t0, t0, 0.2, t0, ALU.mult, ALU.max))
                linked(it, V.scalar_tensor_tensor(t1, t1, 0.2, t1, ALU.mult, ALU.max))
                linked(it, V.tensor_tensor(t0, t0, t1, ALU.subtract))
                V.tensor_scalar(t0, t0, 0.0, None, ALU.min).then_inc(edge_shift_ready, 1)
                hold(dve, edge_exp_ready, it + 1, reg)
                linked(it, V.tensor_tensor(e_w[:, :, E2:FEAT].rearrange("p s (h e) -> p s h e", e=4),
                                       e_val[:, :, 0:16].rearrange("p s (h e) -> p s h e", e=4), bc(e_w[:, :, 0:E2], 4), ALU.mult))

                if not reg:
                    V.engine_nop().then_inc(terms_ready, 1)

                def spread_out(g, s, first=False):
                    if not first:
                        hold(dve, scattered, it * GN + g - 1, reg)
                    at = bass.ts(g, GRP)
                    V.tensor_tensor(dst_lo_oh[s], row(w("iota128"), GRP), bc(field[:, 2, at], P), ALU.is_equal).then_inc(outer_ready, 1 if reg or s else 2)
                    if not reg and s == 0:
                        return
                    V.tensor_tensor(outer[s], bc(e_w[:, at, :], NT), dst_hi_oh[:, at, :].unsqueeze(2).broadcast_to([P, GRP, FEAT, NT]),
                                    ALU.mult).then_inc(outer_ready, 1)

                def onehots(i, s, first=False):
                    if not first:
                        dve.wait_ge(counted, i + (-1))
                    at = bass.ts(i, HG)
                    V.tensor_tensor(oh_hi[s], digit_hi[:, at].unsqueeze(1).broadcast_to([P, NHI, HG]),
                                    digit_values[:, 0:NHI, :], ALU.is_equal).then_inc(onehots_ready, 1)
                    V.tensor_tensor(oh_lo[s], digit_lo[:, at].unsqueeze(1).broadcast_to([P, NLO, HG]),
                                    digit_values[:, :, :], ALU.is_equal).then_inc(onehots_ready, 1)

                def four_groups(r, first=False):
                    for h in range(2):
                        for s in range(2):
                            spread_out(4 * r + (2 * h + s), s, first=first and h == 0)
                        if not reg:
                            onehots(2 * r + h, h, first=first)

                four_groups(0, first=not reg)
                with dve.Fori(1, GN // 4) as r:
                    four_groups(r)
                hold(dve, scattered, it * GN + GN, reg)
                assert steps[0] == PASS_STEPS, steps

            edge_pass(0)
            dve.wait_ge(counted, CAND // HG)
            for o in range(2):
                V.tensor_copy(n_last[64 * o:64 * o + 64, :],
                              ps[0:NLO, 4, 0:NHI].rearrange("p (t o) -> p t o", o=2)[:, :, o]).then_inc(counts_used, 1)
            dve.wait_ge(counts_used, 2)
            more = dve.value_load(flag[0:1, 0:1], min_val=0, max_val=1)
            with dve.If(more > 0):
                with dve.Fori(1, PASSES) as it:
                    more = dve.value_load(flag[0:1, bass.ds(it - 1, 1)], min_val=0, max_val=1)
                    with dve.If(more > 0):
                        take_edges(it)
                        edge_pass(it)

            own, far, top = node_w[:, 1, 0, :, :], node_w[:, 1, 1, :, :], node_w[:, 2, 0, :, :]
            dve.wait_ge(last_ready, 1)
            link(V.tensor_copy(last_node[:, :], ps[:, 5, 0:FEAT]))
            link(V.tensor_tensor(own, table[:, 0:E2, :], dst_score, ALU.add))
            link(V.tensor_tensor(far, dst_score, bc(last_node[:, 0:E2], NT), ALU.add))
            link(V.tensor_tensor(top, dst_score, bc(score_max[:, :], NT), ALU.add))
            for x in (own, far, top):
                link(V.scalar_tensor_tensor(x, x, 0.2, x, ALU.mult, ALU.max))
            link(V.tensor_tensor(own, own, top, ALU.subtract))
            V.tensor_tensor(far, far, top, ALU.subtract).then_inc(node_shift_ready, 1)
            dve.wait_ge(node_exp_ready, 1)
            own, far = node_w[:, 0, 0, :, :], node_w[:, 0, 1, :, :]
            den, rden = node_w[:, 1, 0, :, :], node_w[:, 1, 1, :, :]
            dve.wait_ge(counts_used, 2)
            link(V.tensor_tensor(far, far, n_last[:, :].unsqueeze(1).broadcast_to([P, E2, NT]), ALU.mult))
            sums = ps[:, 7, 0:FEAT * NT].rearrange("p (f t) -> p f t", t=NT)
            link(V.tensor_tensor(den, own, far, ALU.add))
            link(V.tensor_tensor(den, den, sums[:, 0:E2, :], ALU.add))
            link(V.scalar_tensor_tensor(den, den, 1e-16, den, ALU.mult, ALU.add))
            link(V.reciprocal(rden, den))

            def four(x):
                return x.rearrange("p (h e) t -> p h e t", e=4)

            def per_head(x):
                return x.unsqueeze(2).broadcast_to([P, E2, 4, NT])

            a0 = T1[:, :, :, :].rearrange("p k b d -> p (k b d)")[:, 0:16 * NT].rearrange("p (f t) -> p f t", t=NT)
            a1 = T1[:, :, :, :].rearrange("p k b d -> p (k b d)")[:, 512:512 + 16 * NT].rearrange("p (f t) -> p f t", t=NT)
            link(V.tensor_tensor(four(a0), four(table[:, E2:FEAT, :]), per_head(own), ALU.mult))
            link(V.tensor_tensor(four(a1), four(bc(last_node[:, E2:FEAT], NT)), per_head(far), ALU.mult))
            link(V.tensor_tensor(a0, a0, a1, ALU.add))
            link(V.tensor_tensor(a0, a0, sums[:, E2:FEAT, :], ALU.add))
            link(V.tensor_tensor(four(a0), four(a0), per_head(rden), ALU.mult))
            agg = flat(T2)[:, :, 0:16]
            link(V.tensor_tensor(agg.rearrange("p (k b) f -> p k b f", b=B), a0.rearrange("p f (b k) -> p k b f", b=B),
                                 w("b_gat").unsqueeze(1).unsqueeze(1).broadcast_to([P, KB, B, 16]), ALU.add))
            layernorm(agg, agg, 8, 16, flat(XC)[:, :, 0:16], flat(T1)[:, :, 0:16])
            link(V.tensor_tensor(agg, agg, row(w("g_gamma")), ALU.mult))
            link(V.tensor_tensor(agg, agg, row(w("g_beta")), ALU.add))
            sc = pick4[:, 0, :, :]
            link(V.reduce_sum(sc, agg.rearrange("p q (h e) -> p q e h", e=4), AX.X))
            link(V.tensor_scalar(sc, sc, 0.25, None, ALU.mult))
            pick(sc, E2, pick4[:, 1, :, :], gate4[:, :, :])
            link(V.tensor_copy(st[:, 14, :], st[:, 10, :]))
            link(V.scalar_tensor_tensor(sc, pick4[:, 1, :, :], -BIG, sc, ALU.mult, ALU.add))
            pick(sc, E2, pick4[:, 2, :, :], gate4[:, :, :])
            V.tensor_tensor(st[:, 13, :], st[:, 10, :], st[:, 14, :], ALU.subtract).then_inc(gate_shift_ready, 1)
            dve.wait_ge(gate_exp_ready, 1)
            link(V.tensor_scalar(st[:, 14, :], st[:, 12, :], 1.0, None, ALU.add))
            link(V.reciprocal(st[:, 15, :], st[:, 14, :]))
            link(V.tensor_tensor(st[:, 12, :], st[:, 12, :], st[:, 15, :], ALU.mult))
            link(V.tensor_tensor(pick4[:, 1, :, :], pick4[:, 1, :, :], bc(st[:, 15, :], E2), ALU.mult))
            link(V.tensor_tensor(pick4[:, 2, :, :], pick4[:, 2, :, :], bc(st[:, 12, :], E2), ALU.mult))
            link(V.tensor_tensor(gate4[:, :, :], pick4[:, 1, :, :], pick4[:, 2, :, :], ALU.add))
            for v in range(Q):
                s, k = v // BC, v % BC
                kk, b = BC * (s // 2) + k, s % 2
                dve.wait_ge(mlp_out[3], v + 1)
                tmp = T2_flat[:, 0:256].rearrange("p (e d) -> p e d", e=E2)
                link(V.tensor_tensor(tmp, ps[:, v % 3, 0:256].rearrange("p (e d) -> p e d", e=E2), bc(gate4[:, 2 * kk + b, :], D), ALU.mult))
                V.reduce_sum(T1[:, kk, b, :], tmp.rearrange("p e d -> p d e"), AX.X).then_inc(gated, 1)
                dve.wait_ge(gated, v + 1)
            link(V.tensor_tensor(flat(H), flat(H), flat(T1), ALU.add))
            dve.wait_ge(weights_in[5], 16)
            layernorm(flat(H), flat(X), 9)
            dve.wait_ge(v3_ready, 1)
            for c in range(NCH):
                V.tensor_tensor(VT[:, BC * c:BC * c + BC, :, :].rearrange("p k b d -> p (k b) d"),
                                ps[:, 3 + c, 0:CH].rearrange("p (q d) -> p q d", d=D), row(w("bv3"), 6),
                                ALU.add).then_inc(v3_used, 1)

            def largest(u):
                i, base = u // 2, 3 * (u % 2)
                L = (i + 1) * P
                dve.wait_ge(s3_ready, u + 1)
                all3 = ps[:, base:base + 3, :].rearrange("p c n -> p (c n)")
                link(V.tensor_tensor(all3[:, L - P:L], all3[:, L - P:L], w("causal"), ALU.add))
                link(V.tensor_reduce(den3[:, 0, u:u + 1], all3[:, 0:L], AX.X, ALU.max))
                V.tensor_scalar(den3[:, 1, u:u + 1], den3[:, 0, u:u + 1], -SCALE, None, ALU.mult).then_inc(shift3_ready, 1)

            def attended(u):
                i, b = u // 2, u % 2
                dve.wait_ge(o3_ready, u + 1)
                link(V.reciprocal(den3[:, 3, u:u + 1], den3[:, 2, u:u + 1]))
                V.scalar_tensor_tensor(H[:, i, b, :], ps[:, 6 + u % 2, 0:D], den3[:, 3, u:u + 1], H[:, i, b, :],
                                       ALU.mult, ALU.add).then_inc(o3_used, 1)

            largest(0)
            for u in range(Q):
                if u + 1 < Q:
                    largest(u + 1)
                if u:
                    attended(u - 1)
            attended(Q - 1)
            dve.wait_ge(o3_used, Q)

            layernorm(flat(H), flat(X), 10)
            link(V.memset(flat(Z), 0.0))
            dve.wait_ge(router_ready, 2)
            lv = LG[:, :, :].rearrange("p k (b e) -> p (k b) e", b=B)[:, :, 0:E3]
            tmp = QS[:, :, :].rearrange("p k (b e) -> p (k b) e", b=B)
            for c in range(NCH):
                V.tensor_tensor(lv[:, 6 * c:6 * c + 6, :], ps[:, 3 + c, 0:BC * D].rearrange("p (q e) -> p q e", e=E1)[:, :, 0:E3],
                                row(w("bg3"), 6), ALU.add).then_inc(dve_step, 1)
                link.count += 1
            dve.wait_ge(dve_step, link.count)
            first, second = tmp[:, :, E3:2 * E3], tmp[:, :, 2 * E3:3 * E3]
            pick(lv, E3, first, tmp[:, :, 0:E3])
            link(V.scalar_tensor_tensor(lv, first, -BIG, lv, ALU.mult, ALU.add))
            pick(lv, E3, second, tmp[:, :, 0:E3])
            link(V.tensor_tensor(flat(Z)[:, :, E3:2 * E3], first, second, ALU.add))
            V.tensor_scalar(flat(Z)[:, :, 0:E3], flat(Z)[:, :, E3:2 * E3], -1.0, None, ALU.add).then_inc(gates_ready, 1)
            dve.wait_ge(mlp_out[4], 2 * NCH)
            link(V.tensor_tensor(three(H), out_psum(), three(H), ALU.add))
            V.engine_nop().then_inc(h_ready, 1)

        @block.tensor
        def _(pe):
            MM = nc.tensor.matmul
            ident = w("ident")

            def turn(t, n, src):
                pe.wait_ge(norm_ready, n + 1)
                for c in range(NCH):
                    for j in range(BC):
                        last = nc.tensor.transpose(ps[:, c, j * P:(j + 1) * P], blk(src, BC * c + j), ident)
                    last.then_inc(turned, 1)

            def turn_narrow(src, done):
                for c in range(NCH):
                    for j in range(BC):
                        last = nc.tensor.transpose(ps[0:D, 3 + c, j * P:(j + 1) * P], src[:, BC * c + j, :], ident)
                    last.then_inc(done, 1)

            def mlp(m, t, J, w1, w2, gated=False, bias=None):
                def hidden(s):
                    c, b = s // 2, s % 2
                    rows = slice(b * D, (b + 1) * D)
                    if b == 0:
                        pe.wait_ge(xf_ready, NCH * t + c + 1)
                    for j in range(J):
                        n = s * J + j
                        if n >= 5:
                            pe.wait_ge(g_ready[m], n - 4)
                        o = ps[:, 3 + n % 5, 0:CH]
                        if gated:
                            last = MM(o, w(w1)[:, (b * J + j) * P:(b * J + j + 1) * P], (XF, NF)[b][:, c * CH:(c + 1) * CH],
                                      start=True, stop=True)
                        else:
                            last = MM(o, w(w1, rows)[:, j * P:(j + 1) * P], XF[rows, c * CH:(c + 1) * CH], start=True, stop=True)
                        last.then_inc(hid_ready[m], 1)

                def output(s):
                    c, b = s // 2, s % 2
                    pe.wait_ge(g_ready[m], (s + 1) * J)
                    for k in range(BC):
                        o = ps[:, c, k * P + b * D:k * P + (b + 1) * D]
                        for j in range(J):
                            last = MM(o, G[:, s % 2, j, k * P:(k + 1) * P], w(w2)[:, j * D:(j + 1) * D],
                                      start=j == 0, stop=j == J - 1 and bias is None)
                        if bias is not None:
                            at = c * CH + k * P
                            last = MM(o, (XF, NF)[b][:, at:at + P], w(bias)[:, b * D:(b + 1) * D],
                                      start=False, stop=True)
                    last.then_inc(mlp_out[m], 1)

                hidden(0)
                for s in range(2 * NCH):
                    if s + 1 < 2 * NCH:
                        hidden(s + 1)
                    output(s)

            pe.wait_ge(weights_in[0], 16)
            pe.wait_ge(x_in, 16)
            for i, name in enumerate(("tok_Wq", "tok_Wk")):
                for th in range(2):
                    last = MM(ps[:, 2 * i + th, :], w(name), XF[:, th * 512:(th + 1) * 512], start=True, stop=True)
            last.then_inc(tok_proj, 1)
            for k in range(IB):
                last = MM(ps[:, 4 + k // 4, (k % 4) * P:(k % 4 + 1) * P], XF[:, k * P:(k + 1) * P], w("tok_Wv"), start=True, stop=True)
            last.then_inc(tok_proj, 1)
            pe.wait_ge(tok_proj_used, 6)

            def scores(u):
                th, b, j = u // 16, u // IB % 2, u % IB
                rows = slice(b * D, (b + 1) * D)
                if u >= 4:
                    pe.wait_ge(decay_ready, u - 3)
                MM(ps[:, u % 4, :], SA[rows, 1, j * P:(j + 1) * P], SA[rows, 0, th * 512:(th + 1) * 512],
                   start=True, stop=True).then_inc(score_ready, 1)

            def kept(u):
                th, b, j = u // 16, u // IB % 2, u % IB
                pe.wait_ge(decay_ready, u + 1)
                MM(ps[b * D:(b + 1) * D, 6 + th, :], VT[:, j, b, :], ring[:, u % 4, :],
                   start=j == 0, stop=j == IB - 1).then_inc(kept_step, 1)

            for u in range(3):
                scores(u)
            for u in range(32):
                if u + 3 < 32:
                    scores(u + 3)
                kept(u)
            for i in range(2):
                pe.wait_ge(kept_copied, i + 1)
                for k in range(4 * i, 4 * i + 4):
                    last = MM(ps[:, i, (k % 4) * P:(k % 4 + 1) * P], T2_flat[:, k * P:(k + 1) * P], w("tok_Wo"), start=True, stop=True)
                last.then_inc(tok_y, 1)

            pe.wait_ge(weights_in[1], 16)
            bank = ps[:, 5, :]
            for o, lhs, rhs in (
                (bank[:, 0:32], lambda t: w("WxT")[:, t * P:(t + 1) * P], lambda t: w("WqBD")[:, t * HR:(t + 1) * HR]),
                (bank[:, 32:64], lambda t: w("WxT")[:, t * P:(t + 1) * P], lambda t: w("WkBD")[:, t * D:t * D + HR]),
                (bank[:, 64:96], lambda t: w("bxrep")[:, t * P:(t + 1) * P], lambda t: w("WqBD")[:, t * HR:(t + 1) * HR]),
                (bank[0:D, 96:97], lambda t: w("WkBD")[:, t * D:(t + 1) * D], lambda t: w("bxcol")[:, t:t + 1]),
            ):
                for t in range(2):
                    MM(o, lhs(t), rhs(t), start=t == 0, stop=t == 1)
            for t in range(2):
                last = MM(bank[:, 128 + t * D:128 + (t + 1) * D], w("WvT"), w("Wo")[:, t * D:(t + 1) * D], start=True, stop=True)
            last.then_inc(merged_ready, 1)
            turn(0, 1, Z)
            pe.wait_ge(merged_used, 7)
            pe.wait_ge(xf_ready, NCH)
            for c in range(NCH):
                last = MM(ps[0:D, c, 0:CH], WK[:, :], XF[:, c * CH:(c + 1) * CH], start=True, stop=True)
            last.then_inc(klog_ready, 1)
            for c in range(NCH):
                for j in range(BC):
                    last = MM(ps[:, 3 + c, j * D:(j + 1) * D], XF[:, (BC * c + j) * P:(BC * c + j + 1) * P], WQ[:, :],
                              start=True, stop=True)
            last.then_inc(qlog_ready, 1)
            pe.wait_ge(knorm_ready, 1)
            for c in range(NCH):
                for j in range(BC):
                    k = BC * c + j
                    last = nc.tensor.transpose(ps[:, c, j * D:(j + 1) * D], NF[0:D, k * P:(k + 1) * P], ident[0:D, 0:D])
            last.then_inc(kturned, 1)
            pe.wait_ge(kt_ready, 1)
            for k in range(KB):
                last = MM(ps[:, 6, 0:D], blk(Z, k), KT[:, k, :], start=k == 0, stop=k == KB - 1)
            last.then_inc(ut_ready, 1)
            pe.wait_ge(uts_ready, 2)
            for b in range(B):
                rows = slice(b * D, (b + 1) * D)
                for t in range(2):
                    last = MM(ps[:, 7 * b, t * HR:(t + 1) * HR], w("WxD", rows)[:, t * P:(t + 1) * P], UTs[rows, :],
                              start=True, stop=True)
            last.then_inc(kx_ready, 1)
            pe.wait_ge(kxs_ready, 4)
            for b in range(B):
                for t in range(2):
                    last = MM(ps[b * HR:(b + 1) * HR, 6, 128:128 + D], KX[:, b, t, :], WVO[:, t, :], start=t == 0, stop=t == 1)
            last.then_inc(m_ready, 1)
            pe.wait_ge(qs_ready, 1)
            turn_narrow(QS, qturned)
            pe.wait_ge(mb_ready, 2)
            for c in range(NCH):
                pe.wait_ge(qf_ready, c + 1)
                for j in range(BC):
                    k = BC * c + j
                    last = MM(ps[:, c, j * P:(j + 1) * P], NF[0:D, k * P:(k + 1) * P], MB[:, :], start=True, stop=True)
            last.then_inc(attn_ready, 1)
            turn(1, 2, Z)
            mlp(0, 1, 2, "a_W1", "a_W2")

            pe.wait_ge(weights_in[2], 16)
            turn(2, 3, X)
            pe.wait_ge(xf_ready, 3 * NCH)
            for b in range(B):
                rows = slice(b * D, (b + 1) * D)
                for c in range(NCH):
                    last = MM(ps[:, WBANK[b][c], 0:CH], w("wr", rows), XF[rows, c * CH:(c + 1) * CH], start=True, stop=True)
                last.then_inc(wrow_ready, 1)
            pe.wait_ge(wrow_copied, 2 * NCH)
            for k in range(KB):
                for b in range(B):
                    q = 2 * k + b
                    last = nc.tensor.transpose(ps[:, 1, q:q + 1], WROW[0:1, b, k * P:(k + 1) * P], ident[0:1, 0:1])
            last.then_inc(wcol_ready, 1)
            pe.wait_ge(wcol_used, 1)
            mlp(1, 2, 2, "f_w1", "f_w2")

            def count(i, s):
                pe.wait_ge(onehots_ready, 2 * i + 2)
                for t in range(HG):
                    last_mm = MM(ps[0:NLO, 4, 0:NHI], oh_lo[s][:, :, t], oh_hi[s][:, :, t], start=False, stop=False, skip_group_check=True)
                last_mm.then_inc(counted, 1)

            def gates_turn(n):
                pe.wait_ge(gates_ready, n + 1)
                for c in range(NCH):
                    for j in range(BC):
                        last = nc.tensor.transpose(ps[:, 3 + c, j * P:(j + 1) * P], blk(Z, BC * c + j), ident)
                    last.then_inc(gates_turned, 1)
                pe.wait_ge(gates_copied, 3 * NCH * (n + 1))

            def router(t, name):
                pe.wait_ge(xf_ready, NCH * (t + 1))
                for c in range(NCH):
                    for j in range(BC):
                        last = MM(ps[:, 3 + c, j * D:(j + 1) * D], XF[:, (BC * c + j) * P:(BC * c + j + 1) * P], w(name), start=True, stop=True)
                last.then_inc(router_ready, 1)

            def token_product(pairs, done):
                for c in range(NCH):
                    for j in range(BC):
                        at = (BC * c + j) * P
                        for i, (x, m) in enumerate(pairs):
                            last = MM(ps[:, c, j * P:(j + 1) * P], x[:, at:at + P], m, start=i == 0, stop=i == len(pairs) - 1)
                last.then_inc(done, 1)

            pe.wait_ge(weights_in[3], 16)
            turn(3, 4, X)
            for c in range(NCH):
                pe.wait_ge(xf_ready, 3 * NCH + c + 1)
                MM(ps[:, 3 + c, 0:CH], w("WB"), XF[:, c * CH:(c + 1) * CH], start=True, stop=True).then_inc(bu_ready, 1)
            pe.wait_ge(scan_ready, 2)
            token_product([(SA[:, 1, :], w("WC")), (XF[:, :], w("WD"))], y_ready)
            turn(4, 5, X)
            router(4, "rw")
            gates_turn(0)
            mlp(2, 4, 4, "m_W1", "m_W2", gated=True, bias="m_b2")
            pe.wait_ge(weights_in[4], 16)
            turn(5, 6, X)
            pe.wait_ge(xf_ready, 6 * NCH)
            for s, name in enumerate(("Bre", "Bim")):
                for c in range(NCH):
                    MM(ps[:, (3 + s * NCH + c) % 8, 0:CH], w(name), XF[:, c * CH:(c + 1) * CH], start=True, stop=True).then_inc(bu_ready, 1)
            pe.wait_ge(scan_ready, 4)
            pe.wait_ge(coef_ready, 4)
            token_product([(SA[:, 0, :], w("Cre")), (SA[:, 1, :], w("Cim"))], y_ready)

            turn(6, 7, X)
            pe.wait_ge(xf_ready, 7 * NCH)
            for k in range(KB):
                last_mm = MM(ps[:, 3, k * 32:(k + 1) * 32], XF[:, k * P:(k + 1) * P], w("Wgat"), start=True, stop=True)
            last_mm.then_inc(gat_ready, 1)
            pe.wait_ge(parts_ready, 1)
            pe.wait_ge(zeros_ready, 1)
            MM(ps[:, 7, 0:FEAT * NT], zeros[:, :], table[:, 0:FEAT, :].rearrange("p f t -> p (f t)"), start=True, stop=False, skip_group_check=True)

            def edge_pass(it):
                pe.wait_ge(rest_ready, it + 1)
                nc.tensor.transpose(ps[0:1, 4, CH:CH + P], rest8[:, 1:2], ident).then_inc(rest_turned, 1)
                pe.wait_ge(fields_ready, it * 2 + 2)

                def spread(g, s, first=False):
                    if not first:
                        pe.wait_ge(low_read, it * GN + g - 1)
                    for i in range(2):
                        for t in range(GRP):
                            last_mm = MM(ps[:, 5 + s, (i * GRP + t) * P:(i * GRP + t + 1) * P],
                                         lo_b[:, i, bass.ds(GRP * g + t, 1)].broadcast_to([P, P]), ident_b[:, :], start=True, stop=True)
                    last_mm.then_inc(spread_ready, 1)

                def gather(g, s, first=False):
                    pe.wait_ge(oht_ready, it * GN + g + 1)
                    if not first:
                        pe.wait_ge(product_step, (it * GN + g) * 2 - 2)
                    for t in range(GRP):
                        for i, (a, b) in enumerate(((0, 16), (16, FEAT))):
                            for k in range(3):
                                last_mm = MM(ps[:, 2 * s + t, a * NT:b * NT], turned_oh[s][:, (i * GRP + t) * P:(i * GRP + t + 1) * P],
                                             parts[:, k, a:b, :].rearrange("p f t -> p (f t)"), start=k == 0, stop=k == 2)
                    last_mm.then_inc(gathered, 1)

                fresh = isinstance(it, int)
                spread(0, 0, first=fresh)
                spread(1, 1, first=fresh)
                gather(0, 0, first=fresh)
                spread(2, 0)
                gather(1, 1, first=fresh)
                with pe.Fori(1, GN // 2 - 1) as r:
                    spread(2 * r + 1, 1)
                    gather(2 * r, 0)
                    spread(2 * r + 2, 0)
                    gather(2 * r + 1, 1)
                spread(GN - 1, 1)
                gather(GN - 2, 0)
                gather(GN - 1, 1)

                def scatter(g, s, half_g=None):
                    pe.wait_ge(outer_ready, (it * GN + g) * 2 + 2)
                    if fresh and s == 0:
                        pe.wait_ge(pool_outer, half_g + 1)
                    for t in range(GRP):
                        last_mm = MM(ps[:, 7, 0:FEAT * NT], dst_lo_oh[s][:, t, :], outer[s][:, t, :, :].rearrange("p f t -> p (f t)"),
                                     start=False, stop=False, skip_group_check=True)
                    last_mm.then_inc(scattered, 1)

                if fresh:
                    MM(ps[0:NLO, 4, 0:NHI], zeros[:, 0:NLO], zeros[:, 0:NHI], start=True, stop=False, skip_group_check=True)
                with pe.Fori(0, GN // 4) as r:
                    for h in range(2):
                        for s in range(2):
                            scatter(4 * r + (2 * h + s), s, 2 * r + h)
                        if fresh:
                            count(2 * r + h, h)

            edge_pass(0)
            pe.wait_ge(flag_ready, 1)
            more = pe.value_load(flag[0:1, 0:1], min_val=0, max_val=1)
            with pe.If(more > 0):
                with pe.Fori(1, PASSES) as it:
                    more = pe.value_load(flag[0:1, bass.ds(it - 1, 1)], min_val=0, max_val=1)
                    with pe.If(more > 0):
                        edge_pass(it)
            MM(ps[:, 5, 0:FEAT], ident[:, P - 1:P].broadcast_to([P, P]), table[:, 0:FEAT, NT - 1], start=True, stop=True).then_inc(last_ready, 1)

            def hidden(s):
                c, b = s // 2, s % 2
                rows = slice(b * D, (b + 1) * D)
                for j in range(E2):
                    n = s * E2 + j
                    if n >= 5:
                        pe.wait_ge(g_ready[3], n - 4)
                    MM(ps[:, 3 + n % 5, 0:CH], w("g_W1", rows)[:, j * P:(j + 1) * P], XF[rows, c * CH:(c + 1) * CH],
                       start=True, stop=True).then_inc(hid_ready[3], 1)

            def output(s):
                pe.wait_ge(g_ready[3], (s + 1) * E2)
                for k in range(BC):
                    v = BC * s + k
                    if v >= 3:
                        pe.wait_ge(gated, v - 2)
                    MM(ps[:, v % 3, 0:E2 * D], ident[:, 0:1].broadcast_to([P, P]), w("g_b2"), start=True, stop=False)
                    for j in range(E2):
                        last_mm = MM(ps[:, v % 3, j * D:(j + 1) * D], G[:, s % 2, j, k * P:(k + 1) * P], w("g_W2")[:, j * D:(j + 1) * D],
                                     start=False, stop=j == E2 - 1)
                    last_mm.then_inc(mlp_out[3], 1)

            pe.wait_ge(gate_shift_ready, 1)
            hidden(0)
            for s in range(2 * NCH):
                if s + 1 < 2 * NCH:
                    hidden(s + 1)
                output(s)
            pe.wait_ge(weights_in[5], 16)
            turn(7, 9, X)
            pe.wait_ge(xf_ready, 8 * NCH)
            for s, name in enumerate(("Wq3", "Wk3")):
                for c in range(NCH):
                    MM(ps[:, (3 + s * NCH + c) % 8, 0:CH], w(name), XF[:, c * CH:(c + 1) * CH], start=True, stop=True).then_inc(qk3_ready, 1)
            pe.wait_ge(qk3_used, NCH)
            for c in range(NCH):
                for j in range(BC):
                    at = (BC * c + j) * P
                    last = MM(ps[:, 3 + c, j * P:(j + 1) * P], XF[:, at:at + P], w("Wv3"), start=True, stop=True)
            last.then_inc(v3_ready, 1)
            pe.wait_ge(qk3_used, 2 * NCH)

            def scores3(u):
                i, b, base = u // 2, u % 2, 3 * (u % 2)
                rows = slice(b * D, (b + 1) * D)
                if u == 1:
                    pe.wait_ge(v3_used, NCH)
                if u >= 2:
                    pe.wait_ge(pt3_copied, turned_chunks(u - 1))
                L = (i + 1) * P
                for at in range(0, L, 512):
                    n = min(512, L - at)
                    last = MM(ps[:, base + at // 512, 0:n], SA[rows, 0, i * P:(i + 1) * P], SA[rows, 1, at:at + n], start=True, stop=True)
                last.then_inc(s3_ready, 1)

            def turn_probabilities(u):
                pe.wait_ge(p3_ready, u + 1)
                for cc in range(turned_chunks(u), turned_chunks(u + 1)):
                    c = cc - turned_chunks(u)
                    for j in range(4 * c, min(4 * c + 4, u // 2 + 1)):
                        last = nc.tensor.transpose(ps[:, 3 * (u % 2) + c, (j - 4 * c) * P:(j - 4 * c + 1) * P], PR[:, u % 2, j * P:(j + 1) * P], ident)
                    last.then_inc(pt3_ready, 1)

            def values3(u):
                i, b = u // 2, u % 2
                pe.wait_ge(pt3_copied, turned_chunks(u + 1))
                pe.wait_ge(v3_used, NCH)
                if u >= 2:
                    pe.wait_ge(o3_used, u - 1)
                for j in range(i + 1):
                    last = MM(ps[:, 6 + u % 2, 0:D], PT[:, u % 2, j, :], VT[:, j, b, :], start=j == 0, stop=j == i)
                last.then_inc(o3_ready, 1)

            scores3(0)
            for u in range(Q):
                if u + 1 < Q:
                    scores3(u + 1)
                turn_probabilities(u)
                if u:
                    values3(u - 1)
            values3(Q - 1)
            turn(8, 10, X)
            router(8, "Wg3")
            gates_turn(1)
            mlp(4, 8, 8, "e_W1", "e_W2", gated=True, bias="e_b2")


def host_layout(i):
    pack = np.zeros((P, WIDTH), np.float32)

    def put(name, value, rows=slice(0, P)):
        at, width = COLS[name]
        value = np.asarray(value)
        pack[rows, at:at + width] = value.reshape(value.shape[0], -1) if value.ndim > 1 else value

    def blocks(m):
        r, c = m.shape
        o = np.zeros((B, r, B, c), np.float32)
        for b in range(B):
            o[b, :, b, :] = m
        return o.reshape(B * r, B * c)

    def column(v):
        return np.concatenate([v] * B)[:, None]

    def twice(m):
        return np.concatenate([m] * B, axis=0)

    def tiles(m):
        return m.reshape(-1, P, m.shape[-1]).transpose(1, 0, 2).reshape(P, -1)

    put("ident", np.eye(P, dtype=np.float32))
    for n in "qkvo":
        put(f"tok_W{n}", blocks(i[f"L0_tok_W{n}"]))
    put("tok_bq", column(i["L0_tok_bq"])), put("tok_bk", column(i["L0_tok_bk"]))
    put("tok_bv", i["L0_tok_bv"]), put("tok_bo", i["L0_tok_bo"]), put("prelu", i["L0_tok_prelu_a"].reshape(1))

    Wx, bx = i["L0_attn_Wx"], i["L0_attn_bx"]
    WxT = Wx.T.reshape(2, P, D).transpose(1, 0, 2)
    put("WxT", np.concatenate([WxT, WxT], axis=2))
    heads = np.zeros((2, HEADS, DH, HEADS, KR), np.float32)
    mask = np.zeros((HEADS, DH, HEADS, KR), np.float32)
    for h in range(HEADS):
        heads[0, h, :, h, :] = i["L0_attn_Wq"]
        heads[1, h, :, h, :] = i["L0_attn_Wk"]
        mask[h, :, h, :] = 1.0
    put("WqBD", tiles(heads[0].reshape(256, HR)))
    k2 = heads[1].reshape(256, HR)
    put("WkBD", tiles(np.concatenate([k2, k2], axis=1)))
    put("headmask", tiles(mask.reshape(256, HR)))
    put("bxrep", np.broadcast_to(bx.reshape(2, P).T[:, :, None], (P, 2, P)))
    put("bxcol", bx.reshape(2, P).T)
    put("WxD", twice(Wx))
    wvt = np.zeros((4, DH, 4, DH), np.float32)
    for h in range(4):
        wvt[h, :, h, :] = i["L0_attn_Wv"].T
    put("WvT", wvt.reshape(P, P))
    put("Wo", tiles(i["L0_attn_Wo"]))
    put("a_bo", i["L0_attn_bo"])
    for n in ("ln1_g", "ln1_b", "ln2_g", "ln2_b"):
        put(n, column(i[f"L0_attn_{n}"]))

    def mlp(pre, w1, b1, w2, b2, upper):
        put(f"{pre}{upper[0]}1", twice(w1)), put(f"{pre}b1", b1.reshape(-1, P).T)
        put(f"{pre}{upper[0]}2", tiles(w2)), put(f"{pre}b2", b2)

    def other_half(m):
        return np.roll(m, m.shape[1] // 2, axis=1)

    def gated(pre, w1, b2):
        E, _, width = w1.shape
        own = w1.transpose(1, 0, 2).reshape(D, E * width)
        gates, out = np.zeros((D, E, width), np.float32), np.zeros((D, D), np.float32)
        for e in range(E):
            gates[e, e, :] = BIG
        out[E:2 * E] = b2
        gates, none = gates.reshape(D, -1), np.zeros((D, D), np.float32)
        put(pre + "W1", np.concatenate([np.concatenate([own, gates]), np.concatenate([gates, own])], axis=1))
        put(pre + "b2", np.concatenate([np.concatenate([none, out]), np.concatenate([out, none])], axis=1))

    mlp("a_", i["L0_attn_W1"], i["L0_attn_b1"], i["L0_attn_W2"], i["L0_attn_b2"], "W")
    put("wr", np.broadcast_to(column(i["L0_ffn_wr"][:, 0]), (P, P)))
    put("br", i["L0_ffn_br"])
    put("tri", np.tril(np.ones((P, P), np.float32), -1))
    mlp("f_", i["L0_ffn_w1"], i["L0_ffn_b1"], i["L0_ffn_w2"], i["L0_ffn_b2"], "w")

    put("WB", blocks(i["L1_attn_W_B"].T)), put("bB", column(i["L1_attn_b_B"])), put("a", column(i["L1_attn_a"]))
    put("WC", blocks(i["L1_attn_W_C"].T)), put("WD", blocks(i["L1_attn_W_D"].T))
    put("bC", i["L1_attn_b_C"]), put("bD", i["L1_attn_b_D"])
    put("rw", other_half(blocks(i["L1_ffn_router_w"].T))), put("rb", i["L1_ffn_router_b"])
    put("iota", np.arange(E1, dtype=np.float32))
    put("m_b1", i["L1_ffn_b1"].reshape(4, P).T)
    put("m_W2", tiles(i["L1_ffn_W2"].reshape(E1 * H1, D)))
    gated("m_", i["L1_ffn_W1"], i["L1_ffn_b2"])

    put("Bre", blocks(i["L2_attn_B_re"].T)), put("Bim", blocks(i["L2_attn_B_im"].T))
    put("nu", column(i["L2_attn_nu_log"])), put("theta", column(i["L2_attn_theta_log"]))
    put("Cre", blocks(i["L2_attn_C_re"].T)), put("Cim", blocks(i["L2_attn_C_im"].T))
    put("Dskip", i["L2_attn_D"])
    put("Wgat", blocks(i["L2_ffn_W_gat"]))
    put("att_src", i["L2_ffn_att_src"].reshape(-1)), put("att_dst", i["L2_ffn_att_dst"].reshape(-1))
    put("b_gat", i["L2_ffn_b_gat"]), put("g_gamma", i["L2_ffn_ln_gamma"]), put("g_beta", i["L2_ffn_ln_beta"])
    put("g_W1", twice(i["L2_ffn_W1"].transpose(1, 0, 2).reshape(D, -1)))
    put("g_b1", i["L2_ffn_b1"].T), put("g_W2", i["L2_ffn_W2"].transpose(1, 0, 2))
    put("g_b2", i["L2_ffn_b2"].reshape(-1))
    put("iota128", np.arange(P, dtype=np.float32))

    put("iota_p", np.arange(P, dtype=np.float32)[:, None])

    for n in "qkv":
        put(f"W{n}3", blocks(i[f"L3_attn_W{n}"].T))
    put("bq3", column(i["L3_attn_bq"])), put("bk3", column(i["L3_attn_bk"])), put("bv3", i["L3_attn_bv"])
    put("causal", np.triu(np.full((P, P), -BIG, np.float32), 1))
    gate = np.zeros((D, E1), np.float32)
    gate[:, :E3] = i["L3_ffn_Wg"]
    put("Wg3", other_half(blocks(gate))), put("bg3", i["L3_ffn_bg"])
    put("e_b1", i["L3_ffn_b1"].T), put("e_W2", i["L3_ffn_W2"].transpose(1, 0, 2))
    gated("e_", i["L3_ffn_W1"], i["L3_ffn_b2"])
    return pack


def kernel(**inputs):
    import concourse.bacc as bacc
    from concourse.bass_utils import run_bass_kernel_spmd

    i = {k: np.asarray(v) for k, v in inputs.items()}
    nc = bacc.Bacc("TRN2", target_bir_lowering=False, num_devices=1)
    arrays = {
        "xT": np.ascontiguousarray(i["x"].reshape(B, N_IMG, D).transpose(0, 2, 1).reshape(P, N_IMG)),
        "txt": np.ascontiguousarray(i["txt"]),
        "gammaT": np.ascontiguousarray(i["L0_tok_d_gamma_batched"].T),
        "edges": np.ascontiguousarray(i["L2_ffn_edge_index"].reshape(2, P, EC)),
        "weights": host_layout(i),
    }
    args = [nc.dram_tensor(n, a.shape, mybir.dt.from_np(a.dtype), kind="ExternalInput").ap() for n, a in arrays.items()]
    out = nc.dram_tensor("out", (B, N, D), F32, kind="ExternalOutput").ap()
    build(nc, *args, out)
    result = run_bass_kernel_spmd(nc, [arrays], core_ids=[0])
    return result.results[0]["out"]
```

```python
from contextlib import ExitStack

import numpy as np

import concourse.bass as bass
from concourse import mybir

P = 128
B, D = 2, 64
N_IMG, N_TXT = 1024, 128
N = N_IMG + N_TXT
KB = N // P
IB = N_IMG // P
Q = KB * B
CH = 384
NCH = N // CH
BC = CH // P
HEADS, DH, KR = 8, 32, 4
HR = HEADS * KR
EPS = 1e-5
ROOT_SEED = float(0x5F3759DF)
TOPK = int(0.5 * N) - 1
ACT_RANKS = (1, 7)
DT = 1.0 / N
E1, H1 = 32, 16
E2 = 4
E3 = 8
NODES = B * N
NT = NODES // P
FEAT = 20
EDGES = 262144
EC = EDGES // P
SCALE = float(D) ** -0.5
TWO_PI = 2.0 * float(np.pi)
TWO_PI_HI = 6.28125
TWO_PI_LO = TWO_PI - TWO_PI_HI
BIG = 1e30
HG = 24
NHI, NLO = 36, 64
SEG, SEG_TOP = 128, 24
SEGS = EC // SEG
CAND = SEGS * SEG_TOP
SLOTS = 64
PASSES = EC // SLOTS
PASS_STEPS = 17
GRP = 2

ALU = mybir.AluOpType
ACT = mybir.ActivationFunctionType
AX = mybir.AxisListType
F32 = mybir.dt.float32
BF16 = mybir.dt.bfloat16
I32 = mybir.dt.int32

GROUPS = [
    [("ident", P), ("tok_Wq", P), ("tok_Wk", P), ("tok_Wv", P), ("tok_Wo", P), ("tok_bq", 1), ("tok_bk", 1),
     ("tok_bv", D), ("tok_bo", D), ("prelu", 1)],
    [("WxT", 2 * P), ("WqBD", 2 * HR), ("WkBD", 4 * HR), ("bxrep", 2 * P), ("bxcol", 2), ("WxD", 2 * P),
     ("headmask", 2 * HR), ("WvT", P), ("Wo", 2 * D), ("a_bo", D), ("ln1_g", 1), ("ln1_b", 1), ("ln2_g", 1),
     ("ln2_b", 1), ("a_W1", B * 2 * P), ("a_b1", 2), ("a_W2", 2 * D), ("a_b2", D)],
    [("wr", P), ("br", 1), ("tri", P), ("f_w1", B * 2 * P), ("f_b1", 2), ("f_w2", 2 * D), ("f_b2", D)],
    [("WB", P), ("bB", 1), ("a", 1), ("WC", P), ("WD", P), ("bC", D), ("bD", D),
     ("rw", D), ("rb", E1), ("iota", E1), ("m_W1", B * 4 * P), ("m_b1", 4), ("m_W2", 4 * D), ("m_b2", P)],
    [("Bre", P), ("Bim", P), ("nu", 1), ("theta", 1), ("Cre", P), ("Cim", P), ("Dskip", D),
     ("Wgat", 32), ("att_src", 16), ("att_dst", 16), ("b_gat", 16), ("g_gamma", 16), ("g_beta", 16),
     ("g_W1", B * 4 * P), ("g_b1", 4), ("g_W2", 4 * D), ("g_b2", 4 * D), ("iota128", P), ("iota_p", 1)],
    [("Wq3", P), ("Wk3", P), ("Wv3", P), ("bq3", 1), ("bk3", 1), ("bv3", D), ("causal", P),
     ("Wg3", D), ("bg3", E3), ("e_W1", B * 8 * P), ("e_b1", 8), ("e_W2", 8 * D), ("e_b2", P)],
]
COLS, _at = {}, 0
GROUP_COLS = []
for _g in GROUPS:
    _from = _at
    for _name, _width in _g:
        COLS[_name] = (_at, _width)
        _at += _width
    GROUP_COLS.append((_from, _at))
WIDTH = _at


def build(nc, xT, txt, gammaT, edges, weights, out):
    ctx = ExitStack()
    with ctx:
        def sb(name, shape, dt=F32):
            return ctx.enter_context(nc.sbuf_tensor(name, shape, dt))

        def sem(name):
            return ctx.enter_context(nc.semaphore(name))

        ps = ctx.enter_context(nc.psum_tensor("ps", [P, 8, 512], F32))
        W_all = sb("weights_sb", [P, WIDTH])
        H = sb("H", [P, KB, B, D])
        X = sb("X", [P, KB, B, D])
        Z = sb("Z", [P, KB, B, D])
        XC = sb("XC", [P, KB, B, D])
        T1 = sb("T1", [P, KB, B, D])
        T2 = sb("T2", [P, KB, B, D])
        XF = sb("XF", [P, N])
        SA = sb("SA", [P, 2, N])
        VT = sb("VT", [P, KB, B, D])
        G = sb("G", [P, 2, E3, CH])
        gam = sb("gam", [P, IB, N_IMG])
        ring = sb("ring", [P, 4, 512])
        st = sb("st", [P, 16, Q])
        small = sb("small", [P, 64])
        KT = sb("KT", [P, KB, D])
        QS = sb("QS", [P, KB, D])
        LG = sb("LG", [P, KB, D])
        NF = sb("NF", [P, N])
        WQ = sb("WQ", [P, D])
        WK = sb("WK", [P, D])
        BQ = sb("BQ", [P, HR])
        BK = sb("BK", [D, 1])
        WVO = sb("WVO", [P, 2, D])
        UTs = sb("UTs", [P, HR])
        KX = sb("KX", [P, B, 2, HR])
        MB = sb("MB", [D, P])
        powers = sb("powers", [P, 8, 4, 2])
        coef = sb("coef", [P, 8])
        lam = sb("lam", [P, 12])
        lam_i = sb("lam_i", [P, 1], I32)
        bcd = sb("bcd", [P, D])
        iota64 = sb("iota64", [P, E1])
        PR = sb("PR", [P, 2, N])
        PT = sb("PT", [P, 2, KB, P])
        den3 = sb("den3", [P, 4, Q])
        held = sb("held", [1, 128])
        root_i = sb("root_i", [P, Q], I32)

        def w(name, rows=slice(0, P)):
            at, width = COLS[name]
            return W_all[rows, at:at + width]

        T2_flat = T2[:, :, :, :].rearrange("p k b d -> p (k b d)")
        XC_flat = XC[:, :, :, :].rearrange("p k b d -> p (k b d)")
        smaller = sb("smaller", [P, Q])
        junk = (ring[:, :, :].rearrange("p a b -> p (a b)"), T1[:, :, :, :].rearrange("p k b d -> p (k b d)"))
        WROW = SA
        own = (slice(0, D), slice(D, P))
        tok_k = (SA[:, 1, 0:N_IMG], T1[:, :, :, :].rearrange("p k b d -> p (k b d)")[:, 0:N_IMG])
        query3 = (NF, Z[:, :, :, :].rearrange("p k b d -> p (k b d)"))
        WBANK = ((3, 4, 5), (6, 7, 0))

        def flat(t):
            return t[:, :, :, :].rearrange("p k b d -> p (k b) d")

        def blk(t, k):
            return t[:, k, :, :].rearrange("p b d -> p (b d)")

        weights_in = [sem(f"weights_in_{i}") for i in range(len(GROUPS))]
        x_in, txt_in, out_stored = sem("x_in"), sem("txt_in"), sem("out_stored")
        gamma_in = [sem(f"gamma_in_{th}") for th in range(2)]
        dve_step, act_step, pool_step = sem("dve_step"), sem("act_step"), sem("pool_step")
        residual_ready = sem("residual_ready")

        norm_ready = sem("norm_ready")
        turned, xf_ready = sem("turned"), sem("xf_ready")
        h_ready = sem("h_ready")

        def hold(engine, semaphore, value, alone=False):
            engine.wait_ge(semaphore, value)
            if alone:
                nc.vector.memset(held[:, sites[0]:sites[0] + 1], 0.0)
                sites[0] += 1

        sites = [0]

        class Chain:

            def __init__(self, engine, semaphore):
                self.engine, self.semaphore, self.count = engine, semaphore, 0

            def __call__(self, instruction):
                self.count += 1
                instruction.then_inc(self.semaphore, 1)
                self.engine.wait_ge(self.semaphore, self.count)

        t13 = T1[:, :, :, :].rearrange("p (c j) b d -> p c (j b) d", c=NCH)

        words = gam[:, :, :].rearrange("p j t -> p (j t)")
        SAw = SA[:, :, :].rearrange("p a n -> p (a n)")
        PRw = PR[:, :, :].rearrange("p a n -> p (a n)")
        PTw = PT[:, :, :, :].rearrange("p a j n -> p (a j n)")
        Gw = G[:, :, :, :].rearrange("p a j n -> p (a j n)")
        e_src, e_dst = (Gw[:, i * EC:(i + 1) * EC].bitcast(I32) for i in range(2))
        e_last = Gw[:, 2 * EC:3 * EC]
        e_key = words[:, 2 * EC:3 * EC]
        e_flag = PRw[:, 0:EC]
        cand = PTw[:, 0:CAND]
        picked = words[:, 3 * EC:4 * EC]
        cand_i, cand_j = picked[:, 0:CAND].bitcast(I32), picked[:, CAND:2 * CAND].bitcast(I32)
        digit_hi = picked[:, 2 * CAND:2 * CAND + CAND // 2].bitcast(BF16)
        digit_lo = picked[:, 2 * CAND + CAND // 2:3 * CAND].bitcast(BF16)
        half = HG * (NHI + NLO) // 2
        homes = [words[:, 0:half], words[:, half:2 * half]]
        oh_hi = [h[:, 0:HG * NHI // 2].bitcast(BF16).rearrange("p (v t) -> p v t", t=HG) for h in homes]
        oh_lo = [h[:, HG * NHI // 2:half].bitcast(BF16).rearrange("p (v t) -> p v t", t=HG) for h in homes]
        digit_values = sb("digit_values", [P, NLO, HG], BF16)
        zeros = sb("zeros", [P, P])
        ident_b = sb("ident_b", [P, P], BF16)
        key = sb("key", [P, SLOTS])
        key_i = sb("key_i", [P, SLOTS], I32)
        field = sb("field", [P, 4, SLOTS], I32)
        lo_b = sb("lo_b", [P, 2, SLOTS], BF16)
        rest8 = sb("rest8", [P, 8])
        flag = sb("flag", [1, PASSES], I32)
        table = sb("table", [P, FEAT + E2, NT])
        parts = sb("parts", [P, 3, FEAT, NT], BF16)
        dst_score = table[:, FEAT:FEAT + E2, :]
        local_max = sb("local_max", [P, E2])
        score_max = sb("score_max", [P, E2])
        last_node = sb("last_node", [P, FEAT])
        n_last = sb("n_last", [P, NT])
        gate4 = sb("gate4", [P, Q, E2])
        pick4 = sb("pick4", [P, 3, Q, E2])
        e_val = SAw[:, 0:SLOTS * FEAT].rearrange("p (s f) -> p s f", f=FEAT)
        e_tmp = SAw[:, SLOTS * FEAT:SLOTS * (FEAT + 2 * E2)].rearrange("p (a s f) -> p a s f", a=2, f=E2)
        e_w = PRw[:, 0:SLOTS * FEAT].rearrange("p (s f) -> p s f", f=FEAT)
        node_w = PRw[:, SLOTS * FEAT:SLOTS * FEAT + 6 * E2 * NT].rearrange("p (a b h t) -> p a b h t", a=3, b=2, t=NT)
        src_hi_oh = PTw[:, 0:SLOTS * NT].rearrange("p (s t) -> p s t", t=NT)
        dst_hi_oh = PTw[:, SLOTS * NT:2 * SLOTS * NT].rearrange("p (s t) -> p s t", t=NT)
        GF = GRP * FEAT * NT
        product = [Gw[:, s * GF:(s + 1) * GF].rearrange("p (g f t) -> p g f t", g=GRP, t=NT) for s in range(2)]
        outer = [Gw[:, (2 + s) * GF:(3 + s) * GF].rearrange("p (g f t) -> p g f t", g=GRP, t=NT) for s in range(2)]
        dst_lo_oh = [Gw[:, 4 * GF + s * GRP * P:4 * GF + (s + 1) * GRP * P].rearrange("p (g n) -> p g n", g=GRP) for s in range(2)]
        distance = [ring[:, s, GRP * P:2 * GRP * P].bitcast(BF16) for s in range(2)]
        turned_oh = [ring[:, s, 0:GRP * P].bitcast(BF16) for s in range(2)]
        GN = SLOTS // GRP

        def turned_chunks(u):
            return sum((v // 2 + 4) // 4 for v in range(u))

        block = ctx.enter_context(nc.Block())

        (tok_proj, tok_proj_used, score_ready, decay_ready, kept_step, kept_copied, tok_y) = (
            sem("tok_proj"), sem("tok_proj_used"), sem("score_ready"), sem("decay_ready"), sem("kept_step"),
            sem("kept_copied"), sem("tok_y"))
        merged_ready, merged_used = sem("merged_ready"), sem("merged_used")
        (klog_ready, kshift_ready, kexp_ready, knorm_ready, kturned, kt_ready, ut_ready, uts_ready, kx_ready,
         kxs_ready, m_ready, mb_ready) = (sem(n) for n in (
            "klog_ready", "kshift_ready", "kexp_ready", "knorm_ready", "kturned", "kt_ready", "ut_ready", "uts_ready",
            "kx_ready", "kxs_ready", "m_ready", "mb_ready"))
        qlog_ready, qshift_ready, qexp_ready, qs_ready, qturned, qf_ready, attn_ready = (sem(n) for n in (
            "qlog_ready", "qshift_ready", "qexp_ready", "qs_ready", "qturned", "qf_ready", "attn_ready"))
        wrow_ready, wrow_copied, wcol_ready, wcol_used, ranks_ready = (sem(n) for n in (
            "wrow_ready", "wrow_copied", "wcol_ready", "wcol_used", "ranks_ready"))
        hid_ready = [sem(f"hid_ready_{m}") for m in range(5)]
        g_ready = [sem(f"g_ready_{m}") for m in range(5)]
        mlp_out = [sem(f"mlp_out_{m}") for m in range(5)]

        bu_ready, force_ready, scan_ready, y_ready, cd_ready, silu_ready = (sem(n) for n in (
            "bu_ready", "force_ready", "scan_ready", "y_ready", "cd_ready", "silu_ready"))
        coef_ready, lambda_ready = sem("coef_ready"), sem("lambda_ready")
        router_ready, gates_ready, gates_turned, gates_copied = (sem(n) for n in (
            "router_ready", "gates_ready", "gates_turned", "gates_copied"))
        qk3_ready, qk3_used, v3_ready, v3_used, s3_ready, shift3_ready, p3_ready, pt3_ready, pt3_copied, o3_ready, o3_used = (
            sem(n) for n in ("qk3_ready", "qk3_used", "v3_ready", "v3_used", "s3_ready", "shift3_ready", "p3_ready",
                             "pt3_ready", "pt3_copied", "o3_ready", "o3_used"))

        edges_in, picked_out, inside_ready, keys_ready, onehots_ready, counted, counts_used = (sem(n) for n in (
            "edges_in", "picked_out", "inside_ready", "keys_ready", "onehots_ready", "counted", "counts_used"))
        gat_ready, local_max_ready, score_max_ready, last_ready = (sem(n) for n in (
            "gat_ready", "local_max_ready", "score_max_ready", "last_ready"))
        (taken, fields_ready, rest_ready, rest_turned, flag_ready, spread_ready, low_read, oht_ready, gathered, product_step,
         selected, edge_shift_ready, edge_exp_ready, zeros_ready, parts_ready, outer_ready, terms_ready, pool_outer,
         scattered, edge_step) = (sem(n) for n in (
            "taken", "fields_ready", "rest_ready", "rest_turned", "flag_ready", "spread_ready", "low_read", "oht_ready",
            "gathered", "product_step", "selected", "edge_shift_ready", "edge_exp_ready", "zeros_ready", "parts_ready",
            "outer_ready", "terms_ready", "pool_outer", "scattered", "edge_step"))
        sums_read = sem("sums_read")
        node_shift_ready, node_exp_ready, gate_shift_ready, gate_exp_ready, gated = (sem(n) for n in (
            "node_shift_ready", "node_exp_ready", "gate_shift_ready", "gate_exp_ready", "gated"))

        @block.sync
        def _(sp):
            sp.dma_start(W_all[:, slice(*GROUP_COLS[0])], weights[:, slice(*GROUP_COLS[0])]).then_inc(weights_in[0], 16)
            sp.dma_start(XF[:, 0:N_IMG], xT).then_inc(x_in, 16)
            gview = gammaT.rearrange("(j p) t -> p j t", p=P)
            for th in range(2):
                sp.dma_start(gam[:, :, th * 512:(th + 1) * 512], gview[:, :, th * 512:(th + 1) * 512]).then_inc(gamma_in[th], 16)
                if th == 0:
                    for i, dst in enumerate((e_src, e_dst)):
                        sp.dma_start(dst, edges[i]).then_inc(edges_in, 16)
            sp.dma_start(H[:, IB, :, :], txt.rearrange("b p d -> p b d")).then_inc(txt_in, 16)
            for i in range(1, len(GROUPS)):
                sp.dma_start(W_all[:, slice(*GROUP_COLS[i])], weights[:, slice(*GROUP_COLS[i])]).then_inc(weights_in[i], 16)
            for c in range(NCH):
                sp.wait_ge(h_ready, c + 1)
                for b in range(B):
                    sp.dma_start(out[b, c * CH:(c + 1) * CH].rearrange("(k p) d -> p k d", p=P), H[:, BC * c:BC * (c + 1), b, :]).then_inc(out_stored, 16)
            sp.wait_ge(out_stored, 16 * B * NCH)

        @block.gpsimd
        def _(pool):
            nc.gpsimd.memset(zeros[:, :], 0.0).then_inc(zeros_ready, 1)
            for b in range(B):
                pool.wait_ge(zeros_ready, b + 1)
                nc.gpsimd.memset(tok_k[b][own[1 - b], :], 0.0).then_inc(zeros_ready, 1)
            def flat(t):
                return t[:, :, :, :].rearrange("p k b d -> p (k b) d")

            def row(ap):
                return ap.unsqueeze(1).broadcast_to([P, Q, D])

            def residual(n, x, y, op=ALU.add, also=False):
                pool.wait_ge(norm_ready, NCH * (n + 1))
                if also:
                    nc.gpsimd.tensor_tensor(flat(T1), x, y, op).then_inc(pool_step, 1)
                    pool_steps[0] += 1
                    pool.wait_ge(pool_step, pool_steps[0])
                    x, y = flat(H), flat(T1)
                nc.gpsimd.tensor_tensor(flat(H), x, y, ALU.add).then_inc(residual_ready, 1)

            pool_steps = [0]
            pool.wait_ge(norm_ready, NCH * 2)
            nc.gpsimd.tensor_tensor(flat(T1), flat(X), row(w("a_bo")), ALU.add).then_inc(residual_ready, 1)
            pool.wait_ge(inside_ready, 1)
            pool.wait_ge(picked_out, 2 * SEGS * (SEG_TOP // 8))
            for other, op in ((e_flag, ALU.mult), (e_flag, ALU.add)):
                nc.gpsimd.tensor_tensor(e_key, e_key, other, op).then_inc(pool_step, 1)
                pool_steps[0] += 1
                pool.wait_ge(pool_step, pool_steps[0])
            nc.gpsimd.tensor_tensor(e_key, e_key, e_last, ALU.add).then_inc(keys_ready, 1)
            residual(2, flat(T2), row(w("a_b2")), also=True)
            residual(3, flat(H), flat(X))
            residual(4, flat(H), flat(X))
            residual(6, flat(X), row(w("Dskip")), ALU.mult, also=True)
            pool.wait_ge(local_max_ready, 1)
            nc.gpsimd.partition_all_reduce(score_max[:, :], local_max[:, :], P, bass.bass_isa.ReduceOp.max).then_inc(score_max_ready, 1)
            pool.wait_ge(score_max_ready, 1)
            pool.wait_ge(terms_ready, 1)

            def spread_out(g, first=False):
                if not first:
                    pool.wait_ge(scattered, g + (-1))
                at = bass.ts(g, GRP)
                nc.gpsimd.tensor_tensor(outer[0], e_w[:, at, :].unsqueeze(3).broadcast_to([P, GRP, FEAT, NT]),
                                        dst_hi_oh[:, at, :].unsqueeze(2).broadcast_to([P, GRP, FEAT, NT]), ALU.mult).then_inc(pool_outer, 1)

            spread_out(0, first=True)
            with pool.Fori(1, GN // 2) as r:
                spread_out(2 * r)
            pool.wait_ge(pool_outer, GN // 2)
            pool.wait_ge(gate_shift_ready, 1)
            for b in range(B):
                pool.wait_ge(zeros_ready, b + 3)
                nc.gpsimd.memset(query3[b][own[1 - b], 0:N], 0.0).then_inc(zeros_ready, 1)

        @block.scalar
        def _(act):
            step = Chain(act, act_step)

            def input_to_channels(t, scale=None, bias=None):
                for c in range(NCH):
                    act.wait_ge(turned, NCH * t + c + 1)
                    dst, src = XF[:, c * CH:(c + 1) * CH], ps[:, c, 0:CH]
                    if scale is None:
                        nc.scalar.activation(dst, src, ACT.Copy).then_inc(xf_ready, 1)
                    else:
                        nc.scalar.activation(dst, src, ACT.Identity, bias=bias, scale=scale).then_inc(xf_ready, 1)

            def mlp(m, J, func, bias, steps=range(2 * NCH)):
                for s in steps:
                    for j in range(J):
                        n = s * J + j
                        act.wait_ge(hid_ready[m], n + 1)
                        if s >= 2 and j == 0:
                            act.wait_ge(mlp_out[m], (s - 1) * (BC if m == 3 else 1))
                        nc.scalar.activation(G[:, s % 2, j, :], ps[:, 3 + n % 5, 0:CH], func,
                                             bias=bias[:, j:j + 1]).then_inc(g_ready[m], 1)

            act.wait_ge(weights_in[0], 16)
            act.wait_ge(tok_proj, 1)
            for th in range(2):
                at = slice(th * 512, (th + 1) * 512)
                nc.scalar.activation(SA[:, 0, at], ps[:, th, :], ACT.Identity, bias=w("tok_bq"), scale=1.0).then_inc(tok_proj_used, 1)
            for th in range(2):
                at = slice(th * 512, (th + 1) * 512)
                for b in range(B):
                    nc.scalar.activation(tok_k[b][own[b], at], ps[own[b], 2 + th, :], ACT.Identity,
                                         bias=w("tok_bk", own[b]), scale=1.0).then_inc(tok_proj_used, 1)
            for th in range(2):
                act.wait_ge(kept_step, 16 * (th + 1))
                nc.scalar.activation(T2_flat[:, th * 512:(th + 1) * 512], ps[:, 6 + th, :], ACT.Copy).then_inc(kept_copied, 1)

            act.wait_ge(weights_in[1], 16)
            input_to_channels(0, w("ln1_g"), w("ln1_b"))
            act.wait_ge(kshift_ready, 1)
            nc.scalar.activation(NF[0:D, :].rearrange("p (c n) -> p c n", c=NCH), ps[0:D, 0:NCH, 0:CH], ACT.Exp,
                                 bias=small[0:D, 4:5], accum_out=small[0:D, 5:6]).then_inc(kexp_ready, 1)
            act.wait_ge(qshift_ready, 1)
            nc.scalar.activation(QS[:, :, :], LG[:, :, :], ACT.Exp).then_inc(qexp_ready, 1)
            act.wait_ge(weights_in[4], 16)
            step(nc.scalar.activation(lam[:, 0:1], w("nu"), ACT.Exp))
            step(nc.scalar.activation(lam[:, 1:2], lam[:, 0:1], ACT.Exp, scale=-1.0))
            nc.scalar.activation(lam[:, 2:3], w("theta"), ACT.Exp).then_inc(lambda_ready, 1)
            act.wait_ge(coef_ready, 1)
            nc.scalar.activation(lam[:, 5:6], lam[:, 3:4], ACT.Sin).then_inc(lambda_ready, 1)
            nc.scalar.activation(lam[:, 6:7], lam[:, 4:5], ACT.Sin).then_inc(lambda_ready, 1)
            for c in range(NCH):
                act.wait_ge(qturned, c + 1)
                nc.scalar.activation(NF[0:D, c * CH:(c + 1) * CH], ps[0:D, 3 + c, 0:CH], ACT.Copy).then_inc(qf_ready, 1)
            input_to_channels(1, w("ln2_g"), w("ln2_b"))
            mlp(0, 2, ACT.Gelu, w("a_b1"))

            act.wait_ge(weights_in[2], 16)
            input_to_channels(2)
            for b in range(B):
                act.wait_ge(wrow_ready, b + 1)
                for c in range(NCH):
                    nc.scalar.activation(WROW[:, b, c * CH:(c + 1) * CH], ps[:, WBANK[b][c], 0:CH], ACT.Identity,
                                         bias=w("br"), scale=1.0).then_inc(wrow_copied, 1)
            mlp(1, 2, ACT.Gelu_apprx_tanh, w("f_b1"))
            act.wait_ge(wcol_used, 1)
            ranked = 0
            for k in ACT_RANKS:
                for b in range(B):
                    q = 2 * k + b
                    if ranked:
                        act.wait_ge(ranks_ready, 2 * ranked)
                    ranked += 1
                    step(nc.scalar.activation(XC_flat, WROW[:, b, :], ACT.Sign, bias=st[:, 5, q:q + 1], scale=-1.0))
                    nc.scalar.activation(T2_flat[:, 0:k * P], XC_flat[:, 0:k * P], ACT.Relu,
                                         accum_out=smaller[:, q:q + 1]).then_inc(ranks_ready, 1)
                    nc.scalar.activation(T2_flat[:, k * P:N], XC_flat[:, k * P:N], ACT.Relu, scale=-1.0,
                                         accum_out=st[:, 7, q:q + 1]).then_inc(ranks_ready, 1)

            def input_beside_gates():
                for c in range(NCH):
                    nc.scalar.activation(NF[D:P, c * CH:(c + 1) * CH], ps[D:P, c, 0:CH], ACT.Copy).then_inc(gates_copied, 1)

            def gates_to_channels():
                for c in range(NCH):
                    act.wait_ge(gates_turned, gates[0] * NCH + c + 1)
                    for x, rows in ((XF, slice(D, P)), (NF, slice(0, D))):
                        nc.scalar.activation(x[rows, c * CH:(c + 1) * CH], ps[rows, 3 + c, 0:CH], ACT.Copy).then_inc(gates_copied, 1)
                gates[0] += 1

            gates = [0]
            input_to_channels(3)
            act.wait_ge(coef_ready, 2)
            for c in range(NCH):
                act.wait_ge(bu_ready, c + 1)
                for s in range(2):
                    nc.scalar.activation(SA[:, s, c * CH:(c + 1) * CH], ps[:, 3 + c, 0:CH], ACT.Identity,
                                         bias=coef[:, 4 + s:5 + s], scale=coef[:, 2 + s:3 + s]).then_inc(force_ready, 1)
            for c in range(NCH):
                act.wait_ge(cd_ready, c + 1)
                q = slice(2 * BC * c, 2 * BC * (c + 1))
                step(nc.scalar.activation(flat(Z)[:, q], flat(T1)[:, q], ACT.Gelu))
            for c in range(NCH):
                q = slice(2 * BC * c, 2 * BC * (c + 1))
                nc.scalar.activation(flat(T2)[:, q], flat(Z)[:, q], ACT.Sigmoid).then_inc(silu_ready, 1)
            input_to_channels(4)
            input_beside_gates()
            gates_to_channels()
            mlp(2, 4, ACT.Relu, w("m_b1"))
            act.wait_ge(coef_ready, 3)
            step(nc.scalar.activation(lam[:, 8:9], lam[:, 7:8], ACT.Sqrt))
            input_to_channels(5)
            for s in range(2):
                for c in range(NCH):
                    act.wait_ge(bu_ready, NCH + s * NCH + c + 1)
                    nc.scalar.activation(SA[:, s, c * CH:(c + 1) * CH], ps[:, (3 + s * NCH + c) % 8, 0:CH], ACT.Copy,
                                         scale=lam[:, 8:9]).then_inc(force_ready, 1)

            input_to_channels(6)

            def edge_pass(it):
                def turned_onehots(g, s, first=False):
                    act.wait_ge(spread_ready, it * GN + g + 1)
                    nc.scalar.activation(distance[s], ps[:, 5 + s, :], ACT.Abs, bias=w("iota_p"), scale=-1.0).then_inc(low_read, 1)
                    act.wait_ge(low_read, it * GN + g + 1)
                    if not first:
                        act.wait_ge(gathered, it * GN + g - 1)
                    nc.scalar.activation(turned_oh[s], distance[s], ACT.Relu, bias=1.0, scale=-1.0).then_inc(oht_ready, 1)

                for s in range(2):
                    turned_onehots(s, s, first=isinstance(it, int))
                with act.Fori(1, GN // 2) as r:
                    for s in range(2):
                        turned_onehots(2 * r + s, s)
                act.wait_ge(edge_shift_ready, it + 1)
                nc.scalar.activation(e_w[:, :, 0:E2], e_tmp[:, 0, :, :], ACT.Exp).then_inc(edge_exp_ready, 1)

            edge_pass(0)
            act.wait_ge(flag_ready, 1)
            more = act.value_load(flag[0:1, 0:1], min_val=0, max_val=1)
            with act.If(more > 0):
                with act.Fori(1, PASSES) as it:
                    more = act.value_load(flag[0:1, bass.ds(it - 1, 1)], min_val=0, max_val=1)
                    with act.If(more > 0):
                        edge_pass(it)
            act.wait_ge(node_shift_ready, 1)
            nc.scalar.activation(node_w[:, 0, :, :, :], node_w[:, 1, :, :, :], ACT.Exp).then_inc(node_exp_ready, 1)
            mlp(3, 4, ACT.Gelu, w("g_b1"), range(2))
            nc.scalar.activation(smaller[:, 0:1], zeros[:, 0:1], ACT.Exp)
            act.wait_ge(gate_shift_ready, 1)
            nc.scalar.activation(st[:, 12, :], st[:, 13, :], ACT.Exp).then_inc(gate_exp_ready, 1)
            mlp(3, 4, ACT.Gelu, w("g_b1"), range(2, 2 * NCH))
            act.wait_ge(weights_in[5], 16)
            input_to_channels(7)
            for c in range(NCH):
                act.wait_ge(qk3_ready, c + 1)
                for b in range(B):
                    nc.scalar.activation(query3[b][own[b], c * CH:(c + 1) * CH], ps[own[b], 3 + c, 0:CH], ACT.Identity,
                                         bias=w("bq3", own[b]), scale=1.0).then_inc(qk3_used, 1)
            for c in range(NCH):
                act.wait_ge(qk3_ready, NCH + c + 1)
                nc.scalar.activation(SA[:, 1, c * CH:(c + 1) * CH], ps[:, (3 + NCH + c) % 8, 0:CH], ACT.Identity,
                                     bias=w("bk3"), scale=1.0).then_inc(qk3_used, 1)

            def expo(u):
                L = (u // 2 + 1) * P
                act.wait_ge(shift3_ready, u + 1)
                if u >= 2:
                    act.wait_ge(pt3_ready, turned_chunks(u - 1))
                nc.scalar.activation(PR[:, u % 2, 0:L], ps[:, 3 * (u % 2):3 * (u % 2) + 3, :].rearrange("p c n -> p (c n)")[:, 0:L],
                                     ACT.Exp, bias=den3[:, 1, u:u + 1], scale=SCALE, accum_out=den3[:, 2, u:u + 1]).then_inc(p3_ready, 1)

            def copies(u):
                if u >= 2:
                    act.wait_ge(o3_ready, u - 1)
                for cc in range(turned_chunks(u), turned_chunks(u + 1)):
                    act.wait_ge(pt3_ready, cc + 1)
                    c = cc - turned_chunks(u)
                    j, m = 4 * c, min(4, u // 2 + 1 - 4 * c)
                    nc.scalar.activation(PT[:, u % 2, j:j + m, :], ps[:, 3 * (u % 2) + c, 0:m * P].rearrange("p (j n) -> p j n", n=P),
                                         ACT.Copy).then_inc(pt3_copied, 1)

            expo(0)
            for u in range(Q):
                copies(u)
                if u + 1 < Q:
                    expo(u + 1)
            input_to_channels(8)
            input_beside_gates()
            gates_to_channels()
            mlp(4, 8, ACT.Gelu, w("e_b1"))

        @block.vector
        def _(dve):
            link = Chain(dve, dve_step)
            V = nc.vector

            def bc(ap, n):
                return ap.unsqueeze(ap.ndim).broadcast_to(list(ap.shape) + [n])

            def row(ap, n=Q):
                return ap.unsqueeze(1).broadcast_to([ap.shape[0], n, ap.shape[1]])

            def layernorm(src, dst, n, width=D, centred=None, squares=None, arrive=None):
                centred = flat(XC) if centred is None else centred
                squares = flat(T1) if squares is None else squares
                for c in range(NCH if arrive else 1):
                    q = slice(2 * BC * c, 2 * BC * (c + 1)) if arrive else slice(0, Q)
                    if arrive:
                        arrive(c)
                    link(V.reduce_sum(st[:, 0, q], src[:, q], AX.X))
                    link(V.scalar_tensor_tensor(centred[:, q], bc(st[:, 0, q], width), -1.0 / width, src[:, q], ALU.mult, ALU.add))
                    link(V.tensor_tensor(squares[:, q], centred[:, q], centred[:, q], ALU.mult))
                    link(V.reduce_sum(st[:, 4, q], squares[:, q], AX.X))
                link(V.tensor_scalar(st[:, 2, :], st[:, 4, :], 1.0 / width, EPS, ALU.mult, ALU.add))
                link(V.tensor_scalar(root_i[:, :], st[:, 2, :].bitcast(I32), 1, None, ALU.logical_shift_right))
                V.tensor_scalar(st[:, 1, :], st[:, 2, :], -0.5, None, ALU.mult).then_inc(dve_step, 1)
                link.count += 1
                link(V.tensor_scalar(st[:, 3, :].bitcast(I32), root_i[:, :], -1.0, ROOT_SEED, ALU.mult, ALU.add))
                for _ in range(3):
                    link(V.tensor_tensor(st[:, 0, :], st[:, 3, :], st[:, 3, :], ALU.mult))
                    link(V.tensor_tensor(st[:, 0, :], st[:, 0, :], st[:, 1, :], ALU.mult))
                    link(V.scalar_tensor_tensor(st[:, 3, :], st[:, 0, :], 1.5, st[:, 3, :], ALU.add, ALU.mult))
                for c in range(NCH):
                    q = slice(2 * BC * c, 2 * BC * (c + 1))
                    V.tensor_tensor(dst[:, q], centred[:, q], bc(st[:, 3, q], width), ALU.mult).then_inc(norm_ready, 1)
                dve.wait_ge(norm_ready, NCH * (n + 1))

            def chunk(t, c):
                return t[:, BC * c:BC * (c + 1), :, :].rearrange("p j b d -> p (j b d)")

            def out_psum():
                return ps[:, 0:NCH, 0:CH]

            def powers_of(levels=7):
                for l in range(levels):
                    now, then = powers[:, l], powers[:, l + 1]
                    V.tensor_tensor(now[:, 3, :], now[:, 1, :], now[:, 2, :], ALU.mult).then_inc(dve_step, 1)
                    V.tensor_tensor(then[:, 0, :], now[:, 0, :], now[:, 0, :], ALU.mult).then_inc(dve_step, 1)
                    V.scalar_tensor_tensor(then[:, 1:3, :], now[:, 1:3, :], 2.0, now[:, 0, :].unsqueeze(1).broadcast_to([P, 2, 2]),
                                           ALU.mult, ALU.mult).then_inc(dve_step, 1)
                    link.count += 3
                    dve.wait_ge(dve_step, link.count)
                    link(V.tensor_tensor(then[:, 0, :], then[:, 0, :], now[:, 3, :], ALU.add))

            final = float(NODES - 1)

            def last_keys(i):
                if i == 0:
                    dve.wait_ge(edges_in, 32)
                    link(V.tensor_scalar(e_flag, e_src, final, None, ALU.is_ge))
                elif i == 1:
                    link(V.scalar_tensor_tensor(e_flag, e_dst, float(NODES), e_flag, ALU.is_lt, ALU.mult))
                elif i == 2:
                    link(V.tensor_scalar(e_last, e_dst, 4096.0, final + 1.0, ALU.mult, ALU.add))
                else:
                    link(V.tensor_tensor(e_last, e_last, e_flag, ALU.mult))

            def pick_last(j, replace, first):
                for k in range(first, first + 4):
                    segment = e_last[:, k * SEG:(k + 1) * SEG]
                    top = cand[:, k * SEG_TOP + 8 * j:k * SEG_TOP + 8 * j + 8]
                    if replace:
                        dve.wait_ge(picked_out, 2 * SEGS * j + k + 1)
                        V.match_replace(segment, top, segment, 0.0).then_inc(picked_out, 1)
                    else:
                        if j:
                            dve.wait_ge(picked_out, 2 * SEGS * (j - 1) + SEGS + k + 1)
                        V.max(top, segment).then_inc(picked_out, 1)

            def inside_keys():
                link(V.tensor_scalar(e_flag, e_src, final, None, ALU.is_lt))
                link(V.scalar_tensor_tensor(e_flag, e_dst, float(NODES), e_flag, ALU.is_lt, ALU.mult))
                V.scalar_tensor_tensor(e_key, e_dst, 4096.0, e_src, ALU.mult, ALU.add).then_inc(inside_ready, 1)

            def edge_digits():
                link(V.tensor_scalar(cand_i, cand, -1.0, None, ALU.add))
                link(V.tensor_scalar(cand_j, cand_i, 12, NLO - 1, ALU.logical_shift_right, ALU.bitwise_and))
                link(V.tensor_scalar(cand_i, cand_i, 18, None, ALU.arith_shift_right))
                link(V.tensor_copy(digit_hi, cand_i))
                link(V.tensor_copy(digit_lo, cand_j))
                dve.wait_ge(weights_in[4], 16)
                link(V.tensor_copy(ident_b[:, :], w("ident")))
                link(V.tensor_copy(digit_values[:, :, :], bc(w("iota128")[:, 0:NLO], HG)))

            steps = [0]

            def linked(it, instruction):
                steps[0] += 1
                instruction.then_inc(edge_step, 1)
                hold(dve, edge_step, it * PASS_STEPS + steps[0], not isinstance(it, int))

            def take_edges(it, first, end):
                reg = not isinstance(it, int)
                for j in range(first, end):
                    V.max(key[:, 8 * j:8 * j + 8], e_key).then_inc(taken, 1)
                    hold(dve, taken, it * (2 * (SLOTS // 8)) + (2 * j + 1), reg)
                    V.match_replace(e_key, key[:, 8 * j:8 * j + 8], e_key, 0.0).then_inc(taken, 1)
                    hold(dve, taken, it * (2 * (SLOTS // 8)) + (2 * j + 2), reg)

            def edge_fields(it):
                reg = not isinstance(it, int)
                steps[0] = 0
                linked(it, V.max(rest8[:, :], e_key))
                V.tensor_copy(rest8[:, 1:2], rest8[:, 0:1]).then_inc(rest_ready, 1)
                linked(it, V.tensor_scalar(key_i[:, :], key[:, :], -1.0, None, ALU.add))
                linked(it, V.tensor_scalar(field[:, 0, :], key_i[:, :], P - 1, None, ALU.bitwise_and))
                linked(it, V.tensor_scalar(field[:, 1, :], key_i[:, :], 7, 31, ALU.logical_shift_right, ALU.bitwise_and))
                linked(it, V.tensor_scalar(field[:, 2, :], key_i[:, :], 12, P - 1, ALU.logical_shift_right, ALU.bitwise_and))
                linked(it, V.tensor_scalar(field[:, 3, :], key_i[:, :], 19, None, ALU.arith_shift_right))
                for i in range(2):
                    V.tensor_copy(lo_b[:, i, :], field[:, 2 * i, :]).then_inc(fields_ready, 1)
                linked(it, V.tensor_tensor(src_hi_oh, bc(field[:, 1, :], NT), row(w("iota128")[:, 0:NT], SLOTS), ALU.is_equal))
                linked(it, V.tensor_tensor(dst_hi_oh, bc(field[:, 3, :], NT), row(w("iota128")[:, 0:NT], SLOTS), ALU.is_equal))

            dve.wait_ge(weights_in[0], 16)
            dve.wait_ge(tok_proj, 2)
            for i in range(2):
                V.tensor_tensor(VT[:, 4 * i:4 * i + 4, :, :].rearrange("p k b d -> p (k b) d"),
                                ps[:, 4 + i, :].rearrange("p (q d) -> p q d", d=D), row(w("tok_bv"), 8),
                                ALU.add).then_inc(tok_proj_used, 1)
            for th in range(2):
                dve.wait_ge(gamma_in[th], 16)
                for u in range(16 * th, 16 * th + 16):
                    dve.wait_ge(score_ready, u + 1)
                    if u >= 4:
                        dve.wait_ge(kept_step, u - 3)
                    V.tensor_tensor(ring[:, u % 4, :], ps[:, u % 4, :],
                                    gam[:, u % IB, th * 512:(th + 1) * 512], ALU.mult).then_inc(decay_ready, 1)
                    if 4 <= u < 8:
                        last_keys(u - 4)
                    elif u >= 8:
                        round_, part = (u - 8) // 8, (u - 8) % 8
                        pick_last(round_, part >= 4, 4 * (part % 4))
            for i in range(2):
                dve.wait_ge(tok_y, i + 1)
                y = flat(T1)[:, 0:8, :]
                link(V.tensor_tensor(y, ps[:, i, :].rearrange("p (q d) -> p q d", d=D), row(w("tok_bo"), 8), ALU.add))
                neg = flat(XC)[:, 0:8, :]
                link(V.tensor_scalar(neg, y, 0.0, w("prelu"), ALU.min, ALU.mult))
                link(V.scalar_tensor_tensor(flat(H)[:, 8 * i:8 * i + 8, :], y, 0.0, neg, ALU.max, ALU.add))
            dve.wait_ge(txt_in, 16)

            dve.wait_ge(weights_in[1], 16)
            dve.wait_ge(merged_ready, 1)
            V.memset(WQ[:, :], 0.0).then_inc(dve_step, 1)
            V.memset(WK[:, :], 0.0).then_inc(dve_step, 1)
            link.count += 2
            link(V.memset(MB[:, :], 0.0))
            for b in range(B):
                rows = slice(b * D, (b + 1) * D)
                V.tensor_copy(WQ[rows, b * HR:(b + 1) * HR], ps[rows, 5, 0:HR]).then_inc(merged_used, 1)
                V.tensor_copy(WK[rows, b * HR:(b + 1) * HR], ps[rows, 5, HR:2 * HR]).then_inc(merged_used, 1)
            V.tensor_copy(BQ[:, :], ps[:, 5, 64:96]).then_inc(merged_used, 1)
            V.tensor_copy(BK[:, :], ps[0:D, 5, 96:97]).then_inc(merged_used, 1)
            V.tensor_copy(WVO[:, :, :], ps[:, 5, 128:256].rearrange("p (t d) -> p t d", t=2)).then_inc(merged_used, 1)
            layernorm(flat(H), flat(X), 0)
            layernorm(flat(X), flat(Z), 1)
            inside_keys()
            dve.wait_ge(klog_ready, 1)
            dve.wait_ge(merged_used, 7)
            link(V.tensor_reduce(small[0:D, 0:1], ps[0:D, 0:NCH, 0:CH], AX.XY, ALU.max))
            link(V.tensor_tensor(small[0:D, 1:2], small[0:D, 0:1], BK[:, :], ALU.add))
            V.tensor_tensor(small[0:D, 4:5], BK[:, :], small[0:D, 1:2], ALU.subtract).then_inc(kshift_ready, 1)
            dve.wait_ge(kexp_ready, 1)
            link(V.reciprocal(small[0:D, 6:7], small[0:D, 5:6]))
            V.tensor_scalar(NF[0:D, :], NF[0:D, :], small[0:D, 6:7], None, ALU.mult).then_inc(knorm_ready, 1)
            dve.wait_ge(qlog_ready, 1)
            lq = LG[:, :, :].rearrange("p (c j) (b r) -> p c (j b) r", c=NCH, b=B)
            bq = BQ[:, :].unsqueeze(1).broadcast_to([P, BC * B, HR])
            for c in range(NCH):
                V.tensor_tensor(lq[:, c], ps[:, 3 + c, 0:BC * D].rearrange("p (q r) -> p q r", r=HR), bq,
                                ALU.add).then_inc(dve_step, 1)
                link.count += 1
            dve.wait_ge(dve_step, link.count)
            l4 = LG[:, :, :].rearrange("p k (g r) -> p (k g) r", r=KR)
            q4 = QS[:, :, :].rearrange("p k (g r) -> p (k g) r", r=KR)
            gsum = T2_flat[:, 0:KB * 16]
            link(V.tensor_reduce(gsum, l4, AX.X, ALU.max))
            V.tensor_tensor(l4, l4, bc(gsum, KR), ALU.subtract).then_inc(qshift_ready, 1)
            dve.wait_ge(kturned, 1)
            V.tensor_copy(KT[:, :, :].rearrange("p (c j) r -> p c (j r)", c=NCH), ps[:, 0:NCH, 0:BC * D]).then_inc(kt_ready, 1)
            dve.wait_ge(qexp_ready, 1)
            link(V.reduce_sum(gsum, q4, AX.X))
            grec = T2_flat[:, 256:256 + KB * 16]
            link(V.reciprocal(grec, gsum))
            V.tensor_tensor(q4, q4, bc(grec, KR), ALU.mult).then_inc(qs_ready, 1)
            dve.wait_ge(lambda_ready, 1)
            link(V.tensor_scalar(lam_i[:, :], lam[:, 2:3], 1.0 / TWO_PI, None, ALU.mult))
            link(V.tensor_copy(lam[:, 9:10], lam_i[:, :]))
            link(V.scalar_tensor_tensor(lam[:, 3:4], lam[:, 9:10], -TWO_PI_HI, lam[:, 2:3], ALU.mult, ALU.add))
            link(V.scalar_tensor_tensor(lam[:, 3:4], lam[:, 9:10], -TWO_PI_LO, lam[:, 3:4], ALU.mult, ALU.add))
            link(V.tensor_scalar(lam[:, 3:4], lam[:, 3:4], 3.1415925, -3.1415925, ALU.min, ALU.max))
            link(V.scalar_tensor_tensor(lam[:, 4:5], lam[:, 3:4], -1.0, lam[:, 3:4], ALU.mult, ALU.max))
            V.tensor_scalar(lam[:, 4:5], lam[:, 4:5], -1.0, TWO_PI / 4, ALU.mult, ALU.add).then_inc(coef_ready, 1)
            dve.wait_ge(ut_ready, 1)
            for b in range(B):
                rows = slice(b * D, (b + 1) * D)
                V.tensor_scalar(UTs[rows, :], ps[rows, 6, b * HR:(b + 1) * HR], w("ln1_g", rows), w("ln1_b", rows),
                                ALU.mult, ALU.add).then_inc(uts_ready, 1)
            dve.wait_ge(kx_ready, 1)
            for b in range(B):
                for t in range(2):
                    V.scalar_tensor_tensor(KX[:, b, t, :], ps[:, 7 * b, t * HR:(t + 1) * HR],
                                           w("bxcol")[:, t:t + 1], w("headmask")[:, t * HR:(t + 1) * HR],
                                           ALU.add, ALU.mult).then_inc(kxs_ready, 1)
            dve.wait_ge(m_ready, 1)
            for b in range(B):
                V.tensor_copy(MB[b * HR:(b + 1) * HR, b * D:(b + 1) * D],
                              ps[b * HR:(b + 1) * HR, 6, 128:128 + D]).then_inc(mb_ready, 1)
            dve.wait_ge(residual_ready, 1)
            dve.wait_ge(qs_ready, 1)

            def attended_chunk(c):
                dve.wait_ge(attn_ready, c + 1)
                link(V.tensor_tensor(chunk(T2, c), ps[:, c, 0:CH], chunk(T1, c), ALU.add))

            layernorm(flat(T2), flat(Z), 2, arrive=attended_chunk)
            dve.wait_ge(weights_in[3], 16)
            link(V.tensor_scalar(coef[:, 0:1], w("a"), DT * DT, 1.0, ALU.mult, ALU.add))
            link(V.reciprocal(powers[:, 0, 0, 0:1], coef[:, 0:1]))
            link(V.tensor_scalar(powers[:, 0, 2, 0:1], powers[:, 0, 0, 0:1], DT, None, ALU.mult))
            link(V.scalar_tensor_tensor(powers[:, 0, 1, 0:1], powers[:, 0, 2, 0:1], -1.0, w("a"), ALU.mult, ALU.mult))
            link(V.tensor_copy(coef[:, 2:3], powers[:, 0, 2, 0:1]))
            link(V.tensor_scalar(coef[:, 3:4], coef[:, 2:3], DT, None, ALU.mult))
            link(V.tensor_tensor(coef[:, 4:5], coef[:, 2:3], w("bB"), ALU.mult))
            V.tensor_tensor(coef[:, 5:6], coef[:, 3:4], w("bB"), ALU.mult).then_inc(coef_ready, 1)
            link(V.tensor_tensor(bcd[:, :], w("bC"), w("bD"), ALU.add))
            link(V.tensor_scalar(iota64[:, :], w("iota"), 64.0, None, ALU.add))
            dve.wait_ge(lambda_ready, 3)
            link(V.tensor_tensor(powers[:, 0, 0, 1:2], lam[:, 1:2], lam[:, 6:7], ALU.mult))
            link(V.tensor_tensor(powers[:, 0, 2, 1:2], lam[:, 1:2], lam[:, 5:6], ALU.mult))
            link(V.tensor_scalar(powers[:, 0, 1, 1:2], powers[:, 0, 2, 1:2], -1.0, None, ALU.mult))
            link(V.tensor_tensor(lam[:, 10:11], powers[:, 0, 2, 1:2], powers[:, 0, 2, 1:2], ALU.mult))
            link(V.scalar_tensor_tensor(lam[:, 10:11], powers[:, 0, 0, 1:2], powers[:, 0, 0, 1:2], lam[:, 10:11], ALU.mult, ALU.add))
            link(V.tensor_scalar(lam[:, 10:11], lam[:, 10:11], -1.0, 1.0, ALU.mult, ALU.add))
            V.tensor_scalar(lam[:, 7:8], lam[:, 10:11], 0.0, None, ALU.max).then_inc(coef_ready, 1)
            powers_of()
            V.tensor_scalar(w("Cim"), w("Cim"), -1.0, None, ALU.mult).then_inc(coef_ready, 1)

            edge_digits()
            dve.wait_ge(keys_ready, 1)
            take_edges(0, 0, 1)

            def after_mlp(m):
                def add(c):
                    dve.wait_ge(mlp_out[m], 2 * (c + 1))
                    link(V.tensor_tensor(chunk(H, c), ps[:, c, 0:CH], chunk(H, c), ALU.add))
                return add

            dve.wait_ge(weights_in[2], 16)
            dve.wait_ge(residual_ready, 2)
            layernorm(flat(H), flat(X), 3, arrive=after_mlp(0))
            dve.wait_ge(wcol_ready, 1)
            WC = st[:, 5, :]
            V.tensor_copy(WC, ps[:, 1, 0:Q]).then_inc(wcol_used, 1)
            dve.wait_ge(wcol_used, 1)
            link(V.memset(st[:, 6, :], 0.0))

            def compared(instruction):
                instruction.then_inc(dve_step, 1)
                link.count += 1
                dve.wait_ge(dve_step, link.count - 1)

            for k in range(KB):
                for b in range(B):
                    q = 2 * k + b
                    wq = WC[:, q:q + 1]
                    if k and k not in ACT_RANKS:
                        compared(V.tensor_scalar(junk[link.count % 2][:, 0:k * P], WROW[:, b, 0:k * P], wq, None, ALU.is_ge, ALU.add,
                                                 accum_out=st[:, 6, q:q + 1]))
                    if k not in ACT_RANKS:
                        compared(V.tensor_scalar(junk[link.count % 2][:, 0:N - k * P], WROW[:, b, k * P:N], wq, None, ALU.is_gt, ALU.add,
                                                 accum_out=st[:, 7, q:q + 1]))
                    compared(V.scalar_tensor_tensor(junk[link.count % 2][:, 0:P], WROW[:, b, k * P:(k + 1) * P], wq, w("tri"), ALU.is_equal,
                                                    ALU.mult, accum_out=st[:, 8, q:q + 1]))
            dve.wait_ge(dve_step, link.count)
            dve.wait_ge(ranks_ready, 2 * B * len(ACT_RANKS))
            for k in ACT_RANKS:
                V.tensor_scalar(st[:, 6, 2 * k:2 * k + 2], smaller[:, 2 * k:2 * k + 2], -1.0, float(k * P), ALU.mult, ALU.add).then_inc(dve_step, 1)
            link.count += len(ACT_RANKS)
            dve.wait_ge(dve_step, link.count)
            link(V.tensor_tensor(st[:, 6, :], st[:, 6, :], st[:, 7, :], ALU.add))
            link(V.tensor_tensor(st[:, 6, :], st[:, 6, :], st[:, 8, :], ALU.add))
            link(V.scalar_tensor_tensor(st[:, 9, :], st[:, 6, :], float(TOPK), WC, ALU.is_lt, ALU.mult))
            dve.wait_ge(mlp_out[1], 2 * NCH)
            out3 = out_psum().rearrange("p c (q d) -> p c q d", d=D)
            for c in range(NCH):
                V.tensor_tensor(t13[:, c], out3[:, c], row(w("f_b2"), BC * B), ALU.add).then_inc(dve_step, 1)
                link.count += 1
            dve.wait_ge(dve_step, link.count)
            link(V.tensor_tensor(flat(T1), flat(T1), bc(st[:, 9, :], D), ALU.mult))
            dve.wait_ge(residual_ready, 3)
            link(V.tensor_tensor(flat(H), flat(H), flat(T1), ALU.add))

            def scan(n):
                def update(dst, src, l, done=None):
                    p0, q0, r0 = (powers[:, l, i, n:n + 1] for i in range(3))
                    link(V.scalar_tensor_tensor(SA[:, :, dst], SA[:, :, src], p0, SA[:, :, dst], ALU.mult, ALU.add))
                    a = V.scalar_tensor_tensor(SA[:, 0, dst], SA[:, 1, src], q0, SA[:, 0, dst], ALU.mult, ALU.add)
                    a.then_inc(done if done is not None else dve_step, 1)
                    b = V.scalar_tensor_tensor(SA[:, 1, dst], SA[:, 0, src], r0, SA[:, 1, dst], ALU.mult, ALU.add)
                    if done is not None:
                        b.then_inc(done, 1)
                    else:
                        link.count += 1
                        link(b)

                for l in range(7):
                    d = 1 << l
                    update(slice(2 * d - 1, N, 2 * d), slice(d - 1, N - d, 2 * d), l)
                for i in range(1, KB):
                    update(slice(P * (i + 1) - 1, P * (i + 1)), slice(P * i - 1, P * i), 7)
                for l in range(6, -1, -1):
                    d = 1 << l
                    update(slice(3 * d - 1, N, 2 * d), slice(2 * d - 1, N - d, 2 * d), l, scan_ready if l == 0 else None)

            def pick(logits, E, onehot, tmp):
                link(V.tensor_reduce(st[:, 10, :], logits, AX.X, ALU.max))
                link(V.tensor_tensor(tmp, logits, bc(st[:, 10, :], E), ALU.is_equal))
                link(V.scalar_tensor_tensor(tmp, tmp, -64.0, row(iota64[:, 0:E]), ALU.mult, ALU.add))
                link(V.tensor_reduce(st[:, 11, :], tmp, AX.X, ALU.min))
                link(V.tensor_tensor(onehot, row(w("iota")[:, 0:E]), bc(st[:, 11, :], E), ALU.is_equal))

            layernorm(flat(H), flat(X), 4)
            dve.wait_ge(force_ready, 2 * NCH)
            scan(0)
            out3 = out_psum().rearrange("p c (q d) -> p c q d", d=D)
            for c in range(NCH):
                dve.wait_ge(y_ready, c + 1)
                V.tensor_tensor(t13[:, c], out3[:, c], row(bcd[:, :], BC * B), ALU.add).then_inc(cd_ready, 1)

            dve.wait_ge(residual_ready, 4)

            def after_silu(c):
                dve.wait_ge(silu_ready, c + 1)
                link(V.tensor_tensor(chunk(T1, c), chunk(Z, c), chunk(T2, c), ALU.mult))
                link(V.tensor_tensor(chunk(H, c), chunk(H, c), chunk(T1, c), ALU.add))

            layernorm(flat(H), flat(X), 5, arrive=after_silu)
            dve.wait_ge(router_ready, 1)
            lv = LG[:, :, :].rearrange("p k (b e) -> p (k b) e", b=B)
            for c in range(NCH):
                V.tensor_tensor(lv[:, 6 * c:6 * c + 6, :], ps[:, 3 + c, 0:BC * D].rearrange("p (q e) -> p q e", e=E1),
                                row(w("rb"), 6), ALU.add).then_inc(dve_step, 1)
                link.count += 1
            dve.wait_ge(dve_step, link.count)
            pick(lv, E1, flat(Z)[:, :, E1:2 * E1], QS[:, :, :].rearrange("p k (b e) -> p (k b) e", b=B))
            V.tensor_scalar(flat(Z)[:, :, 0:E1], flat(Z)[:, :, E1:2 * E1], -1.0, None, ALU.add).then_inc(gates_ready, 1)
            take_edges(0, 1, SLOTS // 8)
            edge_fields(0)

            def after_experts(c):
                dve.wait_ge(mlp_out[2], 2 * (c + 1))
                link(V.scalar_tensor_tensor(chunk(H, c), ps[:, c, 0:CH], 0.0, chunk(H, c), ALU.max, ALU.add))

            layernorm(flat(H), flat(X), 6, arrive=after_experts)
            dve.wait_ge(force_ready, 4 * NCH)
            scan(1)
            dve.wait_ge(residual_ready, 5)

            def after_scan(c):
                dve.wait_ge(y_ready, NCH + c + 1)
                link(V.tensor_tensor(chunk(H, c), ps[:, c, 0:CH], chunk(H, c), ALU.add))

            layernorm(flat(H), flat(X), 7, arrive=after_scan)
            dve.wait_ge(gat_ready, 1)
            hg = ps[:, 3, 0:Q * 16]
            link(V.tensor_copy(table[:, E2:FEAT, :].rearrange("p f (b k) -> p k b f", b=B), hg.rearrange("p (k b f) -> p k b f", b=B, f=16)))
            hq = hg.rearrange("p (q f) -> p q f", f=16)
            prod = flat(T1)[:, :, 0:16]
            for att, dst in (("att_src", table[:, 0:E2, :]), ("att_dst", dst_score)):
                link(V.tensor_tensor(prod, hq, row(w(att)), ALU.mult))
                link(V.reduce_sum(pick4[:, 0, :, :], prod.rearrange("p q (h e) -> p q h e", e=4), AX.X))
                link(V.tensor_copy(dst.rearrange("p h (b k) -> p k b h", b=B), pick4[:, 0, :, :].rearrange("p (k b) h -> p k b h", b=B)))
            V.tensor_reduce(local_max[:, :], table[:, 0:E2, :], AX.X, ALU.max).then_inc(local_max_ready, 1)
            left = T2_flat[:, 0:FEAT * NT].rearrange("p (f t) -> p f t", t=NT)
            link(V.tensor_copy(parts[:, 0, :, :], table[:, E2:, :]))
            link(V.tensor_tensor(left, table[:, E2:, :], parts[:, 0, :, :], ALU.subtract))
            link(V.tensor_copy(parts[:, 1, :, :], left))
            link(V.tensor_tensor(left, left, parts[:, 1, :, :], ALU.subtract))
            V.tensor_copy(parts[:, 2, :, :], left).then_inc(parts_ready, 1)
            dve.wait_ge(score_max_ready, 1)

            def edge_pass(it):
                reg = not isinstance(it, int)
                hold(dve, rest_turned, it + 1, reg)
                linked(it, V.tensor_reduce(small[0:1, 8:9], ps[0:1, 4, CH:CH + P], AX.X, ALU.max))
                V.tensor_scalar(flag[:, bass.ds(it, 1)], small[0:1, 8:9], 1.0, None, ALU.min).then_inc(flag_ready, 1)

                def mask(g, s, first=False):
                    hold(dve, gathered, it * GN + g + 1, reg)
                    if not first:
                        hold(dve, selected, it * GN + g - 1, reg)
                    at = bass.ts(g, GRP)
                    rows_of = ps[:, 2 * s:2 * s + GRP, 0:FEAT * NT].rearrange("p g (f t) -> p g f t", t=NT)
                    V.tensor_tensor(product[s][:, :, 0:16, :], rows_of[:, :, 0:16, :],
                                    src_hi_oh[:, at, :].unsqueeze(2).broadcast_to([P, GRP, 16, NT]), ALU.mult).then_inc(product_step, 1)
                    V.tensor_tensor(product[s][:, :, 16:FEAT, :], rows_of[:, :, 16:FEAT, :],
                                    dst_hi_oh[:, at, :].unsqueeze(2).broadcast_to([P, GRP, E2, NT]), ALU.mult).then_inc(product_step, 1)

                def select(g, s):
                    hold(dve, product_step, (it * GN + g) * 2 + 2, reg)
                    V.reduce_sum(e_val[:, bass.ts(g, GRP), :], product[s], AX.X).then_inc(selected, 1)

                for s in range(2):
                    mask(s, s, first=not reg)
                select(0, 0)
                with dve.Fori(1, GN // 2) as r:
                    mask(2 * r, 0)
                    select(2 * r + (-1), 1)
                    mask(2 * r + 1, 1)
                    select(2 * r, 0)
                select(GN - 1, 1)
                hold(dve, selected, (it + 1) * GN, reg)
                t0, t1, dsc = e_tmp[:, 0, :, :], e_tmp[:, 1, :, :], e_val[:, :, 16:FEAT]
                linked(it, V.tensor_tensor(e_w[:, :, 0:16], e_val[:, :, 0:16], row(w("att_src"), SLOTS), ALU.mult))
                linked(it, V.reduce_sum(t0, e_w[:, :, 0:16].rearrange("p s (h e) -> p s h e", e=4), AX.X))
                linked(it, V.tensor_tensor(t0, t0, dsc, ALU.add))
                linked(it, V.tensor_tensor(t1, dsc, row(score_max[:, :], SLOTS), ALU.add))
                linked(it, V.scalar_tensor_tensor(t0, t0, 0.2, t0, ALU.mult, ALU.max))
                linked(it, V.scalar_tensor_tensor(t1, t1, 0.2, t1, ALU.mult, ALU.max))
                linked(it, V.tensor_tensor(t0, t0, t1, ALU.subtract))
                V.tensor_scalar(t0, t0, 0.0, None, ALU.min).then_inc(edge_shift_ready, 1)
                hold(dve, edge_exp_ready, it + 1, reg)
                linked(it, V.tensor_tensor(e_w[:, :, E2:FEAT].rearrange("p s (h e) -> p s h e", e=4),
                                       e_val[:, :, 0:16].rearrange("p s (h e) -> p s h e", e=4), bc(e_w[:, :, 0:E2], 4), ALU.mult))

                if not reg:
                    V.engine_nop().then_inc(terms_ready, 1)

                def spread_out(g, s, first=False):
                    if not first:
                        hold(dve, scattered, it * GN + g - 1, reg)
                    at = bass.ts(g, GRP)
                    V.tensor_tensor(dst_lo_oh[s], row(w("iota128"), GRP), bc(field[:, 2, at], P), ALU.is_equal).then_inc(outer_ready, 1 if reg or s else 2)
                    if not reg and s == 0:
                        return
                    V.tensor_tensor(outer[s], bc(e_w[:, at, :], NT), dst_hi_oh[:, at, :].unsqueeze(2).broadcast_to([P, GRP, FEAT, NT]),
                                    ALU.mult).then_inc(outer_ready, 1)

                def onehots(i, s, first=False):
                    if not first:
                        dve.wait_ge(counted, i - 1)
                    at = bass.ts(i, HG)
                    V.tensor_tensor(oh_hi[s], digit_hi[:, at].unsqueeze(1).broadcast_to([P, NHI, HG]),
                                    digit_values[:, 0:NHI, :], ALU.is_equal).then_inc(onehots_ready, 1)
                    V.tensor_tensor(oh_lo[s], digit_lo[:, at].unsqueeze(1).broadcast_to([P, NLO, HG]),
                                    digit_values[:, :, :], ALU.is_equal).then_inc(onehots_ready, 1)

                def four_groups(r, first=False):
                    for h in range(2):
                        for s in range(2):
                            spread_out(4 * r + (2 * h + s), s, first=first and h == 0)
                        if not reg:
                            onehots(2 * r + h, h, first=first)

                four_groups(0, first=not reg)
                with dve.Fori(1, GN // 4) as r:
                    four_groups(r)
                hold(dve, scattered, it * GN + GN, reg)
                assert steps[0] == PASS_STEPS, steps

            edge_pass(0)
            dve.wait_ge(counted, CAND // HG)
            for o in range(2):
                V.tensor_copy(n_last[64 * o:64 * o + 64, :],
                              ps[0:NLO, 4, 0:NHI].rearrange("p (t o) -> p t o", o=2)[:, :, o]).then_inc(counts_used, 1)
            dve.wait_ge(counts_used, 2)
            more = dve.value_load(flag[0:1, 0:1], min_val=0, max_val=1)
            with dve.If(more > 0):
                with dve.Fori(1, PASSES) as it:
                    more = dve.value_load(flag[0:1, bass.ds(it - 1, 1)], min_val=0, max_val=1)
                    with dve.If(more > 0):
                        take_edges(it, 0, SLOTS // 8)
                        edge_fields(it)
                        edge_pass(it)

            own, far, top = node_w[:, 1, 0, :, :], node_w[:, 1, 1, :, :], node_w[:, 2, 0, :, :]
            dve.wait_ge(last_ready, 1)
            link(V.tensor_copy(last_node[:, :], ps[:, 5, 0:FEAT]))
            link(V.tensor_tensor(own, table[:, 0:E2, :], dst_score, ALU.add))
            link(V.tensor_tensor(far, dst_score, bc(last_node[:, 0:E2], NT), ALU.add))
            link(V.tensor_tensor(top, dst_score, bc(score_max[:, :], NT), ALU.add))
            for x in (own, far, top):
                link(V.scalar_tensor_tensor(x, x, 0.2, x, ALU.mult, ALU.max))
            link(V.tensor_tensor(own, own, top, ALU.subtract))
            V.tensor_tensor(far, far, top, ALU.subtract).then_inc(node_shift_ready, 1)
            dve.wait_ge(node_exp_ready, 1)
            own, far = node_w[:, 0, 0, :, :], node_w[:, 0, 1, :, :]
            den, rden = node_w[:, 1, 0, :, :], node_w[:, 1, 1, :, :]
            dve.wait_ge(counts_used, 2)
            link(V.tensor_tensor(far, far, n_last[:, :].unsqueeze(1).broadcast_to([P, E2, NT]), ALU.mult))
            sums = ps[:, 7, 0:FEAT * NT].rearrange("p (f t) -> p f t", t=NT)
            link(V.tensor_tensor(den, own, far, ALU.add))
            link(V.tensor_tensor(den, den, sums[:, 0:E2, :], ALU.add))
            link(V.scalar_tensor_tensor(den, den, 1e-16, den, ALU.mult, ALU.add))
            link(V.reciprocal(rden, den))

            def four(x):
                return x.rearrange("p (h e) t -> p h e t", e=4)

            def per_head(x):
                return x.unsqueeze(2).broadcast_to([P, E2, 4, NT])

            a0 = T1[:, :, :, :].rearrange("p k b d -> p (k b d)")[:, 0:16 * NT].rearrange("p (f t) -> p f t", t=NT)
            a1 = T1[:, :, :, :].rearrange("p k b d -> p (k b d)")[:, 512:512 + 16 * NT].rearrange("p (f t) -> p f t", t=NT)
            link(V.tensor_tensor(four(a0), four(table[:, E2:FEAT, :]), per_head(own), ALU.mult))
            link(V.tensor_tensor(four(a1), four(bc(last_node[:, E2:FEAT], NT)), per_head(far), ALU.mult))
            link(V.tensor_tensor(a0, a0, a1, ALU.add))
            V.tensor_tensor(a0, a0, sums[:, E2:FEAT, :], ALU.add).then_inc(sums_read, 1)
            dve.wait_ge(sums_read, 1)
            link(V.tensor_tensor(four(a0), four(a0), per_head(rden), ALU.mult))
            agg = flat(T2)[:, :, 0:16]
            link(V.tensor_tensor(agg.rearrange("p (k b) f -> p k b f", b=B), a0.rearrange("p f (b k) -> p k b f", b=B),
                                 w("b_gat").unsqueeze(1).unsqueeze(1).broadcast_to([P, KB, B, 16]), ALU.add))
            layernorm(agg, agg, 8, 16, flat(XC)[:, :, 0:16], flat(T1)[:, :, 0:16])
            link(V.tensor_tensor(agg, agg, row(w("g_gamma")), ALU.mult))
            link(V.tensor_tensor(agg, agg, row(w("g_beta")), ALU.add))
            sc = pick4[:, 0, :, :]
            link(V.reduce_sum(sc, agg.rearrange("p q (h e) -> p q e h", e=4), AX.X))
            link(V.tensor_scalar(sc, sc, 0.25, None, ALU.mult))
            pick(sc, E2, pick4[:, 1, :, :], gate4[:, :, :])
            link(V.tensor_copy(st[:, 14, :], st[:, 10, :]))
            link(V.scalar_tensor_tensor(sc, pick4[:, 1, :, :], -BIG, sc, ALU.mult, ALU.add))
            pick(sc, E2, pick4[:, 2, :, :], gate4[:, :, :])
            V.tensor_tensor(st[:, 13, :], st[:, 10, :], st[:, 14, :], ALU.subtract).then_inc(gate_shift_ready, 1)
            dve.wait_ge(gate_exp_ready, 1)
            link(V.tensor_scalar(st[:, 14, :], st[:, 12, :], 1.0, None, ALU.add))
            link(V.reciprocal(st[:, 15, :], st[:, 14, :]))
            link(V.tensor_tensor(st[:, 12, :], st[:, 12, :], st[:, 15, :], ALU.mult))
            link(V.tensor_tensor(pick4[:, 1, :, :], pick4[:, 1, :, :], bc(st[:, 15, :], E2), ALU.mult))
            link(V.tensor_tensor(pick4[:, 2, :, :], pick4[:, 2, :, :], bc(st[:, 12, :], E2), ALU.mult))
            link(V.tensor_tensor(gate4[:, :, :], pick4[:, 1, :, :], pick4[:, 2, :, :], ALU.add))
            dve.wait_ge(weights_in[5], 16)

            def after_gated(c):
                for v in range(2 * BC * c, 2 * BC * (c + 1)):
                    s, k = v // BC, v % BC
                    kk, b = BC * (s // 2) + k, s % 2
                    dve.wait_ge(mlp_out[3], v + 1)
                    tmp = T2_flat[:, (v % 2) * 256:(v % 2 + 1) * 256].rearrange("p (e d) -> p e d", e=E2)
                    link(V.tensor_tensor(tmp, ps[:, v % 3, 0:256].rearrange("p (e d) -> p e d", e=E2), bc(gate4[:, 2 * kk + b, :], D), ALU.mult))
                    V.reduce_sum(T1[:, kk, b, :], tmp.rearrange("p e d -> p d e"), AX.X).then_inc(gated, 1)
                dve.wait_ge(gated, 2 * BC * (c + 1))
                link(V.tensor_tensor(chunk(H, c), chunk(H, c), chunk(T1, c), ALU.add))

            layernorm(flat(H), flat(X), 9, arrive=after_gated)
            dve.wait_ge(v3_ready, 1)
            for c in range(NCH):
                V.tensor_tensor(VT[:, BC * c:BC * c + BC, :, :].rearrange("p k b d -> p (k b) d"),
                                ps[:, 3 + c, 0:CH].rearrange("p (q d) -> p q d", d=D), row(w("bv3"), 6),
                                ALU.add).then_inc(v3_used, 1)

            def largest(u):
                i, base = u // 2, 3 * (u % 2)
                L = (i + 1) * P
                dve.wait_ge(s3_ready, u + 1)
                all3 = ps[:, base:base + 3, :].rearrange("p c n -> p (c n)")
                link(V.tensor_tensor(all3[:, L - P:L], all3[:, L - P:L], w("causal"), ALU.add))
                link(V.tensor_reduce(den3[:, 0, u:u + 1], all3[:, 0:L], AX.X, ALU.max))
                V.tensor_scalar(den3[:, 1, u:u + 1], den3[:, 0, u:u + 1], -SCALE, None, ALU.mult).then_inc(shift3_ready, 1)

            def attended(u):
                i, b = u // 2, u % 2
                dve.wait_ge(o3_ready, u + 1)
                link(V.reciprocal(den3[:, 3, u:u + 1], den3[:, 2, u:u + 1]))
                V.scalar_tensor_tensor(H[:, i, b, :], ps[:, 6 + u % 2, 0:D], den3[:, 3, u:u + 1], H[:, i, b, :],
                                       ALU.mult, ALU.add).then_inc(o3_used, 1)

            def after_attention(c):
                units = 2 * BC
                if c == 0:
                    largest(0)
                for u in range(units * c + (c > 0), min(units * (c + 1) + 1, Q)):
                    if u + 1 < Q:
                        largest(u + 1)
                    if u:
                        attended(u - 1)
                if c == NCH - 1:
                    attended(Q - 1)
                dve.wait_ge(o3_used, units * (c + 1))

            layernorm(flat(H), flat(X), 10, arrive=after_attention)
            link(V.memset(flat(Z), 0.0))
            dve.wait_ge(router_ready, 2)
            lv = LG[:, :, :].rearrange("p k (b e) -> p (k b) e", b=B)[:, :, 0:E3]
            tmp = QS[:, :, :].rearrange("p k (b e) -> p (k b) e", b=B)
            for c in range(NCH):
                V.tensor_tensor(lv[:, 6 * c:6 * c + 6, :], ps[:, 3 + c, 0:BC * D].rearrange("p (q e) -> p q e", e=E1)[:, :, 0:E3],
                                row(w("bg3"), 6), ALU.add).then_inc(dve_step, 1)
                link.count += 1
            dve.wait_ge(dve_step, link.count)
            first, second = tmp[:, :, E3:2 * E3], tmp[:, :, 2 * E3:3 * E3]
            pick(lv, E3, first, tmp[:, :, 0:E3])
            link(V.scalar_tensor_tensor(lv, first, -BIG, lv, ALU.mult, ALU.add))
            pick(lv, E3, second, tmp[:, :, 0:E3])
            link(V.tensor_tensor(flat(Z)[:, :, E3:2 * E3], first, second, ALU.add))
            V.tensor_scalar(flat(Z)[:, :, 0:E3], flat(Z)[:, :, E3:2 * E3], -1.0, None, ALU.add).then_inc(gates_ready, 1)
            for c in range(NCH):
                dve.wait_ge(mlp_out[4], 2 * (c + 1))
                V.tensor_tensor(chunk(H, c), ps[:, c, 0:CH], chunk(H, c), ALU.add).then_inc(h_ready, 1)

        @block.tensor
        def _(pe):
            MM = nc.tensor.matmul
            ident = w("ident")

            def turn(t, n, src):
                for c in range(NCH):
                    pe.wait_ge(norm_ready, NCH * n + c + 1)
                    for j in range(BC):
                        last = nc.tensor.transpose(ps[:, c, j * P:(j + 1) * P], blk(src, BC * c + j), ident)
                    last.then_inc(turned, 1)

            def turn_narrow(src, done):
                for c in range(NCH):
                    for j in range(BC):
                        last = nc.tensor.transpose(ps[0:D, 3 + c, j * P:(j + 1) * P], src[:, BC * c + j, :], ident)
                    last.then_inc(done, 1)

            def mlp(m, t, J, w1, w2, gated=False, bias=None):
                def hidden(s):
                    c, b = s // 2, s % 2
                    rows = slice(b * D, (b + 1) * D)
                    if b == 0:
                        pe.wait_ge(xf_ready, NCH * t + c + 1)
                    for j in range(J):
                        n = s * J + j
                        if n >= 5:
                            pe.wait_ge(g_ready[m], n - 4)
                        o = ps[:, 3 + n % 5, 0:CH]
                        last = MM(o, w(w1)[:, (b * J + j) * P:(b * J + j + 1) * P],
                                  (XF, NF)[b if gated else 0][:, c * CH:(c + 1) * CH], start=True, stop=True)
                        last.then_inc(hid_ready[m], 1)

                def output(s):
                    c, b = s // 2, s % 2
                    pe.wait_ge(g_ready[m], (s + 1) * J)
                    for k in range(BC):
                        o = ps[:, c, k * P + b * D:k * P + (b + 1) * D]
                        for j in range(J):
                            last = MM(o, G[:, s % 2, j, k * P:(k + 1) * P], w(w2)[:, j * D:(j + 1) * D],
                                      start=j == 0, stop=j == J - 1 and bias is None)
                        if bias is not None:
                            at = c * CH + k * P
                            last = MM(o, (XF, NF)[b][:, at:at + P], w(bias)[:, b * D:(b + 1) * D],
                                      start=False, stop=True)
                    last.then_inc(mlp_out[m], 1)

                hidden(0)
                for s in range(2 * NCH):
                    if s + 1 < 2 * NCH:
                        hidden(s + 1)
                    output(s)

            pe.wait_ge(weights_in[0], 16)
            pe.wait_ge(x_in, 16)
            for i, name in enumerate(("tok_Wq", "tok_Wk")):
                for th in range(2):
                    last = MM(ps[:, 2 * i + th, :], w(name), XF[:, th * 512:(th + 1) * 512], start=True, stop=True)
            last.then_inc(tok_proj, 1)
            for k in range(IB):
                last = MM(ps[:, 4 + k // 4, (k % 4) * P:(k % 4 + 1) * P], XF[:, k * P:(k + 1) * P], w("tok_Wv"), start=True, stop=True)
            last.then_inc(tok_proj, 1)
            pe.wait_ge(tok_proj_used, 8)
            pe.wait_ge(zeros_ready, 3)

            def scores(u):
                th, b, j = u // 16, u // IB % 2, u % IB
                if u >= 4:
                    pe.wait_ge(decay_ready, u - 3)
                MM(ps[:, u % 4, :], tok_k[b][:, j * P:(j + 1) * P], SA[:, 0, th * 512:(th + 1) * 512],
                   start=True, stop=True).then_inc(score_ready, 1)

            def kept(u):
                th, b, j = u // 16, u // IB % 2, u % IB
                pe.wait_ge(decay_ready, u + 1)
                MM(ps[b * D:(b + 1) * D, 6 + th, :], VT[:, j, b, :], ring[:, u % 4, :],
                   start=j == 0, stop=j == IB - 1).then_inc(kept_step, 1)

            for u in range(3):
                scores(u)
            for u in range(32):
                if u + 3 < 32:
                    scores(u + 3)
                kept(u)
            for i in range(2):
                pe.wait_ge(kept_copied, i + 1)
                for k in range(4 * i, 4 * i + 4):
                    last = MM(ps[:, i, (k % 4) * P:(k % 4 + 1) * P], T2_flat[:, k * P:(k + 1) * P], w("tok_Wo"), start=True, stop=True)
                last.then_inc(tok_y, 1)

            pe.wait_ge(weights_in[1], 16)
            bank = ps[:, 5, :]
            for o, lhs, rhs in (
                (bank[:, 0:32], lambda t: w("WxT")[:, t * P:(t + 1) * P], lambda t: w("WqBD")[:, t * HR:(t + 1) * HR]),
                (bank[:, 32:64], lambda t: w("WxT")[:, t * P:(t + 1) * P], lambda t: w("WkBD")[:, t * D:t * D + HR]),
                (bank[:, 64:96], lambda t: w("bxrep")[:, t * P:(t + 1) * P], lambda t: w("WqBD")[:, t * HR:(t + 1) * HR]),
                (bank[0:D, 96:97], lambda t: w("WkBD")[:, t * D:(t + 1) * D], lambda t: w("bxcol")[:, t:t + 1]),
            ):
                for t in range(2):
                    MM(o, lhs(t), rhs(t), start=t == 0, stop=t == 1)
            for t in range(2):
                last = MM(bank[:, 128 + t * D:128 + (t + 1) * D], w("WvT"), w("Wo")[:, t * D:(t + 1) * D], start=True, stop=True)
            last.then_inc(merged_ready, 1)
            turn(0, 1, Z)
            pe.wait_ge(merged_used, 7)
            pe.wait_ge(xf_ready, NCH)
            for c in range(NCH):
                last = MM(ps[0:D, c, 0:CH], WK[:, :], XF[:, c * CH:(c + 1) * CH], start=True, stop=True)
            last.then_inc(klog_ready, 1)
            for c in range(NCH):
                for j in range(BC):
                    last = MM(ps[:, 3 + c, j * D:(j + 1) * D], XF[:, (BC * c + j) * P:(BC * c + j + 1) * P], WQ[:, :],
                              start=True, stop=True)
            last.then_inc(qlog_ready, 1)
            pe.wait_ge(knorm_ready, 1)
            for c in range(NCH):
                for j in range(BC):
                    k = BC * c + j
                    last = nc.tensor.transpose(ps[:, c, j * D:(j + 1) * D], NF[0:D, k * P:(k + 1) * P], ident[0:D, 0:D])
            last.then_inc(kturned, 1)
            pe.wait_ge(kt_ready, 1)
            for k in range(KB):
                last = MM(ps[:, 6, 0:D], blk(Z, k), KT[:, k, :], start=k == 0, stop=k == KB - 1)
            last.then_inc(ut_ready, 1)
            pe.wait_ge(uts_ready, 2)
            for b in range(B):
                rows = slice(b * D, (b + 1) * D)
                for t in range(2):
                    last = MM(ps[:, 7 * b, t * HR:(t + 1) * HR], w("WxD", rows)[:, t * P:(t + 1) * P], UTs[rows, :],
                              start=True, stop=True)
            last.then_inc(kx_ready, 1)
            pe.wait_ge(qs_ready, 1)
            turn_narrow(QS, qturned)
            pe.wait_ge(kxs_ready, 4)
            for b in range(B):
                for t in range(2):
                    last = MM(ps[b * HR:(b + 1) * HR, 6, 128:128 + D], KX[:, b, t, :], WVO[:, t, :], start=t == 0, stop=t == 1)
            last.then_inc(m_ready, 1)
            pe.wait_ge(mb_ready, 2)
            for c in range(NCH):
                pe.wait_ge(qf_ready, c + 1)
                for j in range(BC):
                    k = BC * c + j
                    last = MM(ps[:, c, j * P:(j + 1) * P], NF[0:D, k * P:(k + 1) * P], MB[:, :], start=True, stop=True)
                last.then_inc(attn_ready, 1)
            turn(1, 2, Z)
            mlp(0, 1, 2, "a_W1", "a_W2")

            pe.wait_ge(weights_in[2], 16)
            turn(2, 3, X)
            pe.wait_ge(xf_ready, 3 * NCH)
            for b in range(B):
                rows = slice(b * D, (b + 1) * D)
                for c in range(NCH):
                    last = MM(ps[:, WBANK[b][c], 0:CH], w("wr", rows), XF[rows, c * CH:(c + 1) * CH], start=True, stop=True)
                last.then_inc(wrow_ready, 1)
            pe.wait_ge(wrow_copied, 2 * NCH)
            for k in range(KB):
                for b in range(B):
                    q = 2 * k + b
                    last = nc.tensor.transpose(ps[:, 1, q:q + 1], WROW[0:1, b, k * P:(k + 1) * P], ident[0:1, 0:1])
            last.then_inc(wcol_ready, 1)
            pe.wait_ge(wcol_used, 1)
            mlp(1, 2, 2, "f_w1", "f_w2")

            def count(i, s):
                pe.wait_ge(onehots_ready, 2 * i + 2)
                for t in range(HG):
                    last_mm = MM(ps[0:NLO, 4, 0:NHI], oh_lo[s][:, :, t], oh_hi[s][:, :, t], start=False, stop=False, skip_group_check=True)
                last_mm.then_inc(counted, 1)

            def gates_turn(n):
                pe.wait_ge(gates_ready, n + 1)
                for c in range(NCH):
                    for j in range(BC):
                        last = nc.tensor.transpose(ps[:, 3 + c, j * P:(j + 1) * P], blk(Z, BC * c + j), ident)
                    last.then_inc(gates_turned, 1)
                pe.wait_ge(gates_copied, 3 * NCH * (n + 1))

            def router(t, name):
                pe.wait_ge(xf_ready, NCH * (t + 1))
                for c in range(NCH):
                    for j in range(BC):
                        last = MM(ps[:, 3 + c, j * D:(j + 1) * D], XF[:, (BC * c + j) * P:(BC * c + j + 1) * P], w(name), start=True, stop=True)
                last.then_inc(router_ready, 1)

            def token_product(pairs, done):
                for c in range(NCH):
                    for j in range(BC):
                        at = (BC * c + j) * P
                        for i, (x, m) in enumerate(pairs):
                            last = MM(ps[:, c, j * P:(j + 1) * P], x[:, at:at + P], m, start=i == 0, stop=i == len(pairs) - 1)
                    last.then_inc(done, 1)

            pe.wait_ge(weights_in[3], 16)
            turn(3, 4, X)
            for c in range(NCH):
                pe.wait_ge(xf_ready, 3 * NCH + c + 1)
                MM(ps[:, 3 + c, 0:CH], w("WB"), XF[:, c * CH:(c + 1) * CH], start=True, stop=True).then_inc(bu_ready, 1)
            pe.wait_ge(scan_ready, 2)
            token_product([(SA[:, 1, :], w("WC")), (XF[:, :], w("WD"))], y_ready)
            turn(4, 5, X)
            router(4, "rw")
            gates_turn(0)
            mlp(2, 4, 4, "m_W1", "m_W2", gated=True, bias="m_b2")
            pe.wait_ge(weights_in[4], 16)
            turn(5, 6, X)
            pe.wait_ge(xf_ready, 6 * NCH)
            for s, name in enumerate(("Bre", "Bim")):
                for c in range(NCH):
                    MM(ps[:, (3 + s * NCH + c) % 8, 0:CH], w(name), XF[:, c * CH:(c + 1) * CH], start=True, stop=True).then_inc(bu_ready, 1)
            pe.wait_ge(scan_ready, 4)
            pe.wait_ge(coef_ready, 4)
            token_product([(SA[:, 0, :], w("Cre")), (SA[:, 1, :], w("Cim"))], y_ready)

            turn(6, 7, X)
            pe.wait_ge(xf_ready, 7 * NCH)
            for k in range(KB):
                last_mm = MM(ps[:, 3, k * 32:(k + 1) * 32], XF[:, k * P:(k + 1) * P], w("Wgat"), start=True, stop=True)
            last_mm.then_inc(gat_ready, 1)
            pe.wait_ge(parts_ready, 1)
            pe.wait_ge(zeros_ready, 1)
            MM(ps[:, 7, 0:FEAT * NT], zeros[:, :], table[:, 0:FEAT, :].rearrange("p f t -> p (f t)"), start=True, stop=False, skip_group_check=True)

            def edge_pass(it):
                pe.wait_ge(rest_ready, it + 1)
                nc.tensor.transpose(ps[0:1, 4, CH:CH + P], rest8[:, 1:2], ident).then_inc(rest_turned, 1)
                pe.wait_ge(fields_ready, it * 2 + 2)

                def spread(g, s, first=False):
                    if not first:
                        pe.wait_ge(low_read, it * GN + g - 1)
                    for i in range(2):
                        for t in range(GRP):
                            last_mm = MM(ps[:, 5 + s, (i * GRP + t) * P:(i * GRP + t + 1) * P],
                                         lo_b[:, i, bass.ds(GRP * g + t, 1)].broadcast_to([P, P]), ident_b[:, :], start=True, stop=True)
                    last_mm.then_inc(spread_ready, 1)

                def gather(g, s, first=False):
                    pe.wait_ge(oht_ready, it * GN + g + 1)
                    if not first:
                        pe.wait_ge(product_step, (it * GN + g) * 2 - 2)
                    for t in range(GRP):
                        for i, (a, b) in enumerate(((0, 16), (16, FEAT))):
                            for k in range(3):
                                last_mm = MM(ps[:, 2 * s + t, a * NT:b * NT], turned_oh[s][:, (i * GRP + t) * P:(i * GRP + t + 1) * P],
                                             parts[:, k, a:b, :].rearrange("p f t -> p (f t)"), start=k == 0, stop=k == 2)
                    last_mm.then_inc(gathered, 1)

                fresh = isinstance(it, int)
                spread(0, 0, first=fresh)
                spread(1, 1, first=fresh)
                gather(0, 0, first=fresh)
                spread(2, 0)
                gather(1, 1, first=fresh)
                with pe.Fori(1, GN // 2 - 1) as r:
                    spread(2 * r + 1, 1)
                    gather(2 * r, 0)
                    spread(2 * r + 2, 0)
                    gather(2 * r + 1, 1)
                spread(GN - 1, 1)
                gather(GN - 2, 0)
                gather(GN - 1, 1)

                def scatter(g, s, half_g=None):
                    pe.wait_ge(outer_ready, (it * GN + g) * 2 + 2)
                    if fresh and s == 0:
                        pe.wait_ge(pool_outer, half_g + 1)
                    for t in range(GRP):
                        last_mm = MM(ps[:, 7, 0:FEAT * NT], dst_lo_oh[s][:, t, :], outer[s][:, t, :, :].rearrange("p f t -> p (f t)"),
                                     start=False, stop=False, skip_group_check=True)
                    last_mm.then_inc(scattered, 1)

                if fresh:
                    MM(ps[0:NLO, 4, 0:NHI], zeros[:, 0:NLO], zeros[:, 0:NHI], start=True, stop=False, skip_group_check=True)
                with pe.Fori(0, GN // 4) as r:
                    for h in range(2):
                        for s in range(2):
                            scatter(4 * r + (2 * h + s), s, 2 * r + h)
                        if fresh:
                            count(2 * r + h, h)

            edge_pass(0)
            pe.wait_ge(flag_ready, 1)
            more = pe.value_load(flag[0:1, 0:1], min_val=0, max_val=1)
            with pe.If(more > 0):
                with pe.Fori(1, PASSES) as it:
                    more = pe.value_load(flag[0:1, bass.ds(it - 1, 1)], min_val=0, max_val=1)
                    with pe.If(more > 0):
                        edge_pass(it)
            MM(ps[:, 5, 0:FEAT], ident[:, P - 1:P].broadcast_to([P, P]), table[:, 0:FEAT, NT - 1], start=True, stop=True).then_inc(last_ready, 1)

            def hidden(s):
                c, b = s // 2, s % 2
                rows = slice(b * D, (b + 1) * D)
                for j in range(E2):
                    n = s * E2 + j
                    if n >= 5:
                        pe.wait_ge(g_ready[3], n - 4)
                    MM(ps[:, 3 + n % 5, 0:CH], w("g_W1")[:, (b * E2 + j) * P:(b * E2 + j + 1) * P], XF[:, c * CH:(c + 1) * CH],
                       start=True, stop=True).then_inc(hid_ready[3], 1)

            def output(s):
                pe.wait_ge(g_ready[3], (s + 1) * E2)
                for k in range(BC):
                    v = BC * s + k
                    if v >= 3:
                        pe.wait_ge(gated, v - 2)
                    MM(ps[:, v % 3, 0:E2 * D], ident[:, 0:1].broadcast_to([P, P]), w("g_b2"), start=True, stop=False)
                    for j in range(E2):
                        last_mm = MM(ps[:, v % 3, j * D:(j + 1) * D], G[:, s % 2, j, k * P:(k + 1) * P], w("g_W2")[:, j * D:(j + 1) * D],
                                     start=False, stop=j == E2 - 1)
                    last_mm.then_inc(mlp_out[3], 1)

            pe.wait_ge(node_shift_ready, 1)
            hidden(0)
            pe.wait_ge(sums_read, 1)
            for s in range(2 * NCH):
                if s + 1 < 2 * NCH:
                    hidden(s + 1)
                output(s)
            pe.wait_ge(weights_in[5], 16)
            turn(7, 9, X)
            pe.wait_ge(xf_ready, 8 * NCH)
            for s, name in enumerate(("Wq3", "Wk3")):
                for c in range(NCH):
                    MM(ps[:, (3 + s * NCH + c) % 8, 0:CH], w(name), XF[:, c * CH:(c + 1) * CH], start=True, stop=True).then_inc(qk3_ready, 1)
            pe.wait_ge(qk3_used, B * NCH)
            for c in range(NCH):
                for j in range(BC):
                    at = (BC * c + j) * P
                    last = MM(ps[:, 3 + c, j * P:(j + 1) * P], XF[:, at:at + P], w("Wv3"), start=True, stop=True)
            last.then_inc(v3_ready, 1)
            pe.wait_ge(qk3_used, (B + 1) * NCH)
            pe.wait_ge(zeros_ready, 5)

            def scores3(u):
                i, b, base = u // 2, u % 2, 3 * (u % 2)
                if u == 1:
                    pe.wait_ge(v3_used, NCH)
                if u >= 2:
                    pe.wait_ge(pt3_copied, turned_chunks(u - 1))
                L = (i + 1) * P
                for at in range(0, L, 512):
                    n = min(512, L - at)
                    last = MM(ps[:, base + at // 512, 0:n], query3[b][:, i * P:(i + 1) * P], SA[:, 1, at:at + n], start=True, stop=True)
                last.then_inc(s3_ready, 1)

            def turn_probabilities(u):
                pe.wait_ge(p3_ready, u + 1)
                for cc in range(turned_chunks(u), turned_chunks(u + 1)):
                    c = cc - turned_chunks(u)
                    for j in range(4 * c, min(4 * c + 4, u // 2 + 1)):
                        last = nc.tensor.transpose(ps[:, 3 * (u % 2) + c, (j - 4 * c) * P:(j - 4 * c + 1) * P], PR[:, u % 2, j * P:(j + 1) * P], ident)
                    last.then_inc(pt3_ready, 1)

            def values3(u):
                i, b = u // 2, u % 2
                pe.wait_ge(pt3_copied, turned_chunks(u + 1))
                pe.wait_ge(v3_used, NCH)
                if u >= 2:
                    pe.wait_ge(o3_used, u - 1)
                for j in range(i + 1):
                    last = MM(ps[:, 6 + u % 2, 0:D], PT[:, u % 2, j, :], VT[:, j, b, :], start=j == 0, stop=j == i)
                last.then_inc(o3_ready, 1)

            scores3(0)
            for u in range(Q):
                if u + 1 < Q:
                    scores3(u + 1)
                turn_probabilities(u)
                if u:
                    values3(u - 1)
            values3(Q - 1)
            turn(8, 10, X)
            router(8, "Wg3")
            gates_turn(1)
            mlp(4, 8, 8, "e_W1", "e_W2", gated=True, bias="e_b2")


def host_layout(i):
    pack = np.zeros((P, WIDTH), np.float32)

    def put(name, value, rows=slice(0, P)):
        at, width = COLS[name]
        value = np.asarray(value)
        pack[rows, at:at + width] = value.reshape(value.shape[0], -1) if value.ndim > 1 else value

    def blocks(m):
        r, c = m.shape
        o = np.zeros((B, r, B, c), np.float32)
        for b in range(B):
            o[b, :, b, :] = m
        return o.reshape(B * r, B * c)

    def column(v):
        return np.concatenate([v] * B)[:, None]

    def twice(m):
        return np.concatenate([m] * B, axis=0)

    def apart(m):
        none = np.zeros_like(m)
        return np.concatenate([np.concatenate([m, none]), np.concatenate([none, m])], axis=1)

    def tiles(m):
        return m.reshape(-1, P, m.shape[-1]).transpose(1, 0, 2).reshape(P, -1)

    put("ident", np.eye(P, dtype=np.float32))
    for n in "qkvo":
        put(f"tok_W{n}", blocks(i[f"L0_tok_W{n}"]))
    put("tok_bq", column(i["L0_tok_bq"])), put("tok_bk", column(i["L0_tok_bk"]))
    put("tok_bv", i["L0_tok_bv"]), put("tok_bo", i["L0_tok_bo"]), put("prelu", i["L0_tok_prelu_a"].reshape(1))

    Wx, bx = i["L0_attn_Wx"], i["L0_attn_bx"]
    WxT = Wx.T.reshape(2, P, D).transpose(1, 0, 2)
    put("WxT", np.concatenate([WxT, WxT], axis=2))
    heads = np.zeros((2, HEADS, DH, HEADS, KR), np.float32)
    mask = np.zeros((HEADS, DH, HEADS, KR), np.float32)
    for h in range(HEADS):
        heads[0, h, :, h, :] = i["L0_attn_Wq"]
        heads[1, h, :, h, :] = i["L0_attn_Wk"]
        mask[h, :, h, :] = 1.0
    put("WqBD", tiles(heads[0].reshape(256, HR)))
    k2 = heads[1].reshape(256, HR)
    put("WkBD", tiles(np.concatenate([k2, k2], axis=1)))
    put("headmask", tiles(mask.reshape(256, HR)))
    put("bxrep", np.broadcast_to(bx.reshape(2, P).T[:, :, None], (P, 2, P)))
    put("bxcol", bx.reshape(2, P).T)
    put("WxD", twice(Wx))
    wvt = np.zeros((4, DH, 4, DH), np.float32)
    for h in range(4):
        wvt[h, :, h, :] = i["L0_attn_Wv"].T
    put("WvT", wvt.reshape(P, P))
    put("Wo", tiles(i["L0_attn_Wo"]))
    put("a_bo", i["L0_attn_bo"])
    for n in ("ln1_g", "ln1_b", "ln2_g", "ln2_b"):
        put(n, column(i[f"L0_attn_{n}"]))

    def mlp(pre, w1, b1, w2, b2, upper):
        put(f"{pre}{upper[0]}1", apart(w1)), put(f"{pre}b1", b1.reshape(-1, P).T)
        put(f"{pre}{upper[0]}2", tiles(w2)), put(f"{pre}b2", b2)

    def other_half(m):
        return np.roll(m, m.shape[1] // 2, axis=1)

    def gated(pre, w1, b2):
        E, _, width = w1.shape
        own = w1.transpose(1, 0, 2).reshape(D, E * width)
        gates, out = np.zeros((D, E, width), np.float32), np.zeros((D, D), np.float32)
        for e in range(E):
            gates[e, e, :] = BIG
        out[E:2 * E] = b2
        gates, none = gates.reshape(D, -1), np.zeros((D, D), np.float32)
        put(pre + "W1", np.concatenate([np.concatenate([own, gates]), np.concatenate([gates, own])], axis=1))
        put(pre + "b2", np.concatenate([np.concatenate([none, out]), np.concatenate([out, none])], axis=1))

    mlp("a_", i["L0_attn_W1"], i["L0_attn_b1"], i["L0_attn_W2"], i["L0_attn_b2"], "W")
    put("wr", np.broadcast_to(column(i["L0_ffn_wr"][:, 0]), (P, P)))
    put("br", i["L0_ffn_br"])
    put("tri", np.tril(np.ones((P, P), np.float32), -1))
    mlp("f_", i["L0_ffn_w1"], i["L0_ffn_b1"], i["L0_ffn_w2"], i["L0_ffn_b2"], "w")

    put("WB", blocks(i["L1_attn_W_B"].T)), put("bB", column(i["L1_attn_b_B"])), put("a", column(i["L1_attn_a"]))
    put("WC", blocks(i["L1_attn_W_C"].T)), put("WD", blocks(i["L1_attn_W_D"].T))
    put("bC", i["L1_attn_b_C"]), put("bD", i["L1_attn_b_D"])
    put("rw", other_half(blocks(i["L1_ffn_router_w"].T))), put("rb", i["L1_ffn_router_b"])
    put("iota", np.arange(E1, dtype=np.float32))
    put("m_b1", i["L1_ffn_b1"].reshape(4, P).T)
    put("m_W2", tiles(i["L1_ffn_W2"].reshape(E1 * H1, D)))
    gated("m_", i["L1_ffn_W1"], i["L1_ffn_b2"])

    put("Bre", blocks(i["L2_attn_B_re"].T)), put("Bim", blocks(i["L2_attn_B_im"].T))
    put("nu", column(i["L2_attn_nu_log"])), put("theta", column(i["L2_attn_theta_log"]))
    put("Cre", blocks(i["L2_attn_C_re"].T)), put("Cim", blocks(i["L2_attn_C_im"].T))
    put("Dskip", i["L2_attn_D"])
    put("Wgat", blocks(i["L2_ffn_W_gat"]))
    put("att_src", i["L2_ffn_att_src"].reshape(-1)), put("att_dst", i["L2_ffn_att_dst"].reshape(-1))
    put("b_gat", i["L2_ffn_b_gat"]), put("g_gamma", i["L2_ffn_ln_gamma"]), put("g_beta", i["L2_ffn_ln_beta"])
    put("g_W1", apart(i["L2_ffn_W1"].transpose(1, 0, 2).reshape(D, -1)))
    put("g_b1", i["L2_ffn_b1"].T), put("g_W2", i["L2_ffn_W2"].transpose(1, 0, 2))
    put("g_b2", i["L2_ffn_b2"].reshape(-1))
    put("iota128", np.arange(P, dtype=np.float32))

    put("iota_p", np.arange(P, dtype=np.float32)[:, None])

    for n in "qkv":
        put(f"W{n}3", blocks(i[f"L3_attn_W{n}"].T))
    put("bq3", column(i["L3_attn_bq"])), put("bk3", column(i["L3_attn_bk"])), put("bv3", i["L3_attn_bv"])
    put("causal", np.triu(np.full((P, P), -BIG, np.float32), 1))
    gate = np.zeros((D, E1), np.float32)
    gate[:, :E3] = i["L3_ffn_Wg"]
    put("Wg3", other_half(blocks(gate))), put("bg3", i["L3_ffn_bg"])
    put("e_b1", i["L3_ffn_b1"].T), put("e_W2", i["L3_ffn_W2"].transpose(1, 0, 2))
    gated("e_", i["L3_ffn_W1"], i["L3_ffn_b2"])
    return pack


def kernel(**inputs):
    import concourse.bacc as bacc
    from concourse.bass_utils import run_bass_kernel_spmd

    i = {k: np.asarray(v) for k, v in inputs.items()}
    nc = bacc.Bacc("TRN2", target_bir_lowering=False, num_devices=1)
    arrays = {
        "xT": np.ascontiguousarray(i["x"].reshape(B, N_IMG, D).transpose(0, 2, 1).reshape(P, N_IMG)),
        "txt": np.ascontiguousarray(i["txt"]),
        "gammaT": np.ascontiguousarray(i["L0_tok_d_gamma_batched"].T),
        "edges": np.ascontiguousarray(i["L2_ffn_edge_index"].reshape(2, P, EC)),
        "weights": host_layout(i),
    }
    args = [nc.dram_tensor(n, a.shape, mybir.dt.from_np(a.dtype), kind="ExternalInput").ap() for n, a in arrays.items()]
    out = nc.dram_tensor("out", (B, N, D), F32, kind="ExternalOutput").ap()
    build(nc, *args, out)
    result = run_bass_kernel_spmd(nc, [arrays], core_ids=[0])
    return result.results[0]["out"]
```
